# Optimizing a Trainium2 kernel written in Bass

```python
import numpy as np
import jax
import jax.numpy as jnp

def _softmax(x, axis=-1):
    return jax.nn.softmax(x, axis=axis)

def _gelu(x):
    return jax.nn.gelu(x, approximate=True)

def _silu(x):
    return jax.nn.silu(x)

def _sigmoid(x):
    return jax.nn.sigmoid(x)

def _layernorm(x, axis=-1, eps=1e-05):
    m = jnp.mean(x, axis=axis, keepdims=True)
    v = jnp.var(x, axis=axis, keepdims=True)
    return (x - m) / jnp.sqrt(v + eps)

def _scatter_add(tgt, idx, src, axis=0):
    return tgt.at[idx].add(src)

def _segment_sum(src, seg, n):
    return jax.ops.segment_sum(src, seg, n)
kernel_name = 'mk_prb_d2_jaxref_r8_11617e'

def setup_inputs(seed: int=0):
    np.random.seed(seed)
    _w = jnp.asarray

    def _L0_attn_setup():
        import jax, jax.numpy as jnp
        import numpy as np
        N_HEAD = 16
        N_KV = 4
        N_EMBD = 256
        HEAD_DIM = N_EMBD // N_HEAD
        GROUP = N_HEAD // N_KV
        key = jax.random.key(seed)
        ks = jax.random.split(key, 5)
        B, S = (2, 256)
        scale = 0.02
        return {'x': jax.random.normal(ks[0], (B, S, N_EMBD), dtype=jnp.float32), 'Wq': jax.random.normal(ks[1], (N_EMBD, N_EMBD), dtype=jnp.float32) * scale, 'Wk': jax.random.normal(ks[2], (N_EMBD, N_EMBD // GROUP), dtype=jnp.float32) * scale, 'Wv': jax.random.normal(ks[3], (N_EMBD, N_EMBD // GROUP), dtype=jnp.float32) * scale, 'Wo': jax.random.normal(ks[4], (N_EMBD, N_EMBD), dtype=jnp.float32) * scale}
    _L0_attn_in = _L0_attn_setup()

    def _L0_ffn_setup():
        import jax, jax.numpy as jnp
        import numpy as np
        E, K = (16, 4)
        C, H = (256, 448)
        B, T = (2, 64)
        STD = 0.02
        key = jax.random.key(seed)
        ks = jax.random.split(key, 5)
        x = jax.random.normal(ks[0], (B, T, C), jnp.float32)
        W_up = jax.random.normal(ks[1], (E, H, C), jnp.float32) * STD
        W_gate = jax.random.normal(ks[2], (E, H, C), jnp.float32) * STD
        W_down = jax.random.normal(ks[3], (E, C, H), jnp.float32) * STD
        gate_inp = jax.random.normal(ks[4], (E, C), jnp.float32) * STD
        return {'x': x, 'W_up': W_up, 'W_gate': W_gate, 'W_down': W_down, 'gate_inp': gate_inp}
    _L0_ffn_in = _L0_ffn_setup()

    def _L1_attn_setup():
        import jax, jax.numpy as jnp
        import numpy as np
        B, T, C, H = (4, 512, 256, 16)
        Dh = C // H

        def _feature_map(x):
            return jax.nn.elu(x) + 1.0
        key = jax.random.key(seed)
        ks = jax.random.split(key, 7)
        s = 0.02
        return {'x': jax.random.normal(ks[0], (B, T, C), dtype=jnp.float32), 'cos': jax.random.uniform(ks[1], (T, Dh), dtype=jnp.float32), 'sin': jax.random.uniform(ks[2], (T, Dh), dtype=jnp.float32), 'Wq': jax.random.normal(ks[3], (C, C), dtype=jnp.float32) * s, 'Wk': jax.random.normal(ks[4], (C, C), dtype=jnp.float32) * s, 'Wv': jax.random.normal(ks[5], (C, C), dtype=jnp.float32) * s, 'Wo': jax.random.normal(ks[6], (C, C), dtype=jnp.float32) * s}
    _L1_attn_in = _L1_attn_setup()

    def _L1_ffn_setup():
        import jax, jax.numpy as jnp
        import numpy as np
        B, S, DIM = (2, 256, 256)
        INTER = 128
        E = 8
        K = 2
        N_SHARED = 1
        ROUTE_SCALE = 1.0
        key = jax.random.key(seed)
        ks = jax.random.split(key, 8)
        s_in = 1.0 / np.sqrt(DIM)
        s_hid = 1.0 / np.sqrt(INTER)
        return {'x': jax.random.normal(ks[0], (B, S, DIM), dtype=jnp.float32), 'gate_w': jax.random.normal(ks[1], (E, DIM), dtype=jnp.float32) * s_in, 'w1': jax.random.normal(ks[2], (E, INTER, DIM), dtype=jnp.float32) * s_in, 'w2': jax.random.normal(ks[3], (E, DIM, INTER), dtype=jnp.float32) * s_hid, 'w3': jax.random.normal(ks[4], (E, INTER, DIM), dtype=jnp.float32) * s_in, 'ws1': jax.random.normal(ks[5], (N_SHARED * INTER, DIM), dtype=jnp.float32) * s_in, 'ws2': jax.random.normal(ks[6], (DIM, N_SHARED * INTER), dtype=jnp.float32) * s_hid, 'ws3': jax.random.normal(ks[7], (N_SHARED * INTER, DIM), dtype=jnp.float32) * s_in}
    _L1_ffn_in = _L1_ffn_setup()
    _d = {'L0_attn_x': _L0_attn_in['x'], 'L0_attn_Wq': _L0_attn_in['Wq'], 'L0_attn_Wk': _L0_attn_in['Wk'], 'L0_attn_Wv': _L0_attn_in['Wv'], 'L0_attn_Wo': _L0_attn_in['Wo'], 'L0_ffn_W_up': _L0_ffn_in['W_up'], 'L0_ffn_W_gate': _L0_ffn_in['W_gate'], 'L0_ffn_W_down': _L0_ffn_in['W_down'], 'L0_ffn_gate_inp': _L0_ffn_in['gate_inp'], 'L1_attn_cos': _L1_attn_in['cos'], 'L1_attn_sin': _L1_attn_in['sin'], 'L1_attn_Wq': _L1_attn_in['Wq'], 'L1_attn_Wk': _L1_attn_in['Wk'], 'L1_attn_Wv': _L1_attn_in['Wv'], 'L1_attn_Wo': _L1_attn_in['Wo'], 'L1_ffn_gate_w': _L1_ffn_in['gate_w'], 'L1_ffn_w1': _L1_ffn_in['w1'], 'L1_ffn_w2': _L1_ffn_in['w2'], 'L1_ffn_w3': _L1_ffn_in['w3'], 'L1_ffn_ws1': _L1_ffn_in['ws1'], 'L1_ffn_ws2': _L1_ffn_in['ws2'], 'L1_ffn_ws3': _L1_ffn_in['ws3']}
    _x0 = _d['L0_attn_x']
    _d['L0_attn_x'] = jax.random.normal(jax.random.fold_in(jax.random.key(seed), 1), (2, 512, 256), dtype=_x0.dtype)
    del _x0
    return _d

def reference(L0_attn_x, L0_attn_Wq, L0_attn_Wk, L0_attn_Wv, L0_attn_Wo, L0_ffn_W_up, L0_ffn_W_gate, L0_ffn_W_down, L0_ffn_gate_inp, L1_attn_cos, L1_attn_sin, L1_attn_Wq, L1_attn_Wk, L1_attn_Wv, L1_attn_Wo, L1_ffn_gate_w, L1_ffn_w1, L1_ffn_w2, L1_ffn_w3, L1_ffn_ws1, L1_ffn_ws2, L1_ffn_ws3):

    def _L0_attn_ref(x, Wq, Wk, Wv, Wo):
        import jax, jax.numpy as jnp
        import numpy as np
        N_HEAD = 16
        N_KV = 4
        N_EMBD = 256
        HEAD_DIM = N_EMBD // N_HEAD
        GROUP = N_HEAD // N_KV
        B, S, _ = x.shape
        scale = HEAD_DIM ** (-0.5)
        q = (x @ Wq).reshape(B, S, N_KV, GROUP, HEAD_DIM)
        k = (x @ Wk).reshape(B, S, N_KV, HEAD_DIM)
        v = (x @ Wv).reshape(B, S, N_KV, HEAD_DIM)
        scores = jnp.einsum('bqkgd,bskd->bkgqs', q, k) * scale
        causal = jnp.triu(jnp.ones((S, S), dtype=bool), k=1)
        scores = jnp.where(causal, jnp.finfo(scores.dtype).min, scores)
        attn = jax.nn.softmax(scores, axis=-1)
        out = jnp.einsum('bkgqs,bskd->bqkgd', attn, v)
        out = out.reshape(B, S, N_EMBD)
        return out @ Wo

    def _L0_ffn_ref(x, W_up, W_gate, W_down, gate_inp):
        import jax, jax.numpy as jnp
        import numpy as np
        E, K = (16, 4)
        C, H = (256, 448)
        B, T = (2, 64)
        STD = 0.02
        b, t, c = x.shape
        xf = x.reshape(b * t, c)
        logits = xf @ gate_inp.T
        topv, topi = jax.lax.top_k(logits, K)
        w = jax.nn.softmax(topv.astype(jnp.float32), axis=-1).astype(x.dtype)
        n = xf.shape[0]
        dense_w = jnp.zeros((n, E), x.dtype).at[jnp.arange(n)[:, None], topi].set(w)
        u = jnp.einsum('nc,ehc->neh', xf, W_up)
        g = jnp.einsum('nc,ehc->neh', xf, W_gate)
        h = jax.nn.silu(g) * u
        y = jnp.einsum('neh,ech,ne->nc', h, W_down, dense_w)
        return y.reshape(b, t, c)

    def _L1_attn_ref(x, cos, sin, Wq, Wk, Wv, Wo):
        import jax, jax.numpy as jnp
        import numpy as np
        B, T, C, H = (4, 512, 256, 16)
        Dh = C // H

        def _feature_map(x):
            return jax.nn.elu(x) + 1.0
        b, t, c = x.shape
        h, dh = (H, c // H)

        def proj(W):
            y = jnp.einsum('btc,oc->bto', x, W)
            return y.reshape(b, t, h, dh).transpose(0, 2, 1, 3)
        q = _feature_map(proj(Wq))
        k = _feature_map(proj(Wk))
        v = proj(Wv)
        kv = jnp.einsum('bhtd,bhte->bhde', k, v)
        z = 1.0 / (jnp.einsum('bhtd,bhd->bht', q, k.sum(axis=2)) + 1e-06)
        out = jnp.einsum('bhtd,bhde,bht->bhte', q, kv, z)
        out = out.transpose(0, 2, 1, 3).reshape(b, t, c)
        return jnp.einsum('btc,oc->bto', out, Wo)

    def _L1_ffn_ref(x, gate_w, w1, w2, w3, ws1, ws2, ws3):
        import jax, jax.numpy as jnp
        import numpy as np
        B, S, DIM = (2, 256, 256)
        INTER = 128
        E = 8
        K = 2
        N_SHARED = 1
        ROUTE_SCALE = 1.0
        shape = x.shape
        xf = x.reshape(-1, DIM)
        scores = jax.nn.softmax(xf @ gate_w.T, axis=-1)
        weights, idx = jax.lax.top_k(scores, K)
        weights = weights * ROUTE_SCALE
        h = jnp.einsum('td,eid->eti', xf, w1)
        g = jax.nn.silu(h) * jnp.einsum('td,eid->eti', xf, w3)
        eo = jnp.einsum('eti,edi->etd', g, w2)
        comb = jnp.einsum('tke,tk->te', jax.nn.one_hot(idx, E, dtype=xf.dtype), weights)
        y = jnp.einsum('etd,te->td', eo, comb)
        z = jax.nn.silu(xf @ ws1.T) * (xf @ ws3.T) @ ws2.T
        return (y + z).reshape(shape)
    x = L0_attn_x
    xn = _layernorm(x, axis=-1)
    x = x + _L0_attn_ref(xn, L0_attn_Wq, L0_attn_Wk, L0_attn_Wv, L0_attn_Wo) + _L0_ffn_ref(xn, L0_ffn_W_up, L0_ffn_W_gate, L0_ffn_W_down, L0_ffn_gate_inp)
    xn = _layernorm(x, axis=-1)
    x = x + _L1_attn_ref(xn, L1_attn_cos, L1_attn_sin, L1_attn_Wq, L1_attn_Wk, L1_attn_Wv, L1_attn_Wo) + _L1_ffn_ref(xn, L1_ffn_gate_w, L1_ffn_w1, L1_ffn_w2, L1_ffn_w3, L1_ffn_ws1, L1_ffn_ws2, L1_ffn_ws3)
    return x

_drawn_inputs = setup_inputs


def setup_inputs(seed=0):
    import zlib

    import numpy as np

    out = dict(_drawn_inputs(seed))
    spreads = {}
    factors = {'L0_attn_Wq': 8.0,
     'L0_attn_Wk': 7.896,
     'L0_attn_Wv': 3.094,
     'L0_attn_Wo': 3.219,
     'L0_ffn_W_up': 3.334,
     'L0_ffn_W_gate': 3.113,
     'L0_ffn_W_down': 3.161,
     'L0_ffn_gate_inp': 3.601,
     'L1_attn_Wq': 8.0,
     'L1_attn_Wk': 8.0,
     'L1_attn_Wv': 8.0,
     'L1_attn_Wo': 8.0}
    for name, (base, spread) in spreads.items():
        noise = np.random.default_rng([zlib.crc32(name.encode()), seed]).standard_normal(out[name].shape)
        drawn = base * np.exp(spread * noise) if base else spread * noise
        out[name] = jnp.asarray(drawn.astype(out[name].dtype))
    for name, factor in factors.items():
        out[name] = (out[name] * factor).astype(out[name].dtype)
    return out
```

```python
from contextlib import ExitStack

import concourse.bass as bass
from concourse import mybir

F32 = mybir.dt.float32
F32R = mybir.dt.float32r
BF16 = mybir.dt.bfloat16
I32 = mybir.dt.int32
U32 = mybir.dt.uint32
ALU = mybir.AluOpType
ACT = mybir.ActivationFunctionType
AX = mybir.AxisListType

P = 128
D = 256
CC = D // P
BANK = 512
NEG = -3.0e38
EPS_LN = 1e-5


class Moe:

    def __init__(self, tag, experts, choices, shared, hidden, tokens, ring):
        self.tag = tag
        self.router = experts
        self.E = experts + shared
        self.top = choices
        self.K = choices + shared
        self.H = hidden
        self.HP = 112 if hidden % P else P
        self.HB = hidden // self.HP
        self.NT = tokens // P
        routed = (tokens * choices + experts * (P - 1)) // P
        self.tiles = routed + shared * self.NT
        self.ring = ring


def at_least(eng, sem, value):
    if not isinstance(value, int) or value > 0:
        eng.wait_ge(sem, value)


def run_tiles(eng, m, parts):
    n = m.tiles

    def written_out(t):
        parts(m, t, dict(half=t % 2, ug=t < n, hid=1 <= t <= n, row=t + 1 < n, down=2 <= t <= n + 1, store=3 <= t,
                         gathered=16 * ((t + 1) // 2 + 1), stored=16 * ((t - 2) // 2)))

    assert n % 2
    for t in range(4):
        written_out(t)
    with eng.Fori(4, n - 1, 2) as i:
        for u in range(2):
            parts(m, i + u, dict(half=u, ug=True, hid=True, row=True, down=True, store=True,
                                 gathered=i * 8 + 16 * (u + 1), stored=i * 8 - 16))
    for t in range(n - 1, n + 3):
        written_out(t)


def group_order(i):
    s, rest = divmod(i, 8)
    pair, qt = divmod(rest, 4)
    return 2 * pair + s, qt


def build(nc, a, out):
    NTOK = a["x"].shape[0]
    NT = NTOK // P
    NB = 2
    S = NTOK // NB
    TPS = S // P
    HD = 16
    KV = 4
    GRP = 4
    G = NB * KV
    SCALE = HD ** -0.5

    m0 = Moe("m0", 16, 4, 0, 448, NTOK, 2)
    m1 = Moe("m1", 8, 2, 1, 128, NTOK, 4)
    m0.wug_dram, m0.wd_dram = a["wug0"], a["wd0"]
    m1.wug_dram, m1.wd_dram = a["wug1"], a["wd1"]

    unit_of, units = {}, []
    for step in range(-2, G + 1):
        if step + 2 < G:
            units += [("max", step + 2, i) for i in range(16)] + [("neg", step + 2, 0)]
        if step >= 1:
            units.append(("out", step - 1, 0))
    for n, unit in enumerate(units):
        unit_of[unit] = n

    with ExitStack() as ctx:
        def sb(name, shape, dt=F32):
            return ctx.enter_context(nc.sbuf_tensor(name, shape, dt))

        def sem(name):
            return ctx.enter_context(nc.semaphore(name))

        ps = ctx.enter_context(nc.psum_tensor("ps", [P, 8, BANK], F32))

        ident = sb("ident", [P, P])
        identb = sb("identb", [P, P], BF16)
        onesb = sb("onesb", [P, P], BF16)
        before = sb("before", [P, P], BF16)
        mask_qk = sb("mask_qk", [P, P], BF16)
        mask_kq = sb("mask_kq", [P, P], BF16)
        same_head = sb("same_head", [P, P])
        tokid = sb("tokid", [P, NT])
        iota_e = sb("iota_e", [P, m0.E])
        iota_t = sb("iota_t", [1, m0.tiles])
        zeros = sb("zeros", [P, m0.tiles])

        acc = sb("acc", [P, NT, D])
        xn = sb("xn", [P, NT, D])
        xT = sb("xT", [P, CC, NTOK])
        bn = sb("bn", [P, NT, 6])
        mv = sb("mv", [P, NT, 2])
        rstd = sb("rstd", [P, 4, NT])

        wq0, wk0, wv0, wo0 = (sb(n, [P, CC, w]) for n, w in (("wq0", D), ("wk0", KV * HD), ("wv0", KV * HD), ("wo0", D)))
        wq1, wkv1, wo1 = (sb(n, [P, CC, w]) for n, w in (("wq1", D), ("wkv1", 2 * D), ("wo1", D)))

        qa = sb("qa", [P, 8, NTOK], F32R)
        ka = sb("ka", [P, KV, NTOK], F32R)
        vaug = sb("vaug", [P, NT, KV, 2 * HD])
        rowmax = sb("rowmax", [P, G, 16])
        nmax = sb("nmax", [16, 2, G, P], F32R)
        pT = sb("pT", [P, 2, GRP, S])
        oT = sb("oT", [P, 2, S])
        rsum = sb("rsum", [P, 2, TPS, GRP])
        vf = sb("vf", [P, NT, CC, P + 1])
        qhl = pT[:].rearrange("p a j n -> p (a j n)").rearrange("p (w c n) -> p w c n", w=2, c=CC).bitcast(F32R)
        khl = vf[:].rearrange("p t c n -> p (t c n)")[0:KV * HD, 0:2 * NTOK].rearrange("p (w n) -> p w n", w=2).bitcast(F32R)

        xg = sb("xg", [P, 2, D])
        xgT = sb("xgT", [P, 2, CC, P])
        th = sb("th", [P, 2, m0.H])
        ga = sb("ga", [P, 2, m0.H])
        hh = sb("hh", [P, 2, m0.H])
        hT = sb("hT", [P, 2, m0.HB, P])
        ysb = sb("ysb", [P, 2, D])
        yk = sb("yk", [P, 4, D])

        kf = pT[:, 0].rearrange("p j n -> p (j n)").rearrange("p (t c) -> p t c", t=NT)
        qf = pT[:, 1].rearrange("p j n -> p (j n)").rearrange("p (c n) -> p c n", c=CC)
        kvd = oT[:].rearrange("p a n -> p (a n)").rearrange("p (b c w n) -> p b c w n", b=NB, c=CC, w=2)
        emin = sb("emin", [P, 2, BANK])

        for m in (m0, m1):
            t = m.tag
            m.gate = sb(t + "gate", [P, CC, m.router])
            m.logits = sb(t + "logits", [P, NT, m.router])
            m.best = sb(t + "best", [P, NT, 8])
            m.index = sb(t + "index", [P, NT, 8], U32)
            m.choice = sb(t + "choice", [P, NT, m.K])
            m.weight = sb(t + "weight", [P, NT, 8])
            m.wsum = sb(t + "wsum", [P, 2, NT])
            m.onehot = sb(t + "onehot", [P, m.K, NT, m.E])
            m.member = sb(t + "member", [P, NT, m.E], BF16)
            m.earlier = sb(t + "earlier", [P, NT + 1, m.E], BF16)
            m.cnt = sb(t + "cnt", [P, 4, m.E])
            m.cnti = sb(t + "cnti", [P, 2, m.E], I32)
            m.slot = sb(t + "slot", [P, NT, m.E])
            m.slotk = sb(t + "slotk", [P, m.K, NT])
            m.sloti = sb(t + "sloti", [P, m.K, NT], U32)
            m.cmp = sb(t + "cmp", [1, m.tiles, m.E])
            m.tile_e = sb(t + "tile_e", [1, m.tiles])
            m.tab = sb(t + "tab", [1, 3, m.tiles], I32)
            m.cum = sb(t + "cum", [1, m.E], I32)
            m.idrow = sb(t + "idrow", [m.tiles, P])
            m.ids = sb(t + "ids", [P, m.tiles], U32)
            m.wug = sb(t + "wug", [P, m.ring, CC, 2, m.H])
            m.wd = sb(t + "wd", [m.HP, m.ring, m.HB, D])
            m.x_dram = nc.dram_tensor(t + "x", [NTOK, D], F32, kind="Internal").ap()
            m.id_dram = nc.dram_tensor(t + "id", [m.tiles * P, 1], F32, kind="Internal").ap()
            m.y_dram = nc.dram_tensor(t + "y", [m.tiles * P, D], F32, kind="Internal").ap()

            m.w_loaded = sem(t + "w_loaded")
            m.xn_stored = sem(t + "xn_stored")
            m.id_zeroed = sem(t + "id_zeroed")
            m.id_placed = sem(t + "id_placed")
            m.id_loaded = sem(t + "id_loaded")
            m.ids_ps = sem(t + "ids_ps")
            m.ids_ready = sem(t + "ids_ready")
            m.lg_ps = sem(t + "lg_ps")
            m.ex_in = sem(t + "ex_in")
            m.ex_out = sem(t + "ex_out")
            m.member_ready = sem(t + "member_ready")
            m.rank_ps = sem(t + "rank_ps")
            m.slots_ready = sem(t + "slots_ready")
            m.tab_ready = sem(t + "tab_ready")
            m.gathered = [sem(t + f"gathered{i}") for i in range(2)]
            m.x_ps = sem(t + "x_ps")
            m.x_sb = sem(t + "x_sb")
            m.g_ps = sem(t + "g_ps")
            m.u_ps = sem(t + "u_ps")
            m.th_sb = sem(t + "th_sb")
            m.ga_sb = sem(t + "ga_sb")
            m.h_sb = sem(t + "h_sb")
            m.h_ps = sem(t + "h_ps")
            m.hT_sb = sem(t + "hT_sb")
            m.y_ps = sem(t + "y_ps")
            m.y_sb = sem(t + "y_sb")
            m.y_out = [sem(t + f"y_out{i}") for i in range(2)]
            m.back = [sem(t + f"back{i}") for i in range(4)]
            m.added = sem(t + "added")

        x_in = [sem(f"x_in{i}") for i in range(NB)]
        w_in0, w_in1 = sem("w_in0"), sem("w_in1")
        g_in = sem("g_in")
        const = sem("const")
        pool_c = sem("pool_c")
        dve_c = sem("dve_c")
        var_ready = sem("var_ready")
        std_ready = sem("std_ready")
        xn_ready = sem("xn_ready")
        xT_ps = sem("xT_ps")
        xT_act, xT_dve = sem("xT_act"), sem("xT_dve")
        q_ps, q_hi, q_lo = sem("q_ps"), sem("q_hi"), sem("q_lo")
        k_ps, k_hi, k_lo = sem("k_ps"), sem("k_hi"), sem("k_lo")
        v_ps, v_sb = sem("v_ps"), sem("v_sb")
        qa_in, ka_in = sem("qa_in"), sem("ka_in")
        s_ps, s_read = sem("s_ps"), sem("s_read")
        nmax_ready = sem("nmax_ready")
        nmax_in = [sem(f"nmax_in{i}") for i in range(G)]
        st_ps, p_sb = sem("st_ps"), sem("p_sb")
        o_sb = sem("o_sb")
        pv_used = sem("pv_used")
        o_norm = sem("o_norm")
        ot_ps, ot_sb = sem("ot_ps"), sem("ot_sb")
        wo_ps, wo_add = sem("wo_ps"), sem("wo_add")
        q1_ps, q1_min, q1_exp, q1_f = sem("q1_ps"), sem("q1_min"), sem("q1_exp"), sem("q1_f")
        k1_ps, v1_sb, k1_min, k1_exp, k1_f = sem("k1_ps"), sem("v1_sb"), sem("k1_min"), sem("k1_exp"), sem("k1_f")
        kv_ps, kv_sb = sem("kv_ps"), sem("kv_sb")
        nd_ps, nd_read = sem("nd_ps"), sem("nd_read")
        wo1_ps, wo1_add = sem("wo1_ps"), sem("wo1_add")
        out_done = sem("out_done")

        block = ctx.enter_context(nc.Block())
        N_CONST = 10

        @block.sync
        def _(sp):
            x_t = a["x"].rearrange("(t p) c -> p t c", p=P)
            for b in range(NB):
                sp.dma_start(acc[:, b * TPS:(b + 1) * TPS, :], x_t[:, b * TPS:(b + 1) * TPS, :]).then_inc(x_in[b], 16)
            chunked = "(a p) n -> p a n"
            sp.dma_start(m0.gate[:], a["gate0"].rearrange(chunked, p=P)).then_inc(g_in, 16)
            sp.dma_start(m1.gate[:], a["gate1"].rearrange(chunked, p=P)).then_inc(g_in, 16)
            for dst, name in ((wq0, "wq0"), (wk0, "wk0"), (wv0, "wv0"), (wo0, "wo0")):
                sp.dma_start(dst[:], a[name].rearrange(chunked, p=P)).then_inc(w_in0, 16)
            for dst, name in ((wq1, "wq1"), (wkv1, "wkv1"), (wo1, "wo1")):
                sp.dma_start(dst[:], a[name].rearrange(chunked, p=P)).then_inc(w_in1, 16)

            def load_expert(m, e, slot):
                sp.dma_start(m.wug[:, slot], m.wug_dram[e]).then_inc(m.w_loaded, 16)
                sp.dma_start(m.wd[:, slot], m.wd_dram[e]).then_inc(m.w_loaded, 16)

            def zero_ids(m):
                sp.dma_start(m.id_dram.rearrange("(p t) o -> p (t o)", p=P), zeros[:, 0:m.tiles]).then_inc(m.id_zeroed, 16)

            def first_experts(m):
                for e in range(m.ring):
                    if e:
                        sp.wait_ge(m.w_loaded, 32 * e)
                    load_expert(m, e, e)

            def store_xn(m, n):
                sp.wait_ge(xn_ready, NT * (n + 1))
                sp.dma_start(m.x_dram.rearrange("(t p) c -> p t c", p=P), xn[:]).then_inc(m.xn_stored, 16)

            def load_ids(m):
                sp.wait_ge(m.id_placed, 16 * m.K * NT)
                sp.dma_start(m.idrow[:], m.id_dram.rearrange("(t p) o -> t (p o)", p=P)).then_inc(m.id_loaded, 16)

            def other_experts(m):
                sp.wait_ge(m.tab_ready, 1)
                for e in range(m.ring, m.E):
                    sp.wait_ge(m.w_loaded, 32 * e)
                    used = nc.sync.value_load(m.cum[0:1, e - m.ring:e - m.ring + 1], min_val=1, max_val=m.tiles + 1)
                    sp.wait_ge(m.y_ps, used)
                    load_expert(m, e, e % m.ring)

            sp.wait_ge(const, N_CONST)
            zero_ids(m0)
            zero_ids(m1)
            first_experts(m0)
            first_experts(m1)
            store_xn(m0, 0)
            for b in range(NB):
                sp.wait_ge(k_lo, b + 1)
                cols = slice(b * S, (b + 1) * S)
                for s in range(2):
                    for part, r in ((0, 0), (1, 1), (0, 2)):
                        for j in range(KV):
                            sp.dma_start(ka[64 * s + HD * r:64 * s + HD * (r + 1), j, cols].bitcast(F32),
                                         khl[HD * j:HD * (j + 1), part, cols].bitcast(F32)).then_inc(ka_in, 16)
            for h in range(16):
                if h % 8 == 0:
                    sp.wait_ge(q_lo, 2 * (h // 8) + 2)
                for part, r in ((0, 0), (0, 1), (1, 2)):
                    sp.dma_start(qa[64 * (h % 2) + HD * r:64 * (h % 2) + HD * (r + 1), h // 2, :].bitcast(F32),
                                 qhl[HD * (h % 8):HD * (h % 8 + 1), part, h // 8, :].bitcast(F32)).then_inc(qa_in, 16)
            load_ids(m0)
            other_experts(m0)
            for g in range(G):
                sp.wait_ge(nmax_ready, 2 * (g + 1))
                b, kv = divmod(g, KV)
                for s in range(2):
                    for part in range(2):
                        row = 64 * s + 3 * HD + part
                        for pair in range(2):
                            sp.dma_start(qa[row:row + 1, 2 * kv + pair, b * S:(b + 1) * S].bitcast(F32),
                                         nmax[8 * s + 4 * pair:8 * s + 4 * pair + 4, part, g, :].bitcast(F32)).then_inc(nmax_in[g], 16)
            store_xn(m1, 1)
            load_ids(m1)
            other_experts(m1)
            for t in range(NT):
                sp.wait_ge(m1.added, m1.K * (t + 1))
                sp.dma_start(out[t * P:(t + 1) * P, :], acc[:, t, :]).then_inc(out_done, 16)
            sp.wait_ge(out_done, 16 * NT)

        @block.gpsimd
        def _(pool):
            pool.memset(zeros[:], 0.0).then_inc(const, 1)
            pool.memset(ident[:], 0.0).then_inc(pool_c, 1)
            pool.memset(onesb[:], 1.0).then_inc(const, 1)
            pool.memset(before[:], 0.0).then_inc(pool_c, 1)
            pool.memset(mask_qk[:], 0.0).then_inc(pool_c, 1)
            pool.memset(mask_kq[:], 0.0).then_inc(pool_c, 1)
            pool.memset(same_head[:], 1.0).then_inc(pool_c, 1)
            pool.iota(tokid[:], [[P, NT]], base=0, channel_multiplier=1,
                      allow_small_or_imprecise_dtypes=True).then_inc(const, 1)
            pool.iota(iota_e[:], [[1, m0.E]], base=0, channel_multiplier=0,
                      allow_small_or_imprecise_dtypes=True).then_inc(const, 1)
            pool.iota(iota_t[:], [[1, m0.tiles]], base=0, channel_multiplier=0,
                      allow_small_or_imprecise_dtypes=True).then_inc(const, 1)
            pool.wait_ge(pool_c, 5)
            pool.affine_select(out=ident[:], in_=ident[:], compare_op=ALU.not_equal, fill=1.0, base=0,
                               pattern=[[-1, P]], channel_multiplier=1).then_inc(pool_c, 1)
            pool.affine_select(out=before[:], in_=before[:], compare_op=ALU.is_ge, fill=1.0, base=0,
                               pattern=[[-1, P]], channel_multiplier=1).then_inc(const, 1)
            pool.affine_select(out=mask_qk[:], in_=mask_qk[:], compare_op=ALU.is_ge, fill=NEG, base=0,
                               pattern=[[-1, P]], channel_multiplier=1).then_inc(const, 1)
            pool.affine_select(out=mask_kq[:], in_=mask_kq[:], compare_op=ALU.is_ge, fill=NEG, base=0,
                               pattern=[[1, P]], channel_multiplier=-1).then_inc(const, 1)
            heads = same_head[:].rearrange("p (h d) -> p h d", d=HD)
            pool.affine_select(out=heads, in_=heads, compare_op=ALU.is_ge, fill=0.0, base=0,
                               pattern=[[-HD, P // HD], [0, HD]], channel_multiplier=1).then_inc(pool_c, 1)
            pool.wait_ge(pool_c, 7)
            pool.tensor_copy(identb[:], ident[:]).then_inc(const, 1)
            pool.affine_select(out=heads, in_=heads, compare_op=ALU.is_ge, fill=0.0, base=HD - 1,
                               pattern=[[HD, P // HD], [0, HD]], channel_multiplier=-1).then_inc(const, 1)

            def place_ids(m):
                pool.wait_ge(m.slots_ready, 1)
                pool.wait_ge(m.id_zeroed, 16)
                for k in range(m.K):
                    for t in range(NT):
                        pool.indirect_dma_start(
                            out=m.id_dram, out_offset=bass.IndirectOffsetOnAxis(ap=m.sloti[:, k, t:t + 1], axis=0),
                            in_=tokid[:, t:t + 1], in_offset=None).then_inc(m.id_placed, 16)

            def gather_rows(m):
                pool.wait_ge(m.ids_ready, 1)
                pool.wait_ge(m.xn_stored, 16)
                for t in range(m.tiles):
                    at_least(pool, m.x_ps, t - 1)
                    pool.indirect_dma_start(
                        out=xg[:, t % 2, :], out_offset=None, in_=m.x_dram,
                        in_offset=bass.IndirectOffsetOnAxis(ap=m.ids[:, t:t + 1], axis=0)).then_inc(m.gathered[t % 2], 16)

            def gather_back(m):
                pool.wait_ge(m.y_out[0], 16 * ((m.tiles + 1) // 2))
                pool.wait_ge(m.y_out[1], 16 * (m.tiles // 2))
                n = 0
                for t in range(NT):
                    for k in range(m.K):
                        at_least(pool, m.added, n - 3)
                        pool.indirect_dma_start(
                            out=yk[:, n % 4, :], out_offset=None, in_=m.y_dram,
                            in_offset=bass.IndirectOffsetOnAxis(ap=m.sloti[:, k, t:t + 1], axis=0)).then_inc(m.back[n % 4], 16)
                        n += 1

            for m in (m0, m1):
                place_ids(m)
                gather_rows(m)
                gather_back(m)

        @block.scalar
        def _(act):
            def sqrt_var(n):
                act.wait_ge(var_ready, n + 1)
                nc.scalar.activation(rstd[:, 1, :], rstd[:, 0, :], ACT.Sqrt).then_inc(std_ready, 1)

            def evacuate_xT(n):
                for half in range(2):
                    act.wait_ge(xT_ps, NT * n + TPS * (half + 1))
                    nc.scalar.copy(xT[:, 0, half * S:(half + 1) * S], ps[:, half, :]).then_inc(xT_act, 1)

            def route_exp(m):
                act.wait_ge(m.ex_in, 1)
                nc.scalar.activation(m.weight[:], m.weight[:], ACT.Exp).then_inc(m.ex_out, 1)

            def rows(m, t, half):
                act.wait_ge(m.x_ps, t + 1)
                at_least(act, m.u_ps, t - 1)
                nc.scalar.copy(xgT[:, half], ps[:, 4, 0:CC * P].rearrange("p (c n) -> p c n", n=P)).then_inc(m.x_sb, 1)

            def tile_parts(m, t, p):
                if p["ug"]:
                    act.wait_ge(m.g_ps, t + 1)
                    at_least(act, m.ga_sb, t - 1)
                    nc.scalar.activation(th[:, p["half"], 0:m.H], ps[:, 2 + p["half"], 0:m.H], ACT.Tanh,
                                         scale=0.5).then_inc(m.th_sb, 1)
                if p["store"]:
                    act.wait_ge(m.y_sb, t - 2)
                    act.dma_start(m.y_dram[bass.ds((t - 3) * P, P), :],
                                  ysb[:, 1 - p["half"], :]).then_inc(m.y_out[1 - p["half"]], 16)
                if p["hid"]:
                    act.wait_ge(m.h_ps, t)
                    at_least(act, m.y_ps, t - 1)
                    nc.scalar.copy(hT[0:m.HP, 1 - p["half"], 0:m.HB, :],
                                   ps[0:m.HP, 5, 0:m.HB * P].rearrange("p (b n) -> p b n", n=P)).then_inc(m.hT_sb, 1)
                if p["row"]:
                    rows(m, t + 1, 1 - p["half"])

            sqrt_var(0)
            evacuate_xT(0)
            route_exp(m0)
            for c in range(2 * CC):
                act.wait_ge(q_ps, c + 1)
                mm, b = c // 2, c % 2
                nc.scalar.activation(qhl[:, 0, mm, b * S:(b + 1) * S], ps[:, (5 + c) % 8, :], ACT.Copy,
                                     scale=SCALE).then_inc(q_hi, 1)
            for b in range(NB):
                act.wait_ge(k_ps, b + 1)
                nc.scalar.copy(khl[:, 0, b * S:(b + 1) * S], ps[0:KV * HD, 1 + b, :]).then_inc(k_hi, 1)
            rows(m0, 0, 0)
            run_tiles(act, m0, tile_parts)
            for g in range(G):
                for kb in range(TPS):
                    for pair in range(2):
                        n = (g * TPS + kb) * 2 + pair
                        act.wait_ge(st_ps, n + 1)
                        at_least(act, pv_used, g * TPS + kb - 1)
                        first = 3 + 2 * (n % 2)
                        nc.scalar.activation(pT[:, kb % 2, 2 * pair:2 * pair + 2, kb * P:S],
                                             ps[:, first:first + 2, kb * P:S], ACT.Exp).then_inc(p_sb, 1)
                act.wait_ge(pv_used, TPS * (g + 1))
                if g >= 2:
                    act.wait_ge(s_ps, unit_of["out", g - 2, 0] + 1)
                nc.scalar.copy(oT[:, g % 2, :], ps[:, 7, :]).then_inc(o_sb, 1)
            sqrt_var(1)
            evacuate_xT(1)
            route_exp(m1)
            for c in range(2 * CC):
                act.wait_ge(q1_min, c + 1)
                nc.scalar.activation(emin[:, c % 2, :], emin[:, c % 2, :], ACT.Exp).then_inc(q1_exp, 1)
            for t in range(NT):
                act.wait_ge(k1_ps, t + 1)
                nc.scalar.copy(vf[:, t, :, 0:P], ps[:, 1 + t % 3, D:2 * D].rearrange("p (c n) -> p c n", n=P)).then_inc(v1_sb, 1)
                act.wait_ge(k1_min, t + 1)
                nc.scalar.activation(emin[:, t % 2, 0:D], emin[:, t % 2, 0:D], ACT.Exp).then_inc(k1_exp, 1)
            rows(m1, 0, 0)
            run_tiles(act, m1, tile_parts)

        @block.vector
        def _(dve):
            chain = [0]

            def link(ins):
                chain[0] += 1
                ins.then_inc(dve_c, 1)
                dve.wait_ge(dve_c, chain[0])

            def layernorm(n):
                for t in range(NT):
                    if n == 0 and t % TPS == 0:
                        dve.wait_ge(x_in[t // TPS], 16)
                    last = nc.vector.bn_stats(bn[:, t, :], acc[:, t, :])
                link(last)
                for t in range(NT):
                    last = nc.vector.bn_aggr(mv[:, t, :], bn[:, t, :])
                link(last)
                nc.vector.tensor_scalar(rstd[:, 0, :], mv[:, :, 1], EPS_LN, None, ALU.add).then_inc(var_ready, 1)
                dve.wait_ge(std_ready, n + 1)
                link(nc.vector.reciprocal(rstd[:, 2, :], rstd[:, 1, :]))
                link(nc.vector.tensor_tensor(rstd[:, 3, :], rstd[:, 2, :], rstd[:, 2, :], ALU.mult))
                link(nc.vector.tensor_tensor(rstd[:, 3, :], rstd[:, 3, :], rstd[:, 0, :], ALU.mult))
                link(nc.vector.tensor_scalar(rstd[:, 3, :], rstd[:, 3, :], -0.5, 1.5, ALU.mult, ALU.add))
                link(nc.vector.tensor_tensor(rstd[:, 2, :], rstd[:, 2, :], rstd[:, 3, :], ALU.mult))
                if n:
                    dve.wait_ge(ot_ps, CC * 2)
                for t in range(NT):
                    nc.vector.tensor_scalar(xn[:, t, :], acc[:, t, :], mv[:, t, 0:1], rstd[:, 2, t:t + 1],
                                            ALU.subtract, ALU.mult).then_inc(xn_ready, 1)

            def evacuate_xT(n):
                for half in range(2):
                    dve.wait_ge(xT_ps, NT * n + TPS * (half + 1))
                    nc.vector.tensor_copy(xT[:, 1, half * S:(half + 1) * S], ps[:, 2 + half, :]).then_inc(xT_dve, 1)

            def choose(m):
                top, K, E = m.top, m.K, m.E
                dve.wait_ge(m.lg_ps, 1)
                link(nc.vector.tensor_copy(m.logits[:], ps[:, 4, 0:NT * m.router].rearrange("p (t e) -> p t e", t=NT)))
                for t in range(NT):
                    last = nc.vector.max(m.best[:, t, :], m.logits[:, t, :])
                link(last)
                for t in range(NT):
                    last = nc.vector.max_index(m.index[:, t, :], m.best[:, t, :], m.logits[:, t, :])
                link(last)
                nc.vector.tensor_tensor(m.weight[:], m.best[:], m.best[:, :, 0:1].to_broadcast([P, NT, 8]),
                                        ALU.subtract).then_inc(m.ex_in, 1)
                link(nc.vector.tensor_copy(m.choice[:, :, 0:top], m.index[:, :, 0:top]))
                if K > top:
                    link(nc.vector.memset(m.choice[:, :, top:K], float(m.router)))
                for k in range(K):
                    last = nc.vector.tensor_tensor(
                        m.onehot[:, k], m.choice[:, :, k:k + 1].to_broadcast([P, NT, E]),
                        iota_e[:, 0:E].unsqueeze(1).to_broadcast([P, NT, E]), ALU.is_equal)
                link(last)
                link(nc.vector.tensor_tensor(m.member[:], m.onehot[:, 0], m.onehot[:, 1], ALU.add))
                for k in range(2, K):
                    link(nc.vector.tensor_tensor(m.member[:], m.member[:], m.onehot[:, k], ALU.add))
                link(nc.vector.memset(m.earlier[:, 0, :], 0.0))
                for t in range(NT - 1):
                    link(nc.vector.tensor_tensor(m.earlier[:, t + 1, :], m.earlier[:, t, :], m.member[:, t, :], ALU.add))
                nc.vector.tensor_tensor(m.earlier[:, NT, :], m.earlier[:, NT - 1, :], m.member[:, NT - 1, :],
                                        ALU.add).then_inc(m.member_ready, 1)
                dve.wait_ge(m.ex_out, 1)
                n_sum = top if K == top else m.router
                link(nc.vector.tensor_reduce(m.wsum[:, 0, :], m.weight[:, :, 0:n_sum], AX.X, ALU.add))
                link(nc.vector.reciprocal(m.wsum[:, 1, :], m.wsum[:, 0, :]))
                link(nc.vector.tensor_tensor(m.weight[:, :, 0:top], m.weight[:, :, 0:top],
                                             m.wsum[:, 1, :].unsqueeze(2).to_broadcast([P, NT, top]), ALU.mult))
                if K > top:
                    link(nc.vector.memset(m.weight[:, :, top:K], 1.0))

            def slots(m):
                K, E = m.K, m.E
                dve.wait_ge(m.rank_ps, 1)
                count = ps[:, 4, NT * E:(NT + 1) * E]
                link(nc.vector.tensor_scalar(m.cnti[:, 0, :], count, float(P - 1), None, ALU.add))
                link(nc.vector.tensor_scalar(m.cnti[:, 1, :], m.cnti[:, 0, :], 7, None, ALU.logical_shift_right))
                link(nc.vector.tensor_copy(m.cnt[:, 1, :], m.cnti[:, 1, :]))
                link(nc.vector.memset(m.cnt[:, 0, :], 1.0))
                link(nc.vector.tensor_tensor_scan(m.cnt[:, 2, :], m.cnt[:, 0, :], m.cnt[:, 1, :], 0.0, ALU.mult, ALU.add))
                link(nc.vector.tensor_tensor(m.cnt[:, 3, :], m.cnt[:, 2, :], m.cnt[:, 1, :], ALU.subtract))
                link(nc.vector.tensor_scalar(m.cnt[:, 3, :], m.cnt[:, 3, :], float(P), None, ALU.mult))
                link(nc.vector.tensor_tensor(m.slot[:], ps[:, 4, 0:NT * E].rearrange("p (t e) -> p t e", t=NT),
                                             m.cnt[:, 3:4, :].to_broadcast([P, NT, E]), ALU.add))
                for k in range(K):
                    last = nc.vector.tensor_tensor(m.onehot[:, k], m.onehot[:, k], m.slot[:], ALU.mult)
                link(last)
                link(nc.vector.tensor_reduce(m.slotk[:], m.onehot[:], AX.X, ALU.add))
                nc.vector.tensor_copy(m.sloti[:], m.slotk[:]).then_inc(m.slots_ready, 1)
                link(nc.vector.tensor_tensor(m.cmp[:], m.cnt[0:1, 2:3, :].to_broadcast([1, m.tiles, E]),
                                             iota_t[:, 0:m.tiles].unsqueeze(2).to_broadcast([1, m.tiles, E]), ALU.is_le))
                link(nc.vector.tensor_reduce(m.tile_e[:], m.cmp[:], AX.X, ALU.add))
                link(nc.vector.tensor_scalar(m.tab[:, 0, :], m.tile_e[:], float(E - 1), None, ALU.min))
                link(nc.vector.tensor_scalar(m.tab[:, 1, :], m.tab[:, 0, :], 32.0, 32.0, ALU.mult, ALU.add))
                link(nc.vector.tensor_scalar(m.cum[:], m.cnt[0:1, 2, :], 1.0, None, ALU.add))
                nc.vector.tensor_scalar(m.tab[:, 2, :], m.tab[:, 0, :], m.ring - 1, None, ALU.bitwise_and).then_inc(m.tab_ready, 1)

            def integer_ids(m):
                dve.wait_ge(m.ids_ps, 1)
                nc.vector.tensor_copy(m.ids[:], ps[:, 4, 0:m.tiles]).then_inc(m.ids_ready, 1)

            def tile_parts(m, t, p):
                half = p["half"]
                if p["ug"]:
                    dve.wait_ge(m.th_sb, t + 1)
                    nc.vector.scalar_tensor_tensor(out=ga[:, half, 0:m.H], in0=th[:, half, 0:m.H], scalar=1.0,
                                                   in1=ps[:, 2 + half, 0:m.H], op0=ALU.add, op1=ALU.mult).then_inc(m.ga_sb, 1)
                    dve.wait_ge(m.ga_sb, t + 1)
                    dve.wait_ge(m.u_ps, t + 1)
                    at_least(dve, m.h_ps, t - 1)
                    nc.vector.scalar_tensor_tensor(out=hh[:, half, 0:m.H], in0=ga[:, half, 0:m.H], scalar=0.5,
                                                   in1=ps[:, half, 0:m.H], op0=ALU.mult, op1=ALU.mult).then_inc(m.h_sb, 1)
                if p["down"]:
                    dve.wait_ge(m.y_ps, t)
                    at_least(dve, m.y_out[half], p["stored"])
                    nc.vector.tensor_copy(ysb[:, half, :], ps[:, 6, 0:D]).then_inc(m.y_sb, 1)

            def combine(m, pairs):
                for n in pairs:
                    t, k = divmod(n, m.K)
                    dve.wait_ge(m.back[n % 4], 16 * (n // 4 + 1))
                    at_least(dve, m.added, n)
                    ins = nc.vector.scalar_tensor_tensor(out=acc[:, t, :], in0=yk[:, n % 4, :], scalar=m.weight[:, t, k:k + 1],
                                                         in1=acc[:, t, :], op0=ALU.mult, op1=ALU.add)
                    ins.then_inc(m.added, 1)

            dve.wait_ge(const, N_CONST)
            nc.vector.memset(vaug[:], 1.0)
            link(nc.vector.memset(ka[:].bitcast(F32), 1.0))
            layernorm(0)
            evacuate_xT(0)
            choose(m0)
            for b in range(NB):
                dve.wait_ge(k_hi, b + 1)
                nc.vector.tensor_tensor(khl[:, 1, b * S:(b + 1) * S], ps[0:KV * HD, 1 + b, :],
                                        khl[:, 0, b * S:(b + 1) * S].bitcast(F32), ALU.subtract).then_inc(k_lo, 1)
            slots(m0)
            for c in range(2 * CC):
                dve.wait_ge(q_hi, c + 1)
                mm, b = c // 2, c % 2
                nc.vector.scalar_tensor_tensor(out=qhl[:, 1, mm, b * S:(b + 1) * S], in0=ps[:, (5 + c) % 8, :], scalar=SCALE,
                                               in1=qhl[:, 0, mm, b * S:(b + 1) * S].bitcast(F32),
                                               op0=ALU.mult, op1=ALU.subtract).then_inc(q_lo, 1)
            dve.wait_ge(v_ps, 1)
            nc.vector.tensor_copy(vaug[:, :, :, 0:HD],
                                  ps[:, 3, :].rearrange("p (t h d) -> p t h d", t=NT, d=HD)).then_inc(v_sb, 1)
            integer_ids(m0)
            run_tiles(dve, m0, tile_parts)

            def row_max(g):
                for i in range(16):
                    j, qt = group_order(i)
                    n = unit_of["max", g, i]
                    dve.wait_ge(s_ps, n + 1)
                    nc.vector.tensor_reduce(rowmax[:, g, i:i + 1], ps[:, n % 3, 0:(qt + 1) * P], AX.X, ALU.max).then_inc(s_read, 1)

            def neg_max(g):
                n = unit_of["neg", g, 0]
                dve.wait_ge(s_ps, n + 1)
                nc.vector.tensor_scalar(nmax[:, 0, g, :], ps[0:16, n % 3, 0:P], -1.0, None, ALU.mult).then_inc(nmax_ready, 1)
                dve.wait_ge(nmax_ready, 2 * g + 1)
                nc.vector.scalar_tensor_tensor(out=nmax[:, 1, g, :], in0=ps[0:16, n % 3, 0:P], scalar=-1.0,
                                               in1=nmax[:, 0, g, :].bitcast(F32), op0=ALU.mult,
                                               op1=ALU.subtract).then_inc(nmax_ready, 1)

            def normalise(g):
                n = unit_of["out", g, 0]
                b, kv = divmod(g, KV)
                dve.wait_ge(s_ps, n + 1)
                made = ps[:, n % 3, :].rearrange("p (t j d) -> p t j d", t=TPS, d=2 * HD)
                link(nc.vector.reciprocal(rsum[:, g % 2], made[:, :, :, HD]))
                for t in range(TPS):
                    last = nc.vector.tensor_tensor(
                        xn[:, b * TPS + t, kv * 64:(kv + 1) * 64].rearrange("p (j d) -> p j d", d=HD),
                        made[:, t, :, 0:HD], rsum[:, g % 2, t, :].unsqueeze(2).to_broadcast([P, GRP, HD]), ALU.mult)
                last.then_inc(o_norm, 1)

            dve.wait_ge(m0.xn_stored, 16)
            for step in range(-2, G + 1):
                if 0 <= step + 2 < G:
                    row_max(step + 2)
                    neg_max(step + 2)
                if step >= 0:
                    combine(m0, range(4 * step, min(4 * step + 4, m0.K * NT)))
                if 1 <= step:
                    normalise(step - 1)
            for c in range(2 * CC):
                dve.wait_ge(ot_ps, c + 1)
                nc.vector.tensor_copy(xT[:, c // 2, (c % 2) * S:(c % 2 + 1) * S], ps[:, c, :]).then_inc(ot_sb, 1)
            dve.wait_ge(m0.added, m0.K * NT)
            for i in range(NT // 2):
                dve.wait_ge(wo_ps, i + 1)
                last = nc.vector.tensor_tensor(acc[:, 2 * i:2 * i + 2, :], ps[:, 4 + i, :].rearrange("p (t c) -> p t c", t=2),
                                               acc[:, 2 * i:2 * i + 2, :], ALU.add)
                last.then_inc(wo_add, 1)
            dve.wait_ge(wo_add, NT // 2)
            nc.vector.memset(vf[:], 1.0)
            layernorm(1)
            evacuate_xT(1)
            choose(m1)
            slots(m1)
            for c in range(2 * CC):
                dve.wait_ge(q1_ps, c + 1)
                bank = (5 + c) % 8
                at_least(dve, q1_f, c - 1)
                nc.vector.tensor_scalar(emin[:, c % 2, :], ps[:, bank, :], 0.0, None, ALU.min).then_inc(q1_min, 1)
                dve.wait_ge(q1_exp, c + 1)
                nc.vector.scalar_tensor_tensor(out=qf[:, c // 2, (c % 2) * S:(c % 2 + 1) * S], in0=ps[:, bank, :], scalar=0.0,
                                               in1=emin[:, c % 2, :], op0=ALU.max, op1=ALU.add).then_inc(q1_f, 1)
            dve.wait_ge(q1_f, 2 * CC)
            for t in range(NT):
                dve.wait_ge(v1_sb, t + 1)
                at_least(dve, k1_f, t - 1)
                nc.vector.tensor_scalar(emin[:, t % 2, 0:D], ps[:, 1 + t % 3, 0:D], 0.0, None, ALU.min).then_inc(k1_min, 1)
                dve.wait_ge(k1_exp, t + 1)
                nc.vector.scalar_tensor_tensor(out=kf[:, t, :], in0=ps[:, 1 + t % 3, 0:D], scalar=0.0,
                                               in1=emin[:, t % 2, 0:D], op0=ALU.max, op1=ALU.add).then_inc(k1_f, 1)
            for b in range(NB):
                dve.wait_ge(kv_ps, b + 1)
                for c in range(CC):
                    at = 2 * P * c
                    nc.vector.tensor_tensor(kvd[:, b, c, 0, :], ps[:, 5 + b, at:at + P], same_head[:], ALU.mult).then_inc(kv_sb, 1)
                    nc.vector.tensor_scalar(kvd[:, b, c, 1, :], same_head[:], ps[:, 5 + b, at + P:at + P + 1], None,
                                            ALU.mult).then_inc(kv_sb, 1)
            for c in range(2 * CC):
                b, mm = divmod(c, CC)
                dve.wait_ge(nd_ps, c + 1)
                link(nc.vector.tensor_scalar(emin[:, 0, :], ps[:, 2 * (c % 2) + 1, :], 1e-6, None, ALU.add))
                link(nc.vector.reciprocal(emin[:, 1, :], emin[:, 0, :]))
                nc.vector.tensor_tensor(xT[:, mm, b * S:(b + 1) * S], ps[:, 2 * (c % 2), :], emin[:, 1, :], ALU.mult).then_inc(nd_read, 1)
                dve.wait_ge(nd_read, c + 1)
            for i in range(NT // 2):
                dve.wait_ge(wo1_ps, i + 1)
                nc.vector.tensor_tensor(acc[:, 2 * i:2 * i + 2, :], ps[:, 4 + i, :].rearrange("p (t c) -> p t c", t=2),
                                        acc[:, 2 * i:2 * i + 2, :], ALU.add).then_inc(wo1_add, 1)
            dve.wait_ge(wo1_add, NT // 2)
            integer_ids(m1)
            run_tiles(dve, m1, tile_parts)
            combine(m1, range(m1.K * NT))

        @block.tensor
        def _(pe):
            mm_ = nc.tensor.matmul

            def transpose_x(n):
                if n:
                    pe.wait_ge(wo_add, NT // 2)
                for t in range(NT):
                    pe.wait_ge(xn_ready, NT * n + t + 1)
                    for c in range(CC):
                        last = nc.tensor.transpose(ps[:, 2 * c + t // TPS, (t % TPS) * P:(t % TPS + 1) * P],
                                                   xn[:, t, c * P:(c + 1) * P], ident[:])
                    last.then_inc(xT_ps, 1)

            def logits(m):
                for t in range(NT):
                    for c in range(CC):
                        last = mm_(ps[:, 4, t * m.router:(t + 1) * m.router], xT[:, c, t * P:(t + 1) * P], m.gate[:, c, :],
                                   start=c == 0, stop=c == CC - 1)
                last.then_inc(m.lg_ps, 1)

            def ranks(m):
                pe.wait_ge(m.member_ready, 1)
                n = NT * m.E
                mm_(ps[:, 4, 0:n + m.E], onesb[:], m.earlier[:].rearrange("p t e -> p (t e)"), start=True, stop=False,
                    skip_group_check=True)
                mm_(ps[:, 4, 0:n], before[:], m.member[:].rearrange("p t e -> p (t e)"), start=False, stop=True,
                    skip_group_check=True).then_inc(m.rank_ps, 1)

            def turn_ids(m):
                pe.wait_ge(m.id_loaded, 16)
                pe.wait_ge(m.tab_ready, 1)
                nc.tensor.transpose(ps[:, 4, 0:m.tiles], m.idrow[:], ident[0:m.tiles, 0:m.tiles]).then_inc(m.ids_ps, 1)

            def rows(m, t, half):
                pe.wait_ge(m.gathered[half[0]], half[1])
                at_least(pe, m.x_sb, t)
                for c in range(CC):
                    last = nc.tensor.transpose(ps[:, 4, c * P:(c + 1) * P], xg[:, half[0], c * P:(c + 1) * P], ident[:])
                last.then_inc(m.x_ps, 1)

            def tile_parts(m, t, p):
                half = p["half"]

                def slot_of(tile):
                    return nc.tensor.value_load(m.tab[0:1, 2, bass.ds(tile, 1)], min_val=0, max_val=m.ring - 1)

                if p["ug"]:
                    loaded = nc.tensor.value_load(m.tab[0:1, 1, bass.ds(t, 1)], min_val=32, max_val=32 * m.E)
                    slot = slot_of(t)
                    pe.wait_ge(m.w_loaded, loaded)
                    pe.wait_ge(m.x_sb, t + 1)
                    at_least(pe, m.h_sb, t - 1)
                    for which, bank, ready in ((1, 2 + half, m.g_ps), (0, half, m.u_ps)):
                        for c in range(CC):
                            last = mm_(ps[:, bank, 0:m.H], xgT[:, half, c, :],
                                       m.wug[:, bass.ds(slot, 1), c, which, :].rearrange("p a n -> p (a n)"),
                                       start=c == 0, stop=c == CC - 1)
                        last.then_inc(ready, 1)
                if p["hid"]:
                    pe.wait_ge(m.h_sb, t)
                    at_least(pe, m.hT_sb, t - 1)
                    for b in range(m.HB):
                        last = nc.tensor.transpose(ps[0:m.HP, 5, b * P:(b + 1) * P],
                                                   hh[:, 1 - half, b * m.HP:(b + 1) * m.HP], ident[:])
                    last.then_inc(m.h_ps, 1)
                if p["row"]:
                    rows(m, t + 1, (1 - half, p["gathered"]))
                if p["down"]:
                    slot = slot_of(t - 2)
                    pe.wait_ge(m.hT_sb, t - 1)
                    at_least(pe, m.y_sb, t - 2)
                    for b in range(m.HB):
                        last = mm_(ps[:, 6, 0:D], hT[0:m.HP, half, b, :],
                                   m.wd[:, bass.ds(slot, 1), b, :].rearrange("p a n -> p (a n)"),
                                   start=b == 0, stop=b == m.HB - 1)
                    last.then_inc(m.y_ps, 1)

            def first_rows(m):
                rows(m, 0, (0, 16))

            pe.sem_inc(m0.y_ps, 1)
            pe.sem_inc(m1.y_ps, 1)
            pe.wait_ge(const, N_CONST)
            transpose_x(0)
            pe.wait_ge(xT_act, 2)
            pe.wait_ge(xT_dve, 2)
            pe.wait_ge(g_in, 32)
            logits(m0)
            pe.wait_ge(w_in0, 64)
            for b in range(NB):
                for c in range(CC):
                    last = mm_(ps[0:KV * HD, 1 + b, :], wk0[:, c, :], xT[:, c, b * S:(b + 1) * S], start=c == 0, stop=c == CC - 1)
                last.then_inc(k_ps, 1)
            for i in range(2 * CC):
                mm, b = i // 2, i % 2
                for c in range(CC):
                    last = mm_(ps[:, (5 + i) % 8, :], wq0[:, c, mm * P:(mm + 1) * P], xT[:, c, b * S:(b + 1) * S],
                               start=c == 0, stop=c == CC - 1)
                last.then_inc(q_ps, 1)
            for t in range(NT):
                for c in range(CC):
                    last = mm_(ps[:, 3, t * 64:(t + 1) * 64], xT[:, c, t * P:(t + 1) * P], wv0[:, c, :], start=c == 0, stop=c == CC - 1)
            last.then_inc(v_ps, 1)
            ranks(m0)
            turn_ids(m0)
            pe.wait_ge(q_lo, 2 * CC)
            pe.wait_ge(k_lo, NB)
            pe.wait_ge(v_sb, 1)
            pe.wait_ge(m0.ids_ready, 1)
            first_rows(m0)
            run_tiles(pe, m0, tile_parts)

            pe.wait_ge(m0.h_sb, m0.tiles)
            pe.wait_ge(m0.hT_sb, m0.tiles)
            pe.wait_ge(m0.y_sb, m0.tiles)
            pe.wait_ge(ka_in, 16 * 24 * NB)
            pe.wait_ge(qa_in, 16 * 48)

            def free_unit(pe, n):
                if n >= 3:
                    kind, g, i = units[n - 3]
                    if kind == "max":
                        pe.wait_ge(s_read, 16 * g + i + 1)
                    elif kind == "neg":
                        pe.wait_ge(nmax_ready, 2 * g + 2)
                    else:
                        pe.wait_ge(o_norm, g + 1)

            def scores(g, i):
                j, qt = group_order(i)
                b, kv = divmod(g, KV)
                n = unit_of["max", g, i]
                free_unit(pe, n)
                bank, L = n % 3, (qt + 1) * P
                r = 64 * (j % 2)
                h = kv * GRP + j
                q0 = b * S + qt * P
                mm_(ps[:, bank, 0:L], qa[r:r + 3 * HD, h // 2, q0:q0 + P], ka[r:r + 3 * HD, kv, b * S:b * S + L],
                    start=True, stop=False, skip_group_check=True)
                mm_(ps[:, bank, qt * P:L], identb[:], mask_qk[:], start=False, stop=True,
                    skip_group_check=True).then_inc(s_ps, 1)

            def turn_max(g):
                n = unit_of["neg", g, 0]
                free_unit(pe, n)
                pe.wait_ge(s_read, 16 * (g + 1))
                nc.tensor.transpose(ps[0:16, n % 3, 0:P], rowmax[:, g, :], ident[:]).then_inc(s_ps, 1)

            def turn_out(g):
                n = unit_of["out", g, 0]
                free_unit(pe, n)
                pe.wait_ge(o_sb, g + 1)
                for t in range(TPS):
                    last = nc.tensor.transpose(ps[:, n % 3, t * P:(t + 1) * P], oT[:, g % 2, t * P:(t + 1) * P], ident[:])
                last.then_inc(s_ps, 1)

            def transposed_scores(g, kb, pair):
                b, kv = divmod(g, KV)
                n = (g * TPS + kb) * 2 + pair
                at_least(pe, p_sb, n - 1)
                if kb == 0 and pair == 0:
                    pe.wait_ge(nmax_in[g], 128)
                first = 3 + 2 * (n % 2)
                k0 = b * S + kb * P
                for s in range(2):
                    h = kv * GRP + 2 * pair + s
                    r = 64 * s
                    mm_(ps[:, first + s, kb * P:S], ka[r:r + 3 * HD + 2, kv, k0:k0 + P], qa[r:r + 3 * HD + 2, h // 2, k0:(b + 1) * S],
                        start=True, stop=False, skip_group_check=True)
                for s in range(2):
                    last = mm_(ps[:, first + s, kb * P:(kb + 1) * P], identb[:], mask_kq[:], start=False, stop=True,
                               skip_group_check=True)
                last.then_inc(st_ps, 1)

            def weigh_values(g, kb):
                b, kv = divmod(g, KV)
                pe.wait_ge(p_sb, (g * TPS + kb) * 2 + 2)
                if kb == 0:
                    at_least(pe, o_sb, g)
                for j in range(GRP):
                    last = mm_(ps[32 * j:32 * j + 32, 7, kb * P:S], vaug[:, b * TPS + kb, kv, :], pT[:, kb % 2, j, kb * P:S],
                               start=kb == 0, stop=kb == TPS - 1, skip_group_check=True)
                last.then_inc(pv_used, 1)

            for step in range(-2, G + 1):
                todo = list(range(16)) if 0 <= step + 2 < G else []
                if 0 <= step < G:
                    for kb in range(TPS):
                        for pair in range(2):
                            transposed_scores(step, kb, pair)
                            for i in todo[:2]:
                                scores(step + 2, i)
                            todo = todo[2:]
                            if pair == 0 and kb > 0:
                                weigh_values(step, kb - 1)
                    weigh_values(step, TPS - 1)
                else:
                    for i in todo:
                        scores(step + 2, i)
                if 0 <= step + 2 < G:
                    turn_max(step + 2)
                if 1 <= step:
                    turn_out(step - 1)
            pe.wait_ge(o_norm, G)
            for i in range(2 * CC):
                c, b = i // 2, i % 2
                if i == 3:
                    pe.wait_ge(p_sb, 2 * TPS * G)
                for t in range(TPS):
                    last = nc.tensor.transpose(ps[:, i, t * P:(t + 1) * P], xn[:, b * TPS + t, c * P:(c + 1) * P], ident[:])
                last.then_inc(ot_ps, 1)
            pe.wait_ge(ot_sb, 2 * CC)
            pe.wait_ge(o_sb, G)
            for t in range(NT):
                for c in range(CC):
                    last = mm_(ps[:, 4 + t // 2, (t % 2) * D:(t % 2 + 1) * D], xT[:, c, t * P:(t + 1) * P], wo0[:, c, :],
                               start=c == 0, stop=c == CC - 1)
                if t % 2:
                    last.then_inc(wo_ps, 1)

            transpose_x(1)
            pe.wait_ge(xT_act, 4)
            pe.wait_ge(xT_dve, 4)
            logits(m1)
            pe.wait_ge(w_in1, 48)
            for i in range(2 * CC):
                mm, b = i // 2, i % 2
                for c in range(CC):
                    last = mm_(ps[:, (5 + i) % 8, :], wq1[:, c, mm * P:(mm + 1) * P], xT[:, c, b * S:(b + 1) * S],
                               start=c == 0, stop=c == CC - 1)
                last.then_inc(q1_ps, 1)
            for t in range(NT):
                at_least(pe, k1_f, t - 2)
                for c in range(CC):
                    last = mm_(ps[:, 1 + t % 3, :], xT[:, c, t * P:(t + 1) * P], wkv1[:, c, :], start=c == 0, stop=c == CC - 1)
                last.then_inc(k1_ps, 1)
                if t == 2:
                    ranks(m1)
            pe.wait_ge(q1_f, 2 * CC)
            pe.wait_ge(k1_f, NT)
            for b in range(NB):
                for c in range(CC):
                    for t in range(TPS):
                        tt = b * TPS + t
                        last = mm_(ps[:, 5 + b, 2 * P * c:2 * P * c + P + 1], kf[:, tt, c * P:(c + 1) * P], vf[:, tt, c, :],
                                   start=t == 0, stop=t == TPS - 1)
                last.then_inc(kv_ps, 1)
            for i in range(2 * CC):
                b, c = divmod(i, CC)
                pe.wait_ge(kv_sb, 2 * i + 2)
                at_least(pe, nd_read, i - 1)
                for n in range(2):
                    last = mm_(ps[:, 2 * (i % 2) + n, :], kvd[:, b, c, n, :], qf[:, c, b * S:(b + 1) * S], start=True, stop=True)
                last.then_inc(nd_ps, 1)
            pe.wait_ge(nd_read, 2 * CC)
            pe.wait_ge(m1.tab_ready, 1)
            for t in range(NT):
                for c in range(CC):
                    last = mm_(ps[:, 4 + t // 2, (t % 2) * D:(t % 2 + 1) * D], xT[:, c, t * P:(t + 1) * P], wo1[:, c, :],
                               start=c == 0, stop=c == CC - 1)
                if t % 2:
                    last.then_inc(wo1_ps, 1)
            pe.wait_ge(wo1_add, NT // 2)
            turn_ids(m1)
            pe.wait_ge(m1.ids_ready, 1)
            first_rows(m1)
            run_tiles(pe, m1, tile_parts)


_ORDER = ["x", "wq0", "wk0", "wv0", "wo0", "gate0", "wug0", "wd0", "wq1", "wkv1", "wo1", "gate1", "wug1", "wd1"]


def kernel(**inputs):
    import numpy as np
    import concourse.bacc as bacc
    from concourse.bass_utils import run_bass_kernel_spmd

    g = {k: np.asarray(v) for k, v in inputs.items()}

    def gate_up(up, gate):
        both = np.stack([up, gate], 1).transpose(0, 3, 1, 2)
        e, c, two, h = both.shape
        return both.reshape(e, c // P, P, two, h).transpose(0, 2, 1, 3, 4)

    def down(w, hp):
        e, c, h = w.shape
        return w.transpose(0, 2, 1).reshape(e, h // hp, hp, c).transpose(0, 2, 1, 3)

    w1 = np.concatenate([g["L1_ffn_w1"], g["L1_ffn_ws1"][None]])
    w2 = np.concatenate([g["L1_ffn_w2"], g["L1_ffn_ws2"][None]])
    w3 = np.concatenate([g["L1_ffn_w3"], g["L1_ffn_ws3"][None]])
    x = g["L0_attn_x"]
    arrays = {
        "x": x.reshape(-1, D),
        "wq0": g["L0_attn_Wq"], "wk0": g["L0_attn_Wk"], "wv0": g["L0_attn_Wv"], "wo0": g["L0_attn_Wo"],
        "gate0": g["L0_ffn_gate_inp"].T,
        "wug0": gate_up(g["L0_ffn_W_up"], g["L0_ffn_W_gate"]), "wd0": down(g["L0_ffn_W_down"], 112),
        "wq1": g["L1_attn_Wq"].T,
        "wkv1": np.concatenate([g["L1_attn_Wk"].T, g["L1_attn_Wv"].T], 1),
        "wo1": g["L1_attn_Wo"].T,
        "gate1": g["L1_ffn_gate_w"].T,
        "wug1": gate_up(w3, w1), "wd1": down(w2, P),
    }
    arrays = {k: np.ascontiguousarray(v) for k, v in arrays.items()}
    nc = bacc.Bacc("TRN2", target_bir_lowering=False, num_devices=1)
    args = {k: nc.dram_tensor("in_" + k, arrays[k].shape, F32, kind="ExternalInput").ap() for k in _ORDER}
    out = nc.dram_tensor("out", arrays["x"].shape, F32, kind="ExternalOutput").ap()
    build(nc, args, out)
    r = run_bass_kernel_spmd(nc, [{"in_" + k: arrays[k] for k in _ORDER}], core_ids=[0])
    return r.results[0]["out"].reshape(x.shape)
```

```python
from contextlib import ExitStack

import concourse.bass as bass
from concourse import mybir

F32 = mybir.dt.float32
F32R = mybir.dt.float32r
BF16 = mybir.dt.bfloat16
I32 = mybir.dt.int32
U32 = mybir.dt.uint32
ALU = mybir.AluOpType
ACT = mybir.ActivationFunctionType
AX = mybir.AxisListType

P = 128
D = 256
CC = D // P
BANK = 512
NEG = -3.0e38
EPS_LN = 1e-5
XBUF = 4
YBUF = 4


class Moe:

    SHIFT = 9

    def __init__(self, tag, experts, choices, hidden, tokens, ring):
        self.tag = tag
        self.E = experts
        self.K = choices
        self.H = hidden
        self.HP = 112 if hidden % P else P
        self.HB = hidden // self.HP
        self.NT = tokens // P
        self.tiles = (tokens * choices + experts * (P - 1)) // P
        self.ring = ring
        self.reciprocal = (1 << self.SHIFT) // ring + 1
        assert all(e * self.reciprocal >> self.SHIFT == e // ring for e in range(experts))


def at_least(eng, sem, value):
    if not isinstance(value, int) or value > 0:
        eng.wait_ge(sem, value)


def run_tiles(eng, m, parts):
    n = m.tiles

    def written_out(t):
        parts(m, t, dict(half=t % 2, xbuf=(t + 1) % XBUF, ybuf=(t - 2) % YBUF, ug=t < n, hid=1 <= t <= n, row=t + 1 < n,
                         down=2 <= t <= n + 1, gathered=16 * ((t + 1) // XBUF + 1), stored=16 * ((t - 2) // YBUF)))

    peeled = 8
    end = peeled + (n - peeled - 1) // 4 * 4
    for t in range(peeled):
        written_out(t)
    with eng.Fori(peeled, end, 4) as i:
        for u in range(4):
            parts(m, i + u, dict(half=u % 2, xbuf=(u + 1) % XBUF, ybuf=(u - 2) % YBUF, ug=True, hid=True, row=True, down=True,
                                 gathered=i * 4 + 16 * ((u + 1) // XBUF + 1), stored=i * 4 + 16 * ((u - 2) // YBUF)))
    for t in range(end, n + 2):
        written_out(t)


def mixed_steps(m, groups, tps):
    rest = []
    for step in range(-2, groups + 1):
        for i in range(16):
            slot = []
            if step + 2 < groups:
                slot.append(("score", step + 2, i))
            if 0 <= step < groups:
                slot.append(("prob", step, i))
                if i % 4 == 2 and i > 4:
                    slot.append(("value", step, i // 4 - 1))
            if step >= 1:
                if i == 1:
                    slot.append(("value", step - 1, tps - 1))
                if i == 6:
                    slot.append(("out", step - 1))
            if i == 4 and 0 <= step + 1 < groups:
                slot.append(("send", step + 1))
            if i == 9 and 0 <= step + 1 < groups:
                slot.append(("fetch", step + 1))
            if i == 15 and step + 2 < groups:
                slot.append(("neg", step + 2))
            rest.append(slot)
    items = [("rows", 0)]
    along = (groups + 1) * 16
    pieces, taken = 4 * (m.tiles + 1), 0
    for t in range(m.tiles + 1):
        for n, piece in enumerate((([("gate", t)] if t < m.tiles else []) + ([("rows", t + 1)] if t + 1 < m.tiles else []),
                                   [("up", t), ("hidden", t)] if t < m.tiles else [],
                                   [("down", t - 1)] if t else [],
                                   [("turn", t)] if t < m.tiles else [])):
            items += piece
            while taken * pieces < along * (4 * t + n + 1):
                items += rest[taken]
                taken += 1
    left = rest[taken:]
    added = 0
    for n, slot in enumerate(left):
        items += slot
        due = max(0, n - 12) * m.NT // (len(left) - 13)
        items += [("add", t) for t in range(added, due)]
        added = max(added, due)
    return items


def group_order(i):
    s, rest = divmod(i, 8)
    pair, qt = divmod(rest, 4)
    return 2 * pair + s, qt


def build(nc, a, out):
    NTOK = a["x"].shape[0]
    NT = NTOK // P
    NB = 2
    S = NTOK // NB
    TPS = S // P
    HD = 16
    KV = 4
    GRP = 4
    G = NB * KV
    SCALE = HD ** -0.5

    m0 = Moe("m0", 16, 4, 448, NTOK, 3)
    m1 = Moe("m1", 8, 2, 128, NTOK, 4)
    m0.wug_dram, m0.wd_dram = a["wug0"], a["wd0"]
    m1.wug_dram, m1.wd_dram = a["wug1"], a["wd1"]
    steps0 = mixed_steps(m0, G, TPS)
    units = [x for x in steps0 if x[0] in ("score", "neg", "out")]
    unit_of = {x: n for n, x in enumerate(units)}

    with ExitStack() as ctx:
        def sb(name, shape, dt=F32):
            return ctx.enter_context(nc.sbuf_tensor(name, shape, dt))

        def sem(name):
            return ctx.enter_context(nc.semaphore(name))

        ps = ctx.enter_context(nc.psum_tensor("ps", [P, 8, BANK], F32))

        ident = sb("ident", [P, P])
        identb = sb("identb", [P, P], BF16)
        onesb = sb("onesb", [P, P], BF16)
        before = sb("before", [P, P], BF16)
        mask_qk = sb("mask_qk", [P, P], BF16)
        mask_kq = sb("mask_kq", [P, P], BF16)
        same_head = sb("same_head", [P, P])
        tokid = sb("tokid", [P, NT])
        iota_p = sb("iota_p", [P, P])
        place = sb("place", [P, 4, NT])

        acc = sb("acc", [P, NT, D])
        xn = sb("xn", [P, NT, D])
        xT = sb("xT", [P, CC, NTOK])
        bn = sb("bn", [P, NT, 6])
        mv = sb("mv", [P, NT, 2])
        rstd = sb("rstd", [P, 4, NT])

        wq0, wk0, wv0, wo0 = (sb(n, [P, CC, w]) for n, w in (("wq0", D), ("wk0", KV * HD), ("wv0", KV * HD), ("wo0", D)))
        wq1, wkv1, wo1 = (sb(n, [P, CC, w]) for n, w in (("wq1", D), ("wkv1", 2 * D), ("wo1", D)))

        qa = sb("qa", [P, 8, NTOK], F32R)
        ka = sb("ka", [P, KV, NTOK], F32R)
        vaug = sb("vaug", [P, NT, KV, 2 * HD])
        rowmax = sb("rowmax", [P, G, 16])
        pT = sb("pT", [P, 2, GRP, S])
        oT = sb("oT", [P, 2, S])
        rsum = sb("rsum", [P, 2, TPS, GRP])
        vf = sb("vf", [P, NT, CC, P + 1])
        hl = sb("hl", [P, 2, 2, S], F32R)
        sel = sb("sel", [P, 16, P], F32R)
        nmax = sel[0:16].rearrange("p (w g) n -> p w g n", w=2)
        code = oT[:].rearrange("p a n -> p (a n)")[:, 0:4 * P].rearrange("p (w n) -> p w n", w=4)
        shift = sb("shift", [P, 2, 4])
        one_at = sb("one_at", [P, 3, 4])

        xg = sb("xg", [P, XBUF, D])
        xgT = sb("xgT", [P, 2, CC, P])
        work = sb("work", [P, 3, 2, m0.H])
        th, ga, hh = work[:, 0], work[:, 1], work[:, 2]
        hT = sb("hT", [P, 2, m0.HB, P])
        ysb = vf[:].rearrange("p t c n -> p (t c n)")[:, 0:YBUF * D].rearrange("p (b c) -> p b c", b=YBUF)

        kf = pT[:, 0].rearrange("p j n -> p (j n)").rearrange("p (t c) -> p t c", t=NT)
        qf = pT[:, 1].rearrange("p j n -> p (j n)").rearrange("p (c n) -> p c n", c=CC)
        kvd = oT[:].rearrange("p a n -> p (a n)").rearrange("p (b c w n) -> p b c w n", b=NB, c=CC, w=2)
        emin = hT[:].rearrange("p a b n -> p (a b n)").rearrange("p (a n) -> p a n", a=2)

        m0.wug = sb("m0wug", [P, m0.ring, CC, 2, m0.H])
        m0.wd = sb("m0wd", [m0.HP, m0.ring, m0.HB, D])
        w_flat = m0.wug[:].rearrange("p r c w n -> p (r c w n)")
        n_ug, n_d = m1.ring * CC * 2 * m1.H, m1.ring * m1.HB * D
        m1.wug = w_flat[:, 0:n_ug].rearrange("p (r c w n) -> p r c w n", r=m1.ring, c=CC, w=2)
        m1.wd = w_flat[:, n_ug:n_ug + n_d].rearrange("p (r b n) -> p r b n", r=m1.ring, b=m1.HB)
        at = n_ug + n_d
        ws_ug = w_flat[:, at:at + CC * 2 * m1.H].rearrange("p (c w n) -> p c w n", c=CC, w=2)
        at += CC * 2 * m1.H
        ws_d = w_flat[:, at:at + D]
        at += D
        shT = w_flat[:, at:at + NTOK]

        flat = work[:].rearrange("p a b n -> p (a b n)")
        flat_end = 6 * m0.H
        sh_th, sh_ga = (flat[:, flat_end - n * BANK:flat_end - (n - 1) * BANK] for n in (2, 1))
        for m in (m0, m1):
            t = m.tag
            T = m.tiles
            m.hot_row = flat[:, 0:NT * P].bitcast(BF16).rearrange("p (w t r) -> p w t r", w=2, t=NT)
            at = NT * P
            m.hot_tile = flat[:, at:at + NT * T].rearrange("p (t a) -> p t a", t=NT)
            at += NT * T
            assert at + 2 * NT * T <= flat_end - (2 * BANK if m is m1 else 0)
            m.hot_id = flat[:, at:at + 2 * NT * T].bitcast(BF16).rearrange("p (w h t a) -> p w h t a", w=2, h=2, t=NT)
            m.gate = sb(t + "gate", [P, CC, m.E])
            m.logits = sb(t + "logits", [P, NT, m.E])
            m.best = sb(t + "best", [P, NT, 8])
            m.index = sb(t + "index", [P, NT, 8], U32)
            m.choice = sb(t + "choice", [P, NT, m.K])
            m.weight = sb(t + "weight", [P, NT, 8])
            m.wsum = sb(t + "wsum", [P, 2, NT])
            m.onehot = sb(t + "onehot", [P, m.K, NT, m.E])
            m.member = sb(t + "member", [P, NT, m.E], BF16)
            m.earlier = sb(t + "earlier", [P, NT + 1, m.E], BF16)
            m.cnt = sb(t + "cnt", [P, 4, m.E])
            m.cnti = sb(t + "cnti", [P, 2, m.E], I32)
            m.slot = sb(t + "slot", [P, NT, m.E])
            m.slotk = sb(t + "slotk", [P, m.K, NT])
            m.sloti = sb(t + "sloti", [P, m.K, NT], U32)
            m.cmp = sb(t + "cmp", [1, m.tiles, m.E])
            m.tile_e = sb(t + "tile_e", [1, m.tiles])
            m.tab = sb(t + "tab", [1, 3, m.tiles], I32)
            m.cum = sb(t + "cum", [1, m.E], I32)
            m.split = sb(t + "split", [P, 2, m.K * NT], I32)
            m.splitf = sb(t + "splitf", [P, 2, m.K * NT])
            m.taken = sb(t + "taken", [P, m.tiles], I32)
            m.ids = sb(t + "ids", [P, m.tiles], U32)
            m.dest = sb(t + "dest", [P, m.tiles], U32)
            m.spare = sb(t + "spare", [P, 3, m.tiles])
            m.x_dram = nc.dram_tensor(t + "x", [NTOK, D], F32, kind="Internal").ap()
            m.y_dram = nc.dram_tensor(t + "y", [m.K * NTOK + m.tiles * P, D], F32, kind="Internal").ap()
            m.zbuf = 5 if m is m0 else NT
            m.z = (w_flat if m is m0 else pT[:].rearrange("p a j n -> p (a j n)"))[:, 0:m.zbuf * m.K * D].rearrange(
                "p (b k c) -> p b k c", b=m.zbuf, k=m.K)

            m.w_loaded = sem(t + "w_loaded")
            m.xn_stored = sem(t + "xn_stored")
            m.hot_ready = sem(t + "hot_ready")
            m.hot_used = sem(t + "hot_used")
            m.ids_ready = sem(t + "ids_ready")
            m.lg_ps = sem(t + "lg_ps")
            m.ex_in = sem(t + "ex_in")
            m.ex_out = sem(t + "ex_out")
            m.member_ready = sem(t + "member_ready")
            m.rank_ps = sem(t + "rank_ps")
            m.slots_ready = sem(t + "slots_ready")
            m.tab_ready = sem(t + "tab_ready")
            m.gathered = [sem(t + f"gathered{i}") for i in range(XBUF)]
            m.x_ps = sem(t + "x_ps")
            m.x_sb = sem(t + "x_sb")
            m.g_ps = sem(t + "g_ps")
            m.u_ps = sem(t + "u_ps")
            m.th_sb = sem(t + "th_sb")
            m.ga_sb = sem(t + "ga_sb")
            m.h_sb = sem(t + "h_sb")
            m.h_ps = sem(t + "h_ps")
            m.hT_sb = sem(t + "hT_sb")
            m.y_ps = sem(t + "y_ps")
            m.y_sb = sem(t + "y_sb")
            m.y_out = [sem(t + f"y_out{i}") for i in range(YBUF)]
            m.back = [sem(t + f"back{i}") for i in range(NT)]
            m.added = sem(t + "added")

        x_in = [sem(f"x_in{i}") for i in range(NB)]
        w_in0, w_in1 = sem("w_in0"), sem("w_in1")
        g_in = sem("g_in")
        ws_in = sem("ws_in")
        const = sem("const")
        pool_c = sem("pool_c")
        dve_c = sem("dve_c")
        var_ready = sem("var_ready")
        std_ready = sem("std_ready")
        xn_ready = sem("xn_ready")
        xT_ps = sem("xT_ps")
        xT_act, xT_dve = sem("xT_act"), sem("xT_dve")
        q_ps, k_ps = sem("q_ps"), sem("k_ps")
        hi_ready, lo_ready = sem("hi_ready"), sem("lo_ready")
        v_ps, v_sb = sem("v_ps"), sem("v_sb")
        sel_ready = sem("sel_ready")
        sel_ps, qk_in = sem("sel_ps"), sem("qk_in")
        s_ps, s_read = sem("s_ps"), sem("s_read")
        nmax_ready = sem("nmax_ready")
        nmax_out = [sem(f"nmax_out{i}") for i in range(G)]
        nmax_in = [sem(f"nmax_in{i}") for i in range(G)]
        nmax_dram = nc.dram_tensor("nmax", [G, 2, 16, P], F32, kind="Internal").ap()
        st_ps, p_sb = sem("st_ps"), sem("p_sb")
        o_sb = sem("o_sb")
        pv_used = sem("pv_used")
        o_norm = sem("o_norm")
        ot_ps, ot_sb = sem("ot_ps"), sem("ot_sb")
        wo_ps, wo_add = sem("wo_ps"), sem("wo_add")
        q1_ps, q1_min, q1_exp, q1_f = sem("q1_ps"), sem("q1_min"), sem("q1_exp"), sem("q1_f")
        k1_ps, v1_sb, k1_min, k1_exp, k1_f = sem("k1_ps"), sem("v1_sb"), sem("k1_min"), sem("k1_exp"), sem("k1_f")
        kv_ps, kv_sb = sem("kv_ps"), sem("kv_sb")
        nd_ps, nd_read = sem("nd_ps"), sem("nd_read")
        wo1_ps, wo1_add = sem("wo1_ps"), sem("wo1_add")
        sh_g, sh_u = sem("sh_g"), sem("sh_u")
        sh_tanh, sh_ga_ready, sh_sb = sem("sh_tanh"), sem("sh_ga_ready"), sem("sh_sb")
        out_done = sem("out_done")

        block = ctx.enter_context(nc.Block())
        N_CONST = 18

        @block.sync
        def _(sp):
            x_t = a["x"].rearrange("(t p) c -> p t c", p=P)
            for b in range(NB):
                sp.dma_start(acc[:, b * TPS:(b + 1) * TPS, :], x_t[:, b * TPS:(b + 1) * TPS, :]).then_inc(x_in[b], 16)
            chunked = "(a p) n -> p a n"
            sp.dma_start(m0.gate[:], a["gate0"].rearrange(chunked, p=P)).then_inc(g_in, 16)
            sp.dma_start(m1.gate[:], a["gate1"].rearrange(chunked, p=P)).then_inc(g_in, 16)
            for dst, name in ((wq0, "wq0"), (wk0, "wk0"), (wv0, "wv0"), (wo0, "wo0")):
                sp.dma_start(dst[:], a[name].rearrange(chunked, p=P)).then_inc(w_in0, 16)
            for dst, name in ((wq1, "wq1"), (wkv1, "wkv1"), (wo1, "wo1")):
                sp.dma_start(dst[:], a[name].rearrange(chunked, p=P)).then_inc(w_in1, 16)

            def load_expert(m, e, slot):
                sp.dma_start(m.wug[:, slot], m.wug_dram[e]).then_inc(m.w_loaded, 16)
                sp.dma_start(m.wd[:, slot], m.wd_dram[e]).then_inc(m.w_loaded, 16)

            def first_experts(m):
                for e in range(m.ring):
                    if e:
                        sp.wait_ge(m.w_loaded, 32 * e)
                    load_expert(m, e, e)

            def store_xn(m, n):
                sp.wait_ge(xn_ready, NT * (n + 1))
                sp.dma_start(m.x_dram.rearrange("(t p) c -> p t c", p=P), xn[:]).then_inc(m.xn_stored, 16)

            def results_back(m):
                for b in range(YBUF):
                    sp.wait_ge(m.y_out[b], 16 * len(range(b, m.tiles, YBUF)))
                rows_of = m.y_dram[0:m.K * NTOK, :].rearrange("(k t p) c -> t p k c", k=m.K, p=P)
                for t in range(NT):
                    at_least(sp, m.added, m.K * (t - m.zbuf + 1))
                    sp.dma_start(m.z[:, t % m.zbuf], rows_of[t]).then_inc(m.back[t], 16)

            def other_experts(m):
                sp.wait_ge(m.tab_ready, 1)
                for e in range(m.ring, m.E):
                    sp.wait_ge(m.w_loaded, 32 * e)
                    used = nc.sync.value_load(m.cum[0:1, e - m.ring:e - m.ring + 1], min_val=1, max_val=m.tiles + 1)
                    sp.wait_ge(m.y_ps, used)
                    load_expert(m, e, e % m.ring)

            first_experts(m0)
            store_xn(m0, 0)
            other_experts(m0)
            results_back(m0)
            sp.wait_ge(m0.added, m0.K * NT)
            sp.dma_start(ws_ug, a["ws_ug"]).then_inc(ws_in, 16)
            sp.dma_start(ws_d, a["ws_d"]).then_inc(ws_in, 16)
            first_experts(m1)
            store_xn(m1, 1)
            other_experts(m1)
            results_back(m1)
            for t in range(NT):
                sp.wait_ge(m1.added, m1.K * (t + 1))
                sp.dma_start(out[t * P:(t + 1) * P, :], acc[:, t, :]).then_inc(out_done, 16)
            sp.wait_ge(out_done, 16 * NT)

        @block.gpsimd
        def _(pool):
            pool.memset(ident[:], 0.0).then_inc(pool_c, 1)
            pool.memset(onesb[:], 1.0).then_inc(const, 1)
            pool.memset(before[:], 0.0).then_inc(pool_c, 1)
            pool.memset(mask_qk[:], 0.0).then_inc(pool_c, 1)
            pool.memset(mask_kq[:], 0.0).then_inc(pool_c, 1)
            pool.memset(same_head[:], 1.0).then_inc(pool_c, 1)
            pool.iota(tokid[:], [[P, NT]], base=0, channel_multiplier=1,
                      allow_small_or_imprecise_dtypes=True).then_inc(const, 1)
            pool.iota(iota_p[:], [[1, P]], base=0, channel_multiplier=0,
                      allow_small_or_imprecise_dtypes=True).then_inc(const, 1)
            pool.iota(place[:], [[NTOK, 4], [P, NT]], base=NTOK, channel_multiplier=0,
                      allow_small_or_imprecise_dtypes=True).then_inc(const, 1)
            for m in (m0, m1):
                pool.iota(m.spare[:, 0, :], [[P, m.tiles]], base=(m.K + 1) * NTOK, channel_multiplier=1,
                          allow_small_or_imprecise_dtypes=True).then_inc(const, 1)
            pool.iota(shift[:, 0, :], [[-2 * HD, 4]], base=0, channel_multiplier=1,
                      allow_small_or_imprecise_dtypes=True).then_inc(const, 1)
            pool.iota(shift[:, 1, :], [[-HD, 4]], base=0, channel_multiplier=1,
                      allow_small_or_imprecise_dtypes=True).then_inc(const, 1)
            pool.iota(one_at[:, 0, :], [[-64, 2], [-1, 2]], base=-3 * HD, channel_multiplier=1,
                      allow_small_or_imprecise_dtypes=True).then_inc(const, 1)
            pool.memset(code, -1000.0).then_inc(pool_c, 1)
            pool.wait_ge(pool_c, 6)
            for n, (rows_of, step) in enumerate(((slice(0, 2), HD), (slice(2, 3), HD), (slice(0, 3, 2), 0), (slice(1, 2), 0))):
                columns = code[:, n, :].rearrange("p (s r d) -> p s r d", s=2, r=4)[:, :, rows_of, :]
                pool.iota(columns, [[step, 2], [0, columns.shape[2]], [1, HD]], base=0, channel_multiplier=0,
                          allow_small_or_imprecise_dtypes=True).then_inc(const, 1)
            pool.affine_select(out=ident[:], in_=ident[:], compare_op=ALU.not_equal, fill=1.0, base=0,
                               pattern=[[-1, P]], channel_multiplier=1).then_inc(pool_c, 1)
            pool.affine_select(out=before[:], in_=before[:], compare_op=ALU.is_ge, fill=1.0, base=0,
                               pattern=[[-1, P]], channel_multiplier=1).then_inc(const, 1)
            pool.affine_select(out=mask_qk[:], in_=mask_qk[:], compare_op=ALU.is_ge, fill=NEG, base=0,
                               pattern=[[-1, P]], channel_multiplier=1).then_inc(const, 1)
            pool.affine_select(out=mask_kq[:], in_=mask_kq[:], compare_op=ALU.is_ge, fill=NEG, base=0,
                               pattern=[[1, P]], channel_multiplier=-1).then_inc(const, 1)
            heads = same_head[:].rearrange("p (h d) -> p h d", d=HD)
            pool.affine_select(out=heads, in_=heads, compare_op=ALU.is_ge, fill=0.0, base=0,
                               pattern=[[-HD, P // HD], [0, HD]], channel_multiplier=1).then_inc(pool_c, 1)
            pool.wait_ge(pool_c, 8)
            pool.tensor_copy(identb[:], ident[:]).then_inc(const, 1)
            pool.affine_select(out=heads, in_=heads, compare_op=ALU.is_ge, fill=0.0, base=HD - 1,
                               pattern=[[HD, P // HD], [0, HD]], channel_multiplier=-1).then_inc(const, 1)

            def move_rows(m, lag):
                pool.wait_ge(m.ids_ready, 1)
                pool.wait_ge(m.xn_stored, 16)
                for t in range(-XBUF, m.tiles + lag):
                    n = t + XBUF
                    if n < m.tiles:
                        at_least(pool, m.x_ps, n - XBUF + 1)
                        pool.indirect_dma_start(
                            out=xg[:, n % XBUF, :], out_offset=None, in_=m.x_dram,
                            in_offset=bass.IndirectOffsetOnAxis(ap=m.ids[:, n:n + 1], axis=0)).then_inc(m.gathered[n % XBUF], 16)
                    n = t - lag
                    if n >= 0:
                        pool.wait_ge(m.y_sb, n + 1)
                        pool.indirect_dma_start(
                            out=m.y_dram, out_offset=bass.IndirectOffsetOnAxis(ap=m.dest[:, n:n + 1], axis=0),
                            in_=ysb[:, n % YBUF, :], in_offset=None).then_inc(m.y_out[n % YBUF], 16)

            move_rows(m0, 2)
            move_rows(m1, 3)

        @block.scalar
        def _(act):
            def sqrt_var(n):
                act.wait_ge(var_ready, n + 1)
                nc.scalar.activation(rstd[:, 1, :], rstd[:, 0, :], ACT.Sqrt).then_inc(std_ready, 1)

            def evacuate_xT(n):
                for half in range(2):
                    act.wait_ge(xT_ps, NT * n + TPS * (half + 1))
                    nc.scalar.copy(xT[:, 0, half * S:(half + 1) * S], ps[:, half, :]).then_inc(xT_act, 1)

            def route_exp(m):
                act.wait_ge(m.ex_in, 1)
                nc.scalar.activation(m.weight[:], m.weight[:], ACT.Exp).then_inc(m.ex_out, 1)

            def rows(m, t, half, bank=4):
                act.wait_ge(m.x_ps, t + 1)
                at_least(act, m.u_ps, t - 1)
                nc.scalar.copy(xgT[:, half], ps[:, bank, 0:CC * P].rearrange("p (c n) -> p c n", n=P)).then_inc(m.x_sb, 1)

            def tile_parts(m, t, p):
                if p["row"]:
                    rows(m, t + 1, 1 - p["half"])
                if p["ug"]:
                    act.wait_ge(m.g_ps, t + 1)
                    at_least(act, m.ga_sb, t - 1)
                    nc.scalar.activation(th[:, p["half"], 0:m.H], ps[:, 2 + p["half"], 0:m.H], ACT.Tanh,
                                         scale=0.5).then_inc(m.th_sb, 1)
                if p["hid"]:
                    act.wait_ge(m.h_ps, t)
                    at_least(act, m.y_ps, t - 1)
                    nc.scalar.copy(hT[0:m.HP, 1 - p["half"], 0:m.HB, :],
                                   ps[0:m.HP, 5, 0:m.HB * P].rearrange("p (b n) -> p b n", n=P)).then_inc(m.hT_sb, 1)

            def place_block(n):
                for j in range(4):
                    u = 4 * n + j
                    act.wait_ge(sel_ps, u + 1)
                    if n < NB:
                        nc.scalar.activation(ka[:, j, n * S:(n + 1) * S], ps[:, 1 + u % 2, :], ACT.Identity,
                                             bias=one_at[:, 2, 0:1]).then_inc(qk_in, 1)
                    else:
                        half, b = divmod(n - NB, NB)
                        nc.scalar.copy(qa[:, 4 * half + j, b * S:(b + 1) * S], ps[:, 1 + u % 2, :]).then_inc(qk_in, 1)

            sqrt_var(0)
            evacuate_xT(0)
            route_exp(m0)
            act.wait_ge(sel_ready, 1)
            for n in range(NB + 2 * CC):
                at_least(act, sel_ps, 4 * (n - 1))
                if n < NB:
                    act.wait_ge(k_ps, n + 1)
                    nc.scalar.copy(hl[0:KV * HD, n % 2, 0, :], ps[0:KV * HD, 1 + n, :]).then_inc(hi_ready, 1)
                else:
                    act.wait_ge(q_ps, n - NB + 1)
                    nc.scalar.activation(hl[:, n % 2, 0, :], ps[:, (5 + n - NB) % 8, :], ACT.Copy, scale=SCALE).then_inc(hi_ready, 1)
                if n:
                    place_block(n - 1)
            place_block(NB + 2 * CC - 1)
            for kind, *which in steps0:
                m = m0
                if kind == "rows":
                    t, = which
                    rows(m, t, t % 2, 6)
                elif kind == "gate":
                    t, = which
                    act.wait_ge(m.g_ps, t + 1)
                    at_least(act, m.ga_sb, t - 1)
                    nc.scalar.activation(th[:, t % 2, :], ps[:, 4, 0:m.H], ACT.Tanh, scale=0.5).then_inc(m.th_sb, 1)
                elif kind == "turn":
                    t, = which
                    act.wait_ge(m.h_ps, t + 1)
                    at_least(act, m.y_ps, t)
                    nc.scalar.copy(hT[0:m.HP, t % 2], ps[0:m.HP, 7, :].rearrange("p (b n) -> p b n", n=P)).then_inc(m.hT_sb, 1)
                elif kind == "send":
                    g, = which
                    act.wait_ge(nmax_ready, 2 * (g + 1))
                    act.dma_start(nmax_dram[g].rearrange("w i n -> i w n"), nmax[:, :, g, :].bitcast(F32)).then_inc(nmax_out[g], 16)
                elif kind == "fetch":
                    g, = which
                    b, kv = divmod(g, KV)
                    act.wait_ge(nmax_out[g], 16)
                    for s in range(2):
                        row = 64 * s + 3 * HD
                        act.dma_start(qa[row:row + 2, 2 * kv:2 * kv + 2, b * S:(b + 1) * S].bitcast(F32),
                                      nmax_dram[g, :, 8 * s:8 * (s + 1), :].rearrange("w (pair t) n -> w pair (t n)", pair=2)
                                      ).then_inc(nmax_in[g], 16)
                elif kind == "prob":
                    g, i = which
                    kb, j = divmod(i, GRP)
                    n = g * 16 + i
                    act.wait_ge(st_ps, n + 1)
                    at_least(act, pv_used, g * TPS + kb - 1)
                    nc.scalar.activation(pT[:, kb % 2, j, kb * P:S], ps[:, 1 + n % 2, kb * P:S], ACT.Exp).then_inc(p_sb, 1)
                elif kind == "value" and which[1] == TPS - 1:
                    g = which[0]
                    act.wait_ge(pv_used, TPS * (g + 1))
                    if g >= 2:
                        act.wait_ge(s_ps, unit_of["out", g - 2] + 1)
                    nc.scalar.copy(oT[:, g % 2, :], ps[:, 3, :]).then_inc(o_sb, 1)
            sqrt_var(1)
            evacuate_xT(1)
            route_exp(m1)
            for c in range(2 * CC):
                act.wait_ge(q1_min, c + 1)
                nc.scalar.activation(emin[:, c % 2, :], emin[:, c % 2, :], ACT.Exp).then_inc(q1_exp, 1)
            for t in range(NT):
                act.wait_ge(k1_ps, t + 1)
                nc.scalar.copy(vf[:, t, :, 0:P], ps[:, 1 + t % 3, D:2 * D].rearrange("p (c n) -> p c n", n=P)).then_inc(v1_sb, 1)
                act.wait_ge(k1_min, t + 1)
                nc.scalar.activation(emin[:, t % 2, 0:D], emin[:, t % 2, 0:D], ACT.Exp).then_inc(k1_exp, 1)
            for b in range(NB):
                act.wait_ge(sh_g, b + 1)
                at_least(act, sh_ga_ready, b)
                nc.scalar.activation(sh_th, ps[:, 0, :], ACT.Tanh, scale=0.5).then_inc(sh_tanh, 1)
            rows(m1, 0, 0)
            run_tiles(act, m1, tile_parts)

        @block.vector
        def _(dve):
            chain = [0]

            def link(ins):
                chain[0] += 1
                ins.then_inc(dve_c, 1)
                dve.wait_ge(dve_c, chain[0])

            def layernorm(n):
                for t in range(NT):
                    if n == 0 and t % TPS == 0:
                        dve.wait_ge(x_in[t // TPS], 16)
                    last = nc.vector.bn_stats(bn[:, t, :], acc[:, t, :])
                link(last)
                for t in range(NT):
                    last = nc.vector.bn_aggr(mv[:, t, :], bn[:, t, :])
                link(last)
                nc.vector.tensor_scalar(rstd[:, 0, :], mv[:, :, 1], EPS_LN, None, ALU.add).then_inc(var_ready, 1)
                dve.wait_ge(std_ready, n + 1)
                link(nc.vector.reciprocal(rstd[:, 2, :], rstd[:, 1, :]))
                link(nc.vector.tensor_tensor(rstd[:, 3, :], rstd[:, 2, :], rstd[:, 2, :], ALU.mult))
                link(nc.vector.tensor_tensor(rstd[:, 3, :], rstd[:, 3, :], rstd[:, 0, :], ALU.mult))
                link(nc.vector.tensor_scalar(rstd[:, 3, :], rstd[:, 3, :], -0.5, 1.5, ALU.mult, ALU.add))
                link(nc.vector.tensor_tensor(rstd[:, 2, :], rstd[:, 2, :], rstd[:, 3, :], ALU.mult))
                if n:
                    dve.wait_ge(ot_ps, CC * 2)
                for t in range(NT):
                    nc.vector.tensor_scalar(xn[:, t, :], acc[:, t, :], mv[:, t, 0:1], rstd[:, 2, t:t + 1],
                                            ALU.subtract, ALU.mult).then_inc(xn_ready, 1)

            def evacuate_xT(n):
                for half in range(2):
                    dve.wait_ge(xT_ps, NT * n + TPS * (half + 1))
                    nc.vector.tensor_copy(xT[:, 1, half * S:(half + 1) * S], ps[:, 2 + half, :]).then_inc(xT_dve, 1)

            def choose(m):
                K, E = m.K, m.E
                dve.wait_ge(m.lg_ps, 1)
                link(nc.vector.tensor_copy(m.logits[:], ps[:, 4, 0:NT * m.E].rearrange("p (t e) -> p t e", t=NT)))
                for t in range(NT):
                    last = nc.vector.max(m.best[:, t, :], m.logits[:, t, :])
                link(last)
                for t in range(NT):
                    last = nc.vector.max_index(m.index[:, t, :], m.best[:, t, :], m.logits[:, t, :])
                link(last)
                nc.vector.tensor_tensor(m.weight[:], m.best[:], m.best[:, :, 0:1].to_broadcast([P, NT, 8]),
                                        ALU.subtract).then_inc(m.ex_in, 1)
                link(nc.vector.tensor_copy(m.choice[:], m.index[:, :, 0:K]))
                for k in range(K):
                    last = nc.vector.tensor_tensor(
                        m.onehot[:, k], m.choice[:, :, k:k + 1].to_broadcast([P, NT, E]),
                        iota_p[:, 0:E].unsqueeze(1).to_broadcast([P, NT, E]), ALU.is_equal)
                link(last)
                link(nc.vector.tensor_tensor(m.member[:], m.onehot[:, 0], m.onehot[:, 1], ALU.add))
                for k in range(2, K):
                    link(nc.vector.tensor_tensor(m.member[:], m.member[:], m.onehot[:, k], ALU.add))
                link(nc.vector.memset(m.earlier[:, 0, :], 0.0))
                for t in range(NT - 1):
                    link(nc.vector.tensor_tensor(m.earlier[:, t + 1, :], m.earlier[:, t, :], m.member[:, t, :], ALU.add))
                nc.vector.tensor_tensor(m.earlier[:, NT, :], m.earlier[:, NT - 1, :], m.member[:, NT - 1, :],
                                        ALU.add).then_inc(m.member_ready, 1)
                dve.wait_ge(m.ex_out, 1)
                n_sum = K if m is m0 else E
                link(nc.vector.tensor_reduce(m.wsum[:, 0, :], m.weight[:, :, 0:n_sum], AX.X, ALU.add))
                link(nc.vector.reciprocal(m.wsum[:, 1, :], m.wsum[:, 0, :]))
                link(nc.vector.tensor_tensor(m.weight[:, :, 0:K], m.weight[:, :, 0:K],
                                             m.wsum[:, 1, :].unsqueeze(2).to_broadcast([P, NT, K]), ALU.mult))

            def slots(m):
                K, E = m.K, m.E
                dve.wait_ge(m.rank_ps, 1)
                count = ps[:, 4, NT * E:(NT + 1) * E]
                link(nc.vector.tensor_scalar(m.cnti[:, 0, :], count, float(P - 1), None, ALU.add))
                link(nc.vector.tensor_scalar(m.cnti[:, 1, :], m.cnti[:, 0, :], 7, None, ALU.logical_shift_right))
                link(nc.vector.tensor_copy(m.cnt[:, 1, :], m.cnti[:, 1, :]))
                link(nc.vector.memset(m.cnt[:, 0, :], 1.0))
                link(nc.vector.tensor_tensor_scan(m.cnt[:, 2, :], m.cnt[:, 0, :], m.cnt[:, 1, :], 0.0, ALU.mult, ALU.add))
                link(nc.vector.tensor_tensor(m.cnt[:, 3, :], m.cnt[:, 2, :], m.cnt[:, 1, :], ALU.subtract))
                link(nc.vector.tensor_scalar(m.cnt[:, 3, :], m.cnt[:, 3, :], float(P), None, ALU.mult))
                link(nc.vector.tensor_tensor(m.slot[:], ps[:, 4, 0:NT * E].rearrange("p (t e) -> p t e", t=NT),
                                             m.cnt[:, 3:4, :].to_broadcast([P, NT, E]), ALU.add))
                for k in range(K):
                    last = nc.vector.tensor_tensor(m.onehot[:, k], m.onehot[:, k], m.slot[:], ALU.mult)
                link(last)
                link(nc.vector.tensor_reduce(m.slotk[:], m.onehot[:], AX.X, ALU.add))
                nc.vector.tensor_copy(m.sloti[:], m.slotk[:]).then_inc(m.slots_ready, 1)
                link(nc.vector.tensor_tensor(m.cmp[:], m.cnt[0:1, 2:3, :].to_broadcast([1, m.tiles, E]),
                                             iota_p[0:1, 0:m.tiles].unsqueeze(2).to_broadcast([1, m.tiles, E]), ALU.is_le))
                link(nc.vector.tensor_reduce(m.tile_e[:], m.cmp[:], AX.X, ALU.add))
                link(nc.vector.tensor_scalar(m.tile_e[:], m.tile_e[:], float(E - 1), None, ALU.min))
                link(nc.vector.tensor_copy(m.tab[:, 0, :], m.tile_e[:]))
                link(nc.vector.tensor_scalar(m.tab[:, 1, :], m.tab[:, 0, :], 32.0, 32.0, ALU.mult, ALU.add))
                link(nc.vector.tensor_scalar(m.cum[:], m.cnt[0:1, 2, :], 1.0, None, ALU.add))
                link(nc.vector.tensor_scalar(m.tab[:, 2, :], m.tile_e[:], float(m.reciprocal), None, ALU.mult))
                link(nc.vector.tensor_scalar(m.tab[:, 2, :], m.tab[:, 2, :], m.SHIFT, None, ALU.logical_shift_right))
                link(nc.vector.tensor_scalar(m.cmp[:, :, 0], m.tab[:, 2, :], -float(m.ring), None, ALU.mult))
                nc.vector.tensor_tensor(m.tab[:, 2, :], m.cmp[:, :, 0], m.tile_e[:], ALU.add).then_inc(m.tab_ready, 1)

            def place_ids(m):
                T = m.tiles
                dve.wait_ge(m.slots_ready, 1)
                slots_of = m.sloti[:].rearrange("p k t -> p (k t)").bitcast(I32)
                nc.vector.tensor_scalar(m.split[:, 0, :], slots_of, 7, None, ALU.logical_shift_right)
                link(nc.vector.tensor_scalar(m.split[:, 1, :], slots_of, P - 1, None, ALU.bitwise_and))
                link(nc.vector.tensor_copy(m.splitf[:], m.split[:]))
                for k in range(m.K):
                    w = k % 2
                    at_least(dve, m.hot_used, k - 1)
                    tile_of = m.splitf[:, 0, k * NT:(k + 1) * NT]
                    row_of = m.splitf[:, 1, k * NT:(k + 1) * NT]
                    link(nc.vector.tensor_tensor(m.hot_tile, tile_of.unsqueeze(2).to_broadcast([P, NT, T]),
                                                 iota_p[:, 0:T].unsqueeze(1).to_broadcast([P, NT, T]), ALU.is_equal))
                    nc.vector.tensor_scalar(m.hot_id[:, w, 0], m.hot_tile, tokid[:, 0:1], None, ALU.mult)
                    link(nc.vector.tensor_tensor(m.hot_id[:, w, 1], m.hot_tile,
                                                 place[:, k, :].unsqueeze(2).to_broadcast([P, NT, T]), ALU.mult))
                    nc.vector.tensor_tensor(m.hot_row[:, w], row_of.unsqueeze(2).to_broadcast([P, NT, P]),
                                            iota_p[:].unsqueeze(1).to_broadcast([P, NT, P]), ALU.is_equal).then_inc(m.hot_ready, 1)

            def integer_ids(m):
                dve.wait_ge(m.hot_used, m.K)
                taken = ps[:, 4, 0:m.tiles]
                nc.vector.tensor_copy(m.taken[:], taken)
                link(nc.vector.scalar_tensor_tensor(out=m.spare[:, 1, :], in0=taken, scalar=0.0, in1=m.spare[:, 0, :],
                                                    op0=ALU.is_equal, op1=ALU.mult))
                nc.vector.tensor_scalar(m.ids[:].bitcast(I32), m.taken[:], NTOK - 1, None, ALU.bitwise_and)
                link(nc.vector.scalar_tensor_tensor(out=m.spare[:, 2, :], in0=taken, scalar=-float(NTOK), in1=m.spare[:, 1, :],
                                                    op0=ALU.add, op1=ALU.add))
                nc.vector.tensor_copy(m.dest[:], m.spare[:, 2, :]).then_inc(m.ids_ready, 1)

            def tile_parts(m, t, p):
                half = p["half"]
                if p["ug"]:
                    dve.wait_ge(m.th_sb, t + 1)
                    nc.vector.scalar_tensor_tensor(out=ga[:, half, 0:m.H], in0=th[:, half, 0:m.H], scalar=1.0,
                                                   in1=ps[:, 2 + half, 0:m.H], op0=ALU.add, op1=ALU.mult).then_inc(m.ga_sb, 1)
                    dve.wait_ge(m.ga_sb, t + 1)
                    dve.wait_ge(m.u_ps, t + 1)
                    at_least(dve, m.h_ps, t - 1)
                    nc.vector.scalar_tensor_tensor(out=hh[:, half, 0:m.H], in0=ga[:, half, 0:m.H], scalar=0.5,
                                                   in1=ps[:, half, 0:m.H], op0=ALU.mult, op1=ALU.mult).then_inc(m.h_sb, 1)
                if p["down"]:
                    dve.wait_ge(m.y_ps, t)
                    at_least(dve, m.y_out[p["ybuf"]], p["stored"])
                    nc.vector.tensor_copy(ysb[:, p["ybuf"], :], ps[:, 6, 0:D]).then_inc(m.y_sb, 1)

            def combine(m, t):
                dve.wait_ge(m.back[t], 16)
                for k in range(m.K):
                    at_least(dve, m.added, m.K * t + k)
                    nc.vector.scalar_tensor_tensor(out=acc[:, t, :], in0=m.z[:, t % m.zbuf, k, :], scalar=m.weight[:, t, k:k + 1],
                                                   in1=acc[:, t, :], op0=ALU.mult, op1=ALU.add).then_inc(m.added, 1)

            dve.wait_ge(const, N_CONST)
            nc.vector.memset(vaug[:], 1.0)
            for n in range(16):
                nc.vector.tensor_scalar(sel[:, n, :], code[:, n // 4, :], shift[:, n // 8, n % 4:n % 4 + 1], None, ALU.is_equal)
            link(nc.vector.tensor_scalar(one_at[:, 1, :], one_at[:, 0, :], 0.0, None, ALU.is_equal))
            nc.vector.tensor_reduce(one_at[:, 2, 0:1], one_at[:, 1, :], AX.X, ALU.add).then_inc(sel_ready, 1)

            def low_part(n):
                dve.wait_ge(hi_ready, n + 1)
                if n < NB:
                    nc.vector.tensor_tensor(hl[0:KV * HD, n % 2, 1, :], ps[0:KV * HD, 1 + n, :],
                                            hl[0:KV * HD, n % 2, 0, :].bitcast(F32), ALU.subtract).then_inc(lo_ready, 1)
                else:
                    nc.vector.scalar_tensor_tensor(out=hl[:, n % 2, 1, :], in0=ps[:, (5 + n - NB) % 8, :], scalar=SCALE,
                                                   in1=hl[:, n % 2, 0, :].bitcast(F32),
                                                   op0=ALU.mult, op1=ALU.subtract).then_inc(lo_ready, 1)

            layernorm(0)
            evacuate_xT(0)
            choose(m0)
            for n in range(NB):
                low_part(n)
            slots(m0)
            for n in range(NB, NB + 2 * CC):
                low_part(n)
            dve.wait_ge(v_ps, 1)
            nc.vector.tensor_copy(vaug[:, :, :, 0:HD],
                                  ps[:, 3, :].rearrange("p (t h d) -> p t h d", t=NT, d=HD)).then_inc(v_sb, 1)
            place_ids(m0)
            integer_ids(m0)
            dve.wait_ge(m0.xn_stored, 16)
            for kind, *which in steps0:
                m = m0
                if kind == "hidden":
                    t, = which
                    dve.wait_ge(m.th_sb, t + 1)
                    nc.vector.scalar_tensor_tensor(out=ga[:, t % 2, :], in0=th[:, t % 2, :], scalar=1.0,
                                                   in1=ps[:, 4, 0:m.H], op0=ALU.add, op1=ALU.mult).then_inc(m.ga_sb, 1)
                    dve.wait_ge(m.ga_sb, t + 1)
                    dve.wait_ge(m.u_ps, t + 1)
                    at_least(dve, m.h_ps, t - 1)
                    nc.vector.scalar_tensor_tensor(out=hh[:, t % 2, :], in0=ga[:, t % 2, :], scalar=0.5,
                                                   in1=ps[:, 5, 0:m.H], op0=ALU.mult, op1=ALU.mult).then_inc(m.h_sb, 1)
                elif kind == "down":
                    t, = which
                    dve.wait_ge(m.y_ps, t + 2)
                    at_least(dve, m.y_out[t % YBUF], 16 * (t // YBUF))
                    nc.vector.tensor_copy(ysb[:, t % YBUF, :], ps[:, 6, 0:D]).then_inc(m.y_sb, 1)
                elif kind == "score":
                    g, i = which
                    j, qt = group_order(i)
                    dve.wait_ge(s_ps, unit_of[kind, g, i] + 1)
                    nc.vector.tensor_reduce(rowmax[:, g, i:i + 1], ps[:, 0, 0:(qt + 1) * P], AX.X, ALU.max).then_inc(s_read, 1)
                elif kind == "neg":
                    g, = which
                    dve.wait_ge(s_ps, unit_of[kind, g] + 1)
                    nc.vector.tensor_scalar(nmax[:, 0, g, :], ps[0:16, 0, 0:P], -1.0, None, ALU.mult).then_inc(nmax_ready, 1)
                    dve.wait_ge(nmax_ready, 2 * g + 1)
                    nc.vector.scalar_tensor_tensor(out=nmax[:, 1, g, :], in0=ps[0:16, 0, 0:P], scalar=-1.0,
                                                   in1=nmax[:, 0, g, :].bitcast(F32), op0=ALU.mult,
                                                   op1=ALU.subtract).then_inc(nmax_ready, 1)
                elif kind == "out":
                    g, = which
                    b, kv = divmod(g, KV)
                    dve.wait_ge(s_ps, unit_of[kind, g] + 1)
                    made = ps[:, 0, :].rearrange("p (t j d) -> p t j d", t=TPS, d=2 * HD)
                    link(nc.vector.reciprocal(rsum[:, g % 2], made[:, :, :, HD]))
                    for t in range(TPS):
                        last = nc.vector.tensor_tensor(
                            xn[:, b * TPS + t, kv * 64:(kv + 1) * 64].rearrange("p (j d) -> p j d", d=HD),
                            made[:, t, :, 0:HD], rsum[:, g % 2, t, :].unsqueeze(2).to_broadcast([P, GRP, HD]), ALU.mult)
                    last.then_inc(o_norm, 1)
                elif kind == "add":
                    combine(m, which[0])
            for c in range(2 * CC):
                dve.wait_ge(ot_ps, c + 1)
                nc.vector.tensor_copy(xT[:, c // 2, (c % 2) * S:(c % 2 + 1) * S], ps[:, c, :]).then_inc(ot_sb, 1)
            dve.wait_ge(m0.added, m0.K * NT)
            for i in range(NT // 2):
                dve.wait_ge(wo_ps, i + 1)
                last = nc.vector.tensor_tensor(acc[:, 2 * i:2 * i + 2, :], ps[:, 4 + i, :].rearrange("p (t c) -> p t c", t=2),
                                               acc[:, 2 * i:2 * i + 2, :], ALU.add)
                last.then_inc(wo_add, 1)
            dve.wait_ge(wo_add, NT // 2)
            for b in range(YBUF):
                dve.wait_ge(m0.y_out[b], 16 * len(range(b, m0.tiles, YBUF)))
            nc.vector.memset(vf[:], 1.0)
            layernorm(1)
            evacuate_xT(1)
            choose(m1)
            for c in range(2 * CC):
                dve.wait_ge(q1_ps, c + 1)
                bank = (5 + c) % 8
                at_least(dve, q1_f, c - 1)
                nc.vector.tensor_scalar(emin[:, c % 2, :], ps[:, bank, :], 0.0, None, ALU.min).then_inc(q1_min, 1)
                dve.wait_ge(q1_exp, c + 1)
                nc.vector.scalar_tensor_tensor(out=qf[:, c // 2, (c % 2) * S:(c % 2 + 1) * S], in0=ps[:, bank, :], scalar=0.0,
                                               in1=emin[:, c % 2, :], op0=ALU.max, op1=ALU.add).then_inc(q1_f, 1)
            dve.wait_ge(q1_f, 2 * CC)
            for t in range(NT):
                dve.wait_ge(v1_sb, t + 1)
                at_least(dve, k1_f, t - 1)
                nc.vector.tensor_scalar(emin[:, t % 2, 0:D], ps[:, 1 + t % 3, 0:D], 0.0, None, ALU.min).then_inc(k1_min, 1)
                dve.wait_ge(k1_exp, t + 1)
                nc.vector.scalar_tensor_tensor(out=kf[:, t, :], in0=ps[:, 1 + t % 3, 0:D], scalar=0.0,
                                               in1=emin[:, t % 2, 0:D], op0=ALU.max, op1=ALU.add).then_inc(k1_f, 1)
            slots(m1)
            for b in range(NB):
                dve.wait_ge(sh_tanh, b + 1)
                nc.vector.scalar_tensor_tensor(out=sh_ga, in0=sh_th, scalar=1.0, in1=ps[:, 0, :],
                                               op0=ALU.add, op1=ALU.mult).then_inc(sh_ga_ready, 1)
                dve.wait_ge(sh_ga_ready, b + 1)
                dve.wait_ge(sh_u, b + 1)
                nc.vector.scalar_tensor_tensor(out=shT[:, b * S:(b + 1) * S], in0=sh_ga, scalar=0.5, in1=ps[:, 7, :],
                                               op0=ALU.mult, op1=ALU.mult).then_inc(sh_sb, 1)
                dve.wait_ge(kv_ps, b + 1)
                for c in range(CC):
                    at = 2 * P * c
                    nc.vector.tensor_tensor(kvd[:, b, c, 0, :], ps[:, 5 + b, at:at + P], same_head[:], ALU.mult).then_inc(kv_sb, 1)
                    nc.vector.tensor_scalar(kvd[:, b, c, 1, :], same_head[:], ps[:, 5 + b, at + P:at + P + 1], None,
                                            ALU.mult).then_inc(kv_sb, 1)
            place_ids(m1)
            integer_ids(m1)
            for c in range(2 * CC):
                b, mm = divmod(c, CC)
                dve.wait_ge(nd_ps, c + 1)
                link(nc.vector.tensor_scalar(emin[:, 0, :], ps[:, 2 * (c % 2) + 1, :], 1e-6, None, ALU.add))
                link(nc.vector.reciprocal(emin[:, 1, :], emin[:, 0, :]))
                nc.vector.tensor_tensor(xT[:, mm, b * S:(b + 1) * S], ps[:, 2 * (c % 2), :], emin[:, 1, :], ALU.mult).then_inc(nd_read, 1)
                dve.wait_ge(nd_read, c + 1)
            for i in range(NT // 2):
                dve.wait_ge(wo1_ps, i + 1)
                nc.vector.tensor_tensor(acc[:, 2 * i:2 * i + 2, :], ps[:, 4 + i, :].rearrange("p (t c) -> p t c", t=2),
                                        acc[:, 2 * i:2 * i + 2, :], ALU.add).then_inc(wo1_add, 1)
            dve.wait_ge(wo1_add, NT // 2)
            run_tiles(dve, m1, tile_parts)
            for t in range(NT):
                combine(m1, t)

        @block.tensor
        def _(pe):
            mm_ = nc.tensor.matmul

            def transpose_x(n):
                if n:
                    pe.wait_ge(wo_add, NT // 2)
                for t in range(NT):
                    pe.wait_ge(xn_ready, NT * n + t + 1)
                    for c in range(CC):
                        last = nc.tensor.transpose(ps[:, 2 * c + t // TPS, (t % TPS) * P:(t % TPS + 1) * P],
                                                   xn[:, t, c * P:(c + 1) * P], ident[:])
                    last.then_inc(xT_ps, 1)

            def logits(m):
                for t in range(NT):
                    for c in range(CC):
                        last = mm_(ps[:, 4, t * m.E:(t + 1) * m.E], xT[:, c, t * P:(t + 1) * P], m.gate[:, c, :],
                                   start=c == 0, stop=c == CC - 1)
                last.then_inc(m.lg_ps, 1)

            def ranks(m):
                pe.wait_ge(m.member_ready, 1)
                n = NT * m.E
                mm_(ps[:, 4, 0:n + m.E], onesb[:], m.earlier[:].rearrange("p t e -> p (t e)"), start=True, stop=False,
                    skip_group_check=True)
                mm_(ps[:, 4, 0:n], before[:], m.member[:].rearrange("p t e -> p (t e)"), start=False, stop=True,
                    skip_group_check=True).then_inc(m.rank_ps, 1)

            def place_ids(m):
                pe.wait_ge(m.tab_ready, 1)
                for k in range(m.K):
                    pe.wait_ge(m.hot_ready, k + 1)
                    for t in range(NT):
                        for part in range(2):
                            last = mm_(ps[:, 4, 0:m.tiles], m.hot_row[:, k % 2, t, :], m.hot_id[:, k % 2, part, t, :],
                                       start=k == 0 and t == 0 and part == 0, stop=k == m.K - 1 and t == NT - 1 and part == 1)
                    last.then_inc(m.hot_used, 1)

            def rows(m, t, arrived):
                xbuf, count = arrived
                pe.wait_ge(m.gathered[xbuf], count)
                at_least(pe, m.x_sb, t)
                for c in range(CC):
                    last = nc.tensor.transpose(ps[:, 4, c * P:(c + 1) * P], xg[:, xbuf, c * P:(c + 1) * P], ident[:])
                last.then_inc(m.x_ps, 1)

            def tile_parts(m, t, p):
                half = p["half"]

                def slot_of(tile):
                    return nc.tensor.value_load(m.tab[0:1, 2, bass.ds(tile, 1)], min_val=0, max_val=m.ring - 1)

                if p["row"]:
                    rows(m, t + 1, (p["xbuf"], p["gathered"]))
                if p["ug"]:
                    loaded = nc.tensor.value_load(m.tab[0:1, 1, bass.ds(t, 1)], min_val=32, max_val=32 * m.E)
                    slot = slot_of(t)
                    pe.wait_ge(m.w_loaded, loaded)
                    pe.wait_ge(m.x_sb, t + 1)
                    at_least(pe, m.h_sb, t - 1)
                    for which, bank, ready in ((1, 2 + half, m.g_ps), (0, half, m.u_ps)):
                        for c in range(CC):
                            last = mm_(ps[:, bank, 0:m.H], xgT[:, half, c, :],
                                       m.wug[:, bass.ds(slot, 1), c, which, :].rearrange("p a n -> p (a n)"),
                                       start=c == 0, stop=c == CC - 1)
                        last.then_inc(ready, 1)
                if p["hid"]:
                    pe.wait_ge(m.h_sb, t)
                    at_least(pe, m.hT_sb, t - 1)
                    for b in range(m.HB):
                        last = nc.tensor.transpose(ps[0:m.HP, 5, b * P:(b + 1) * P],
                                                   hh[:, 1 - half, b * m.HP:(b + 1) * m.HP], ident[:])
                    last.then_inc(m.h_ps, 1)
                if p["down"]:
                    slot = slot_of(t - 2)
                    pe.wait_ge(m.hT_sb, t - 1)
                    at_least(pe, m.y_sb, t - 2)
                    for b in range(m.HB):
                        last = mm_(ps[:, 6, 0:D], hT[0:m.HP, half, b, :],
                                   m.wd[:, bass.ds(slot, 1), b, :].rearrange("p a n -> p (a n)"),
                                   start=b == 0, stop=b == m.HB - 1)
                    last.then_inc(m.y_ps, 1)

            def first_rows(m):
                rows(m, 0, (0, 16))

            pe.sem_inc(m0.y_ps, 1)
            pe.sem_inc(m1.y_ps, 1)
            pe.wait_ge(const, N_CONST)
            transpose_x(0)
            pe.wait_ge(xT_act, 2)
            pe.wait_ge(xT_dve, 2)
            pe.wait_ge(g_in, 32)
            logits(m0)
            pe.wait_ge(w_in0, 64)
            for b in range(NB):
                for c in range(CC):
                    last = mm_(ps[0:KV * HD, 1 + b, :], wk0[:, c, :], xT[:, c, b * S:(b + 1) * S], start=c == 0, stop=c == CC - 1)
                last.then_inc(k_ps, 1)

            def q_block(i):
                mm, b = divmod(i, NB)
                for c in range(CC):
                    last = mm_(ps[:, (5 + i) % 8, :], wq0[:, c, mm * P:(mm + 1) * P], xT[:, c, b * S:(b + 1) * S],
                               start=c == 0, stop=c == CC - 1)
                last.then_inc(q_ps, 1)

            def select(n):
                pe.wait_ge(hi_ready, n + 1)
                pe.wait_ge(lo_ready, n + 1)
                if n == 0:
                    pe.wait_ge(lo_ready, NB)
                first, height = (8, KV * HD) if n < NB else (0, P)
                for j in range(4):
                    u = 4 * n + j
                    at_least(pe, qk_in, u - 1)
                    for w in range(2):
                        last = mm_(ps[:, 1 + u % 2, :], sel[0:height, first + 4 * w + j, :], hl[0:height, n % 2, w, :],
                                   start=w == 0, stop=w == 1)
                    last.then_inc(sel_ps, 1)

            q_block(0)
            q_block(1)
            ranks(m0)
            for n in range(NB):
                select(n)
            q_block(2)
            q_block(3)
            for t in range(NT):
                for c in range(CC):
                    last = mm_(ps[:, 3, t * 64:(t + 1) * 64], xT[:, c, t * P:(t + 1) * P], wv0[:, c, :], start=c == 0, stop=c == CC - 1)
            last.then_inc(v_ps, 1)
            for n in range(NB, NB + 2 * CC):
                select(n)
            place_ids(m0)
            pe.wait_ge(v_sb, 1)
            pe.wait_ge(m0.ids_ready, 1)
            pe.wait_ge(qk_in, 4 * (NB + 2 * CC))

            def free_unit(n):
                if n:
                    kind, g, *i = units[n - 1]
                    if kind == "score":
                        pe.wait_ge(s_read, 16 * g + i[0] + 1)
                    elif kind == "neg":
                        pe.wait_ge(nmax_ready, 2 * g + 2)
                    else:
                        pe.wait_ge(o_norm, g + 1)

            def slot_of(m, t):
                return nc.tensor.value_load(m.tab[0:1, 2, t:t + 1], min_val=0, max_val=m.ring - 1)

            for kind, *which in steps0:
                m = m0
                if kind == "rows":
                    t, = which
                    pe.wait_ge(m.gathered[t % XBUF], 16 * (t // XBUF + 1))
                    at_least(pe, m.y_sb, t - 2)
                    at_least(pe, m.x_sb, t)
                    for c in range(CC):
                        last = nc.tensor.transpose(ps[:, 6, c * P:(c + 1) * P], xg[:, t % XBUF, c * P:(c + 1) * P], ident[:])
                    last.then_inc(m.x_ps, 1)
                elif kind in ("gate", "up"):
                    t, = which
                    if kind == "gate":
                        slot = slot_of(m, t)
                        loaded = nc.tensor.value_load(m.tab[0:1, 1, t:t + 1], min_val=32, max_val=32 * m.E)
                        pe.wait_ge(m.w_loaded, loaded)
                        pe.wait_ge(m.x_sb, t + 1)
                        at_least(pe, m.ga_sb, t)
                    else:
                        at_least(pe, m.h_sb, t)
                    part, bank, ready = (1, 4, m.g_ps) if kind == "gate" else (0, 5, m.u_ps)
                    for c in range(CC):
                        last = mm_(ps[:, bank, 0:m.H], xgT[:, t % 2, c, :],
                                   m.wug[:, bass.ds(slot, 1), c, part, :].rearrange("p a n -> p (a n)"),
                                   start=c == 0, stop=c == CC - 1)
                    last.then_inc(ready, 1)
                elif kind == "turn":
                    t, = which
                    pe.wait_ge(m.h_sb, t + 1)
                    at_least(pe, m.hT_sb, t)
                    for b in range(m.HB):
                        last = nc.tensor.transpose(ps[0:m.HP, 7, b * P:(b + 1) * P], hh[:, t % 2, b * m.HP:(b + 1) * m.HP], ident[:])
                    last.then_inc(m.h_ps, 1)
                elif kind == "down":
                    t, = which
                    slot_d = slot_of(m, t)
                    pe.wait_ge(m.hT_sb, t + 1)
                    at_least(pe, m.y_sb, t)
                    pe.wait_ge(m.x_sb, min(t + 3, m.tiles))
                    for b in range(m.HB):
                        last = mm_(ps[:, 6, 0:D], hT[0:m.HP, t % 2, b, :],
                                   m.wd[:, bass.ds(slot_d, 1), b, :].rearrange("p a n -> p (a n)"),
                                   start=b == 0, stop=b == m.HB - 1)
                    last.then_inc(m.y_ps, 1)
                elif kind == "score":
                    g, i = which
                    j, qt = group_order(i)
                    b, kv = divmod(g, KV)
                    free_unit(unit_of[kind, g, i])
                    L = (qt + 1) * P
                    r = 64 * (j % 2)
                    h = kv * GRP + j
                    q0 = b * S + qt * P
                    mm_(ps[:, 0, 0:L], qa[r:r + 3 * HD, h // 2, q0:q0 + P], ka[r:r + 3 * HD, kv, b * S:b * S + L],
                        start=True, stop=False, skip_group_check=True)
                    mm_(ps[:, 0, qt * P:L], identb[:], mask_qk[:], start=False, stop=True,
                        skip_group_check=True).then_inc(s_ps, 1)
                elif kind == "neg":
                    g, = which
                    free_unit(unit_of[kind, g])
                    pe.wait_ge(s_read, 16 * (g + 1))
                    nc.tensor.transpose(ps[0:16, 0, 0:P], rowmax[:, g, :], ident[:]).then_inc(s_ps, 1)
                elif kind == "prob":
                    g, i = which
                    kb, j = divmod(i, GRP)
                    b, kv = divmod(g, KV)
                    n = g * 16 + i
                    at_least(pe, p_sb, n - 1)
                    if i == 0:
                        pe.wait_ge(nmax_in[g], 32)
                    k0 = b * S + kb * P
                    r = 64 * (j % 2)
                    h = kv * GRP + j
                    mm_(ps[:, 1 + n % 2, kb * P:S], ka[r:r + 3 * HD + 2, kv, k0:k0 + P], qa[r:r + 3 * HD + 2, h // 2, k0:(b + 1) * S],
                        start=True, stop=False, skip_group_check=True)
                    mm_(ps[:, 1 + n % 2, kb * P:(kb + 1) * P], identb[:], mask_kq[:], start=False, stop=True,
                        skip_group_check=True).then_inc(st_ps, 1)
                elif kind == "value":
                    g, kb = which
                    b, kv = divmod(g, KV)
                    pe.wait_ge(p_sb, g * 16 + 4 * (kb + 1))
                    if kb == 0:
                        at_least(pe, o_sb, g)
                    for j in range(GRP):
                        last = mm_(ps[32 * j:32 * j + 32, 3, kb * P:S], vaug[:, b * TPS + kb, kv, :], pT[:, kb % 2, j, kb * P:S],
                                   start=kb == 0, stop=kb == TPS - 1, skip_group_check=True)
                    last.then_inc(pv_used, 1)
                elif kind == "out":
                    g, = which
                    free_unit(unit_of[kind, g])
                    pe.wait_ge(o_sb, g + 1)
                    for t in range(TPS):
                        last = nc.tensor.transpose(ps[:, 0, t * P:(t + 1) * P], oT[:, g % 2, t * P:(t + 1) * P], ident[:])
                    last.then_inc(s_ps, 1)
            pe.wait_ge(o_norm, G)
            pe.wait_ge(p_sb, 16 * G)
            pe.wait_ge(o_sb, G)
            for i in range(2 * CC):
                c, b = i // 2, i % 2
                for t in range(TPS):
                    last = nc.tensor.transpose(ps[:, i, t * P:(t + 1) * P], xn[:, b * TPS + t, c * P:(c + 1) * P], ident[:])
                last.then_inc(ot_ps, 1)
            pe.wait_ge(ot_sb, 2 * CC)
            pe.wait_ge(m0.h_sb, m0.tiles)
            pe.wait_ge(m0.hT_sb, m0.tiles)
            pe.wait_ge(m0.y_sb, m0.tiles)
            for t in range(NT):
                for c in range(CC):
                    last = mm_(ps[:, 4 + t // 2, (t % 2) * D:(t % 2 + 1) * D], xT[:, c, t * P:(t + 1) * P], wo0[:, c, :],
                               start=c == 0, stop=c == CC - 1)
                if t % 2:
                    last.then_inc(wo_ps, 1)

            def shared_expert(b):
                pe.wait_ge(ws_in, 32)
                at_least(pe, sh_sb, b)
                for part, bank, ready in ((1, 0, sh_g), (0, 7, sh_u)):
                    for c in range(CC):
                        last = mm_(ps[:, bank, :], ws_ug[:, c, part, :], xT[:, c, b * S:(b + 1) * S], start=c == 0, stop=c == CC - 1)
                    last.then_inc(ready, 1)

            transpose_x(1)
            pe.wait_ge(xT_act, 4)
            pe.wait_ge(xT_dve, 4)
            logits(m1)
            pe.wait_ge(w_in1, 48)
            for i in range(2 * CC):
                mm, b = i // 2, i % 2
                for c in range(CC):
                    last = mm_(ps[:, (5 + i) % 8, :], wq1[:, c, mm * P:(mm + 1) * P], xT[:, c, b * S:(b + 1) * S],
                               start=c == 0, stop=c == CC - 1)
                last.then_inc(q1_ps, 1)
            for t in range(NT):
                at_least(pe, k1_f, t - 2)
                for c in range(CC):
                    last = mm_(ps[:, 1 + t % 3, :], xT[:, c, t * P:(t + 1) * P], wkv1[:, c, :], start=c == 0, stop=c == CC - 1)
                last.then_inc(k1_ps, 1)
                if t == 2:
                    ranks(m1)
            pe.wait_ge(q1_f, 2 * CC)
            shared_expert(0)
            pe.wait_ge(k1_f, NT)
            for b in range(NB):
                for c in range(CC):
                    for t in range(TPS):
                        tt = b * TPS + t
                        last = mm_(ps[:, 5 + b, 2 * P * c:2 * P * c + P + 1], kf[:, tt, c * P:(c + 1) * P], vf[:, tt, c, :],
                                   start=t == 0, stop=t == TPS - 1)
                last.then_inc(kv_ps, 1)
            shared_expert(1)
            place_ids(m1)
            for i in range(2 * CC):
                b, c = divmod(i, CC)
                pe.wait_ge(kv_sb, 2 * i + 2)
                at_least(pe, nd_read, i - 1)
                if i == 0:
                    pe.wait_ge(sh_sb, NB)
                for n in range(2):
                    last = mm_(ps[:, 2 * (i % 2) + n, :], kvd[:, b, c, n, :], qf[:, c, b * S:(b + 1) * S], start=True, stop=True)
                last.then_inc(nd_ps, 1)
            pe.wait_ge(nd_read, 2 * CC)
            pe.wait_ge(m1.ids_ready, 1)
            for t in range(NT):
                at = ps[:, 4 + t // 2, (t % 2) * D:(t % 2 + 1) * D]
                for c in range(CC):
                    mm_(at, xT[:, c, t * P:(t + 1) * P], wo1[:, c, :], start=c == 0, stop=False)
                last = mm_(at, shT[:, t * P:(t + 1) * P], ws_d[:], start=False, stop=True)
                if t % 2:
                    last.then_inc(wo1_ps, 1)
            pe.wait_ge(wo1_add, NT // 2)
            first_rows(m1)
            run_tiles(pe, m1, tile_parts)


_ORDER = ["x", "wq0", "wk0", "wv0", "wo0", "gate0", "wug0", "wd0", "wq1", "wkv1", "wo1", "gate1", "wug1", "wd1", "ws_ug", "ws_d"]


def kernel(**inputs):
    import numpy as np
    import concourse.bacc as bacc
    from concourse.bass_utils import run_bass_kernel_spmd

    g = {k: np.asarray(v) for k, v in inputs.items()}

    def gate_up(up, gate):
        both = np.stack([up, gate], 1).transpose(0, 3, 1, 2)
        e, c, two, h = both.shape
        return both.reshape(e, c // P, P, two, h).transpose(0, 2, 1, 3, 4)

    def down(w, hp):
        e, c, h = w.shape
        return w.transpose(0, 2, 1).reshape(e, h // hp, hp, c).transpose(0, 2, 1, 3)

    x = g["L0_attn_x"]
    arrays = {
        "x": x.reshape(-1, D),
        "wq0": g["L0_attn_Wq"], "wk0": g["L0_attn_Wk"], "wv0": g["L0_attn_Wv"], "wo0": g["L0_attn_Wo"],
        "gate0": g["L0_ffn_gate_inp"].T,
        "wug0": gate_up(g["L0_ffn_W_up"], g["L0_ffn_W_gate"]), "wd0": down(g["L0_ffn_W_down"], 112),
        "wq1": g["L1_attn_Wq"].T,
        "wkv1": np.concatenate([g["L1_attn_Wk"].T, g["L1_attn_Wv"].T], 1),
        "wo1": g["L1_attn_Wo"].T,
        "gate1": g["L1_ffn_gate_w"].T,
        "wug1": gate_up(g["L1_ffn_w3"], g["L1_ffn_w1"]), "wd1": down(g["L1_ffn_w2"], P),
        "ws_ug": gate_up(g["L1_ffn_ws3"][None], g["L1_ffn_ws1"][None])[0], "ws_d": g["L1_ffn_ws2"].T,
    }
    arrays = {k: np.ascontiguousarray(v) for k, v in arrays.items()}
    nc = bacc.Bacc("TRN2", target_bir_lowering=False, num_devices=1)
    args = {k: nc.dram_tensor("in_" + k, arrays[k].shape, F32, kind="ExternalInput").ap() for k in _ORDER}
    out = nc.dram_tensor("out", arrays["x"].shape, F32, kind="ExternalOutput").ap()
    build(nc, args, out)
    r = run_bass_kernel_spmd(nc, [{"in_" + k: arrays[k] for k in _ORDER}], core_ids=[0])
    return r.results[0]["out"].reshape(x.shape)
```

```python
from contextlib import ExitStack

import concourse.bass as bass
from concourse import mybir

F32 = mybir.dt.float32
F32R = mybir.dt.float32r
BF16 = mybir.dt.bfloat16
I32 = mybir.dt.int32
U32 = mybir.dt.uint32
ALU = mybir.AluOpType
ACT = mybir.ActivationFunctionType
AX = mybir.AxisListType

P = 128
D = 256
CC = D // P
BANK = 512
NEG = -3.0e38
EPS_LN = 1e-5
XBUF = 4
YBUF = 4
EARLY = 8


class Moe:

    SHIFT = 9

    def __init__(self, tag, experts, choices, hidden, tokens, ring):
        self.tag = tag
        self.E = experts
        self.K = choices
        self.H = hidden
        self.HP = 112 if hidden % P else P
        self.HB = hidden // self.HP
        self.NT = tokens // P
        self.tiles = (tokens * choices + experts * (P - 1)) // P
        self.ring = ring
        self.reciprocal = (1 << self.SHIFT) // ring + 1
        assert all(e * self.reciprocal >> self.SHIFT == e // ring for e in range(experts))


def at_least(eng, sem, value):
    if not isinstance(value, int) or value > 0:
        eng.wait_ge(sem, value)


def run_tiles(eng, m, parts):
    n = m.tiles

    def written_out(t, first, last):
        parts(m, t, dict(count=t - first, next=t + 1 < min(n, last), half=t % 2, xbuf=(t + 1) % XBUF, ybuf=(t - 2) % YBUF,
                         ug=t < n, hid=1 <= t <= n, row=t + 1 < n, down=2 <= t <= n + 1,
                         gathered=16 * ((t + 1 - EARLY) // XBUF + 1) if t + 1 >= EARLY else 0,
                         stored=16 * ((t - 2) // YBUF)))

    peeled = EARLY
    assert peeled % XBUF == 0 and XBUF == YBUF == 4
    end = peeled + (n - peeled - 1) // 4 * 4
    for t in range(peeled):
        written_out(t, 0, peeled)
    with eng.Fori(peeled, end, 4) as i:
        for u in range(4):
            parts(m, i + u, dict(count=u, next=u < 3, half=u % 2, xbuf=(u + 1) % XBUF, ybuf=(u - 2) % YBUF,
                                 ug=True, hid=True, row=True, down=True,
                                 gathered=i * 4 - EARLY * 4 + 16 * ((u + 1) // XBUF + 1), stored=i * 4 + 16 * ((u - 2) // YBUF)))
    for t in range(end, n + 2):
        written_out(t, end, n)


def mixed_steps(m, groups, tps):
    rest = []
    for step in range(-2, groups + 1):
        for i in range(16):
            slot = []
            if 0 <= step < groups:
                slot.append(("prob", step, i))
            if step + 2 < groups:
                slot.append(("score", step + 2, i))
            if 0 <= step < groups and i % 4 == 2 and i > 4:
                slot.append(("value", step, i // 4 - 1))
            if step >= 1:
                if i == 1:
                    slot.append(("value", step - 1, tps - 1))
                if i == 6:
                    slot.append(("out", step - 1))
            if i == 4 and 0 <= step + 1 < groups:
                slot.append(("send", step + 1))
            if i == 9 and 0 <= step + 1 < groups:
                slot.append(("fetch", step + 1))
            if i == 1 and 0 <= step + 1 < groups:
                slot.append(("neg", step + 1))
            rest.append(slot)
    items = [("rows", 0)]
    along = (1, 1, 1, 0)
    taken = 0
    for t in range(m.tiles + 1):
        for n, piece in enumerate((([("gate", t)] if t < m.tiles else []) + ([("rows", t + 1)] if t + 1 < m.tiles else []),
                                   [("up", t), ("hidden", t)] if t < m.tiles else [],
                                   [("down", t - 1)] if t else [],
                                   [("turn", t)] if t < m.tiles else [])):
            items += piece
            for slot in rest[taken:taken + along[n]]:
                items += slot
            taken += along[n]
    left = rest[taken:]
    added = 0
    for n, slot in enumerate(left):
        items += slot
        due = max(0, n - 12) * m.NT // (len(left) - 13)
        items += [("add", t) for t in range(added, due)]
        added = max(added, due)
    return items


def group_order(i):
    s, rest = divmod(i, 8)
    pair, qt = divmod(rest, 4)
    return 2 * pair + s, qt


def build(nc, a, out):
    NTOK = a["x"].shape[0]
    NT = NTOK // P
    NB = 2
    S = NTOK // NB
    TPS = S // P
    HD = 16
    KV = 4
    GRP = 4
    G = NB * KV
    SCALE = HD ** -0.5

    m0 = Moe("m0", 16, 4, 448, NTOK, 3)
    m1 = Moe("m1", 8, 2, 128, NTOK, 8)
    m0.wug_dram, m0.wd_dram = a["wug0"], a["wd0"]
    m1.wug_dram, m1.wd_dram = a["wug1"], a["wd1"]
    steps0 = mixed_steps(m0, G, TPS)
    units = [x for x in steps0 if x[0] in ("score", "neg", "out")]
    unit_of = {x: n for n, x in enumerate(units)}

    with ExitStack() as ctx:
        def sb(name, shape, dt=F32):
            return ctx.enter_context(nc.sbuf_tensor(name, shape, dt))

        def sem(name):
            return ctx.enter_context(nc.semaphore(name))

        ps = ctx.enter_context(nc.psum_tensor("ps", [P, 8, BANK], F32))

        ident = sb("ident", [P, P])
        identb = sb("identb", [P, P], BF16)
        onesb = sb("onesb", [P, P], BF16)
        before = sb("before", [P, P], BF16)
        mask_qk = sb("mask_qk", [P, P], BF16)
        mask_kq = sb("mask_kq", [P, P], BF16)
        same_head = sb("same_head", [P, P])
        tokid = sb("tokid", [P, NT])
        iota_p = sb("iota_p", [P, P])
        place = sb("place", [P, 4, NT])

        acc = sb("acc", [P, NT, D])
        xn = sb("xn", [P, NT, D])
        xT = sb("xT", [P, CC, NTOK])
        bn = sb("bn", [P, NT, 6])
        mv = sb("mv", [P, NT, 2])
        rstd = sb("rstd", [P, 4, NT])

        wqo0 = sb("wqo0", [P, 2, CC, D])
        wq0, wo0 = wqo0[:, 0], wqo0[:, 1]
        wk0, wv0 = (sb(n, [P, CC, KV * HD]) for n in ("wk0", "wv0"))
        wq1, wkv1, wo1 = (sb(n, [P, CC, w]) for n, w in (("wq1", D), ("wkv1", 2 * D), ("wo1", D)))

        qa = sb("qa", [P, 8, NTOK], F32R)
        ka = sb("ka", [P, KV, NTOK], F32R)
        vaug = sb("vaug", [P, NT, KV, 2 * HD])
        rowmax = sb("rowmax", [P, G, 16])
        pT = sb("pT", [P, 2, GRP, S])
        oT = sb("oT", [P, 2, S])
        rsum = sb("rsum", [P, 2, TPS, GRP])
        vf = sb("vf", [P, NT, CC, P + 1])
        hl = sb("hl", [P, 2, 2, S], F32R)
        sel = sb("sel", [P, 16, P], F32R)
        nmax = sel[0:16].rearrange("p (w g) n -> p w g n", w=2)
        code = oT[:].rearrange("p a n -> p (a n)")[:, 0:4 * P].rearrange("p (w n) -> p w n", w=4)
        shift = sb("shift", [P, 2, 4])
        one_at = sb("one_at", [P, 3, 4])

        xg = sb("xg", [P, XBUF, D])
        xgT = sb("xgT", [P, 2, CC, P])
        work = sb("work", [P, 3, 2, m0.H])
        th, ga, hh = work[:, 0], work[:, 1], work[:, 2]
        hT = sb("hT", [P, 2, m0.HB, P])
        ysb = vf[:].rearrange("p t c n -> p (t c n)")[:, 0:YBUF * D].rearrange("p (b c) -> p b c", b=YBUF)

        kf = pT[:, 0].rearrange("p j n -> p (j n)").rearrange("p (t c) -> p t c", t=NT)
        qf = pT[:, 1].rearrange("p j n -> p (j n)").rearrange("p (c n) -> p c n", c=CC)
        att = kf
        KVW = P + P // HD
        kvd = oT[:].rearrange("p a n -> p (a n)").rearrange("p (b c n) -> p b c n", b=NB, c=CC)
        den = sb("den", [P, NT, 2, CC, P // HD])
        emin = hT[:].rearrange("p a b n -> p (a b n)").rearrange("p (a n) -> p a n", a=2)

        m0.wug = sb("m0wug", [P, m0.ring, CC, 2, m0.H])
        wd_flat = sb("m0wd", [P, m0.ring * m0.HB * D])
        m0.wd = wd_flat[0:m0.HP].rearrange("p (r b n) -> p r b n", r=m0.ring, b=m0.HB)
        early = wd_flat[:, 0:EARLY * D].rearrange("p (t c) -> p t c", t=EARLY)
        w_flat = m0.wug[:].rearrange("p r c w n -> p (r c w n)")
        at = m1.ring * CC * 2 * m1.H
        m1.wug = w_flat[:, 0:at].rearrange("p (r c w n) -> p r c w n", r=m1.ring, c=CC, w=2)
        m1.wd = xn[:].rearrange("p (r b) n -> p r b n", b=m1.HB)
        ws_ug = w_flat[:, at:at + CC * 2 * m1.H].rearrange("p (c w n) -> p c w n", c=CC, w=2)
        at += CC * 2 * m1.H
        ws_d = w_flat[:, at:at + D]
        assert at + D <= m0.ring * CC * 2 * m0.H and m1.ring * m1.HB == NT
        shT = wqo0[:].rearrange("p w c n -> p (w c n)")

        flat = work[:].rearrange("p a b n -> p (a b n)")
        flat_end = 6 * m0.H
        sh_th, sh_ga = (flat[:, flat_end - n * BANK:flat_end - (n - 1) * BANK] for n in (2, 1))
        for m in (m0, m1):
            t = m.tag
            T = m.tiles
            m.hot_row = flat[:, 0:NT * P].bitcast(BF16).rearrange("p (w t r) -> p w t r", w=2, t=NT)
            at = NT * P
            m.hot_tile = flat[:, at:at + NT * T].rearrange("p (t a) -> p t a", t=NT)
            at += NT * T
            assert at + 2 * NT * T <= flat_end - (2 * BANK if m is m1 else 0)
            m.hot_id = flat[:, at:at + 2 * NT * T].bitcast(BF16).rearrange("p (w h t a) -> p w h t a", w=2, h=2, t=NT)
            m.gate = sb(t + "gate", [P, CC, m.E])
            m.logits = sb(t + "logits", [P, NT, m.E])
            m.best = sb(t + "best", [P, NT, 8])
            m.index = sb(t + "index", [P, NT, 8], U32)
            m.choice = sb(t + "choice", [P, NT, m.K])
            m.weight = sb(t + "weight", [P, NT, 8])
            m.wsum = sb(t + "wsum", [P, 2, NT])
            m.onehot = sb(t + "onehot", [P, m.K, NT, m.E])
            m.member = sb(t + "member", [P, NT, m.E], BF16)
            m.earlier = sb(t + "earlier", [P, NT + 1, m.E], BF16)
            m.cnt = sb(t + "cnt", [P, 4, m.E])
            m.cnti = sb(t + "cnti", [P, 2, m.E], I32)
            m.slot = sb(t + "slot", [P, NT, m.E])
            m.slotk = sb(t + "slotk", [P, m.K, NT])
            m.sloti = sb(t + "sloti", [P, m.K, NT], U32)
            m.cmp = sb(t + "cmp", [1, m.tiles, m.E])
            m.tile_e = sb(t + "tile_e", [1, m.tiles])
            m.tab = sb(t + "tab", [1, 3, m.tiles], I32)
            m.cum = sb(t + "cum", [1, m.E], I32)
            m.split = sb(t + "split", [P, 2, m.K * NT], I32)
            m.splitf = sb(t + "splitf", [P, 2, m.K * NT])
            m.taken = sb(t + "taken", [P, m.tiles], I32)
            m.ids = sb(t + "ids", [P, m.tiles], U32)
            m.dest = sb(t + "dest", [P, m.tiles], U32)
            m.spare = sb(t + "spare", [P, 3, m.tiles])
            m.x_dram = nc.dram_tensor(t + "x", [NTOK, D], F32, kind="Internal").ap()
            m.y_dram = nc.dram_tensor(t + "y", [m.K * NTOK + m.tiles * P, D], F32, kind="Internal").ap()
            m.zbuf = 5 if m is m0 else NT
            m.z = (w_flat if m is m0 else pT[:].rearrange("p a j n -> p (a j n)"))[:, 0:m.zbuf * m.K * D].rearrange(
                "p (b k c) -> p b k c", b=m.zbuf, k=m.K)

            m.w_loaded = sem(t + "w_loaded")
            m.xn_stored = sem(t + "xn_stored")
            m.hot_ready = sem(t + "hot_ready")
            m.hot_used = sem(t + "hot_used")
            m.ids_ready = sem(t + "ids_ready")
            m.lg_ps = sem(t + "lg_ps")
            m.ex_in = sem(t + "ex_in")
            m.ex_out = sem(t + "ex_out")
            m.member_ready = sem(t + "member_ready")
            m.rank_ps = sem(t + "rank_ps")
            m.slots_ready = sem(t + "slots_ready")
            m.tab_ready = sem(t + "tab_ready")
            if m is m1:
                m.early_in = [sem(f"early_in{i}") for i in range(EARLY)]
            m.gathered = [sem(t + f"gathered{i}") for i in range(XBUF)]
            m.x_ps = sem(t + "x_ps")
            m.x_sb = sem(t + "x_sb")
            m.g_ps = sem(t + "g_ps")
            m.u_ps = sem(t + "u_ps")
            m.th_sb = sem(t + "th_sb")
            m.ga_sb = sem(t + "ga_sb")
            m.h_sb = sem(t + "h_sb")
            m.h_ps = sem(t + "h_ps")
            m.hT_sb = sem(t + "hT_sb")
            m.y_ps = sem(t + "y_ps")
            m.y_sb = sem(t + "y_sb")
            m.y_out = [sem(t + f"y_out{i}") for i in range(YBUF)]
            m.back = [sem(t + f"back{i}") for i in range(NT)]
            m.added = sem(t + "added")

        x_in = [sem(f"x_in{i}") for i in range(NB)]
        w_in0, w_in1 = sem("w_in0"), sem("w_in1")
        g_in = sem("g_in")
        ws_in = sem("ws_in")
        const = sem("const")
        pool_c = sem("pool_c")
        dve_c = sem("dve_c")
        var_ready = sem("var_ready")
        std_ready = sem("std_ready")
        xn_ready = sem("xn_ready")
        xT_ps = sem("xT_ps")
        xT_act, xT_dve = sem("xT_act"), sem("xT_dve")
        q_ps, k_ps = sem("q_ps"), sem("k_ps")
        hi_ready, lo_ready = sem("hi_ready"), sem("lo_ready")
        v_ps, v_sb = sem("v_ps"), sem("v_sb")
        sel_ready = sem("sel_ready")
        sel_ps, qk_in = sem("sel_ps"), sem("qk_in")
        s_ps, s_read = sem("s_ps"), sem("s_read")
        nmax_ready = sem("nmax_ready")
        nmax_out = sem("nmax_out")
        nmax_in = sem("nmax_in")
        nmax_dram = nc.dram_tensor("nmax", [G, 2, 16, P], F32, kind="Internal").ap()
        st_ps, p_sb = sem("st_ps"), sem("p_sb")
        o_sb = sem("o_sb")
        pv_used = sem("pv_used")
        o_norm = sem("o_norm")
        ot_ps, ot_sb = sem("ot_ps"), sem("ot_sb")
        wo_ps, wo_add = sem("wo_ps"), sem("wo_add")
        q1_ps, k1_ps, v1_sb = sem("q1_ps"), sem("k1_ps"), sem("v1_sb")
        relu1, exp1, f1 = sem("relu1"), sem("exp1"), sem("f1")
        kv_ps, kv_sb = sem("kv_ps"), sem("kv_sb")
        nd_ps, nd_read = sem("nd_ps"), sem("nd_read")
        ot1_ps, ot1_sb = sem("ot1_ps"), sem("ot1_sb")
        wo1_ps, wo1_add = sem("wo1_ps"), sem("wo1_add")
        sh_g, sh_u = sem("sh_g"), sem("sh_u")
        sh_tanh, sh_ga_ready, sh_sb = sem("sh_tanh"), sem("sh_ga_ready"), sem("sh_sb")
        out_done = sem("out_done")

        def wait_added(eng, m, t):
            eng.wait_ge(m.added, m.K * (t + 1))

        SHARED_BANKS = ((0, 7), (1, 2))

        block = ctx.enter_context(nc.Block())
        N_CONST = 18

        @block.sync
        def _(sp):
            x_t = a["x"].rearrange("(t p) c -> p t c", p=P)
            for b in range(NB):
                sp.dma_start(acc[:, b * TPS:(b + 1) * TPS, :], x_t[:, b * TPS:(b + 1) * TPS, :]).then_inc(x_in[b], 16)
            chunked = "(a p) n -> p a n"
            sp.dma_start(m0.gate[:], a["gate0"].rearrange(chunked, p=P)).then_inc(g_in, 16)
            sp.dma_start(m1.gate[:], a["gate1"].rearrange(chunked, p=P)).then_inc(g_in, 16)
            for dst, name in ((wq0, "wq0"), (wk0[:], "wk0"), (wv0[:], "wv0"), (wo0, "wo0")):
                sp.dma_start(dst, a[name].rearrange(chunked, p=P)).then_inc(w_in0, 16)
            for dst, name in ((wq1, "wq1"), (wkv1, "wkv1"), (wo1, "wo1")):
                sp.dma_start(dst[:], a[name].rearrange(chunked, p=P)).then_inc(w_in1, 16)

            def load_expert(m, e, slot):
                sp.dma_start(m.wug[:, slot], m.wug_dram[e]).then_inc(m.w_loaded, 16)
                sp.dma_start(m.wd[:, slot], m.wd_dram[e]).then_inc(m.w_loaded, 16)

            def first_experts(m):
                for e in range(m.ring):
                    if e:
                        sp.wait_ge(m.w_loaded, 32 * e)
                    load_expert(m, e, e)

            def store_xn(m, n):
                sp.wait_ge(xn_ready, NT * (n + 1))
                sp.dma_start(m.x_dram.rearrange("(t p) c -> p t c", p=P), xn[:]).then_inc(m.xn_stored, 16)

            def results_back(m):
                for b in range(YBUF):
                    sp.wait_ge(m.y_out[b], 16 * len(range(b, m.tiles, YBUF)))
                rows_of = m.y_dram[0:m.K * NTOK, :].rearrange("(k t p) c -> t p k c", k=m.K, p=P)
                for t in range(NT):
                    if t >= m.zbuf:
                        wait_added(sp, m, t - m.zbuf)
                    sp.dma_start(m.z[:, t % m.zbuf], rows_of[t]).then_inc(m.back[t], 16)

            def other_experts(m):
                sp.wait_ge(m.tab_ready, 1)
                for e in range(m.ring, m.E):
                    sp.wait_ge(m.w_loaded, 32 * e)
                    used = nc.sync.value_load(m.cum[0:1, e - m.ring:e - m.ring + 1], min_val=1, max_val=m.tiles + 1)
                    sp.wait_ge(m.y_ps, used)
                    load_expert(m, e, e % m.ring)

            first_experts(m0)
            store_xn(m0, 0)
            other_experts(m0)
            results_back(m0)
            for t in range(NT):
                wait_added(sp, m0, t)
            sp.dma_start(ws_ug, a["ws_ug"]).then_inc(ws_in, 16)
            sp.dma_start(ws_d, a["ws_d"]).then_inc(ws_in, 16)
            sp.dma_start(m1.wug.rearrange("p e c w n -> p e (c w n)"),
                         m1.wug_dram.rearrange("e p c w n -> p e (c w n)")).then_inc(m1.w_loaded, 16)
            store_xn(m1, 1)
            sp.wait_ge(m1.xn_stored, 16)
            sp.wait_ge(xT_ps, 2 * NT)
            sp.dma_start(m1.wd.rearrange("p e b n -> p e (b n)"),
                         m1.wd_dram.rearrange("e p b n -> p e (b n)")).then_inc(m1.w_loaded, 16)
            results_back(m1)
            for t in range(NT):
                wait_added(sp, m1, t)
                sp.dma_start(out[t * P:(t + 1) * P, :], acc[:, t, :]).then_inc(out_done, 16)
            sp.wait_ge(out_done, 16 * NT)

        @block.gpsimd
        def _(pool):
            pool.memset(ident[:], 0.0).then_inc(pool_c, 1)
            pool.memset(onesb[:], 1.0).then_inc(const, 1)
            pool.memset(before[:], 0.0).then_inc(pool_c, 1)
            pool.memset(mask_qk[:], 0.0).then_inc(pool_c, 1)
            pool.memset(mask_kq[:], 0.0).then_inc(pool_c, 1)
            pool.memset(same_head[:], 1.0).then_inc(pool_c, 1)
            pool.iota(tokid[:], [[P, NT]], base=0, channel_multiplier=1,
                      allow_small_or_imprecise_dtypes=True).then_inc(const, 1)
            pool.iota(iota_p[:], [[1, P]], base=0, channel_multiplier=0,
                      allow_small_or_imprecise_dtypes=True).then_inc(const, 1)
            pool.iota(place[:], [[NTOK, 4], [P, NT]], base=NTOK, channel_multiplier=0,
                      allow_small_or_imprecise_dtypes=True).then_inc(const, 1)
            for m in (m0, m1):
                pool.iota(m.spare[:, 0, :], [[P, m.tiles]], base=(m.K + 1) * NTOK, channel_multiplier=1,
                          allow_small_or_imprecise_dtypes=True).then_inc(const, 1)
            pool.iota(shift[:, 0, :], [[-2 * HD, 4]], base=0, channel_multiplier=1,
                      allow_small_or_imprecise_dtypes=True).then_inc(const, 1)
            pool.iota(shift[:, 1, :], [[-HD, 4]], base=0, channel_multiplier=1,
                      allow_small_or_imprecise_dtypes=True).then_inc(const, 1)
            pool.iota(one_at[:, 0, :], [[-64, 2], [-1, 2]], base=-3 * HD, channel_multiplier=1,
                      allow_small_or_imprecise_dtypes=True).then_inc(const, 1)
            pool.memset(code, -1000.0).then_inc(pool_c, 1)
            pool.wait_ge(pool_c, 6)
            for n, (rows_of, step) in enumerate(((slice(0, 2), HD), (slice(2, 3), HD), (slice(0, 3, 2), 0), (slice(1, 2), 0))):
                columns = code[:, n, :].rearrange("p (s r d) -> p s r d", s=2, r=4)[:, :, rows_of, :]
                pool.iota(columns, [[step, 2], [0, columns.shape[2]], [1, HD]], base=0, channel_multiplier=0,
                          allow_small_or_imprecise_dtypes=True).then_inc(const, 1)
            pool.affine_select(out=ident[:], in_=ident[:], compare_op=ALU.not_equal, fill=1.0, base=0,
                               pattern=[[-1, P]], channel_multiplier=1).then_inc(pool_c, 1)
            pool.affine_select(out=before[:], in_=before[:], compare_op=ALU.is_ge, fill=1.0, base=0,
                               pattern=[[-1, P]], channel_multiplier=1).then_inc(const, 1)
            pool.affine_select(out=mask_qk[:], in_=mask_qk[:], compare_op=ALU.is_ge, fill=NEG, base=0,
                               pattern=[[-1, P]], channel_multiplier=1).then_inc(const, 1)
            pool.affine_select(out=mask_kq[:], in_=mask_kq[:], compare_op=ALU.is_ge, fill=NEG, base=0,
                               pattern=[[1, P]], channel_multiplier=-1).then_inc(const, 1)
            heads = same_head[:].rearrange("p (h d) -> p h d", d=HD)
            pool.affine_select(out=heads, in_=heads, compare_op=ALU.is_ge, fill=0.0, base=0,
                               pattern=[[-HD, P // HD], [0, HD]], channel_multiplier=1).then_inc(pool_c, 1)
            pool.wait_ge(pool_c, 8)
            pool.tensor_copy(identb[:], ident[:]).then_inc(const, 1)
            pool.affine_select(out=heads, in_=heads, compare_op=ALU.is_ge, fill=0.0, base=HD - 1,
                               pattern=[[HD, P // HD], [0, HD]], channel_multiplier=-1).then_inc(const, 1)

            def move_rows(m, lag):
                pool.wait_ge(m.ids_ready, 1)
                pool.wait_ge(m.xn_stored, 16)
                own = EARLY if m is m1 else 0
                for t in range(own):
                    pool.indirect_dma_start(
                        out=early[:, t, :], out_offset=None, in_=m.x_dram,
                        in_offset=bass.IndirectOffsetOnAxis(ap=m.ids[:, t:t + 1], axis=0)).then_inc(m.early_in[t], 16)

                def gather(n):
                    if n >= own + XBUF:
                        pool.wait_ge(m.x_ps, n - XBUF + 1)
                    pool.indirect_dma_start(
                        out=xg[:, n % XBUF, :], out_offset=None, in_=m.x_dram,
                        in_offset=bass.IndirectOffsetOnAxis(ap=m.ids[:, n:n + 1], axis=0)).then_inc(m.gathered[n % XBUF], 16)

                for n in range(own, own + XBUF):
                    gather(n)
                for t in range(m.tiles + lag):
                    if own + XBUF <= t + XBUF < m.tiles:
                        gather(t + XBUF)
                    n = t - lag
                    if n >= 0:
                        pool.wait_ge(m.y_sb, n + 1)
                        pool.indirect_dma_start(
                            out=m.y_dram, out_offset=bass.IndirectOffsetOnAxis(ap=m.dest[:, n:n + 1], axis=0),
                            in_=ysb[:, n % YBUF, :], in_offset=None).then_inc(m.y_out[n % YBUF], 16)

            for m, lag in ((m0, 2), (m1, 3)):
                move_rows(m, lag)

        @block.scalar
        def _(act):
            def sqrt_var(n):
                act.wait_ge(var_ready, n + 1)
                nc.scalar.activation(rstd[:, 1, :], rstd[:, 0, :], ACT.Sqrt).then_inc(std_ready, 1)

            def evacuate_xT(n):
                for half in range(2):
                    act.wait_ge(xT_ps, NT * n + TPS * (half + 1))
                    nc.scalar.copy(xT[:, 0, half * S:(half + 1) * S], ps[:, half, :]).then_inc(xT_act, 1)

            def route_exp(m):
                act.wait_ge(m.ex_in, 1)
                nc.scalar.activation(m.weight[:], m.weight[:], ACT.Exp).then_inc(m.ex_out, 1)

            def rows(m, t, half, bank=4):
                act.wait_ge(m.x_ps, t + 1)
                at_least(act, m.u_ps, t - 1)
                nc.scalar.copy(xgT[:, half], ps[:, bank, 0:CC * P].rearrange("p (c n) -> p c n", n=P)).then_inc(m.x_sb, 1)

            def tile_parts(m, t, p):
                if p["row"]:
                    rows(m, t + 1, 1 - p["half"])
                if p["ug"]:
                    act.wait_ge(m.g_ps, t + 1)
                    at_least(act, m.ga_sb, t - 1)
                    nc.scalar.activation(th[:, p["half"], 0:m.H], ps[:, 2 + p["half"], 0:m.H], ACT.Tanh,
                                         scale=0.5).then_inc(m.th_sb, 1)
                if p["hid"]:
                    act.wait_ge(m.h_ps, t)
                    at_least(act, m.y_ps, t - 1)
                    nc.scalar.copy(hT[0:m.HP, 1 - p["half"], 0:m.HB, :],
                                   ps[0:m.HP, 5, 0:m.HB * P].rearrange("p (b n) -> p b n", n=P)).then_inc(m.hT_sb, 1)

            def place_block(n):
                for j in range(4):
                    u = 4 * n + j
                    act.wait_ge(sel_ps, u + 1)
                    if n < NB:
                        nc.scalar.activation(ka[:, j, n * S:(n + 1) * S], ps[:, 1 + u % 2, :], ACT.Identity,
                                             bias=one_at[:, 2, 0:1]).then_inc(qk_in, 1)
                    else:
                        half, b = divmod(n - NB, NB)
                        nc.scalar.copy(qa[:, 4 * half + j, b * S:(b + 1) * S], ps[:, 1 + u % 2, :]).then_inc(qk_in, 1)

            sqrt_var(0)
            evacuate_xT(0)
            route_exp(m0)
            act.wait_ge(sel_ready, 1)
            for n in range(NB + 2 * CC):
                at_least(act, sel_ps, 4 * (n - 1))
                if n < NB:
                    act.wait_ge(k_ps, n + 1)
                    nc.scalar.copy(hl[0:KV * HD, n % 2, 0, :], ps[0:KV * HD, 1 + n, :]).then_inc(hi_ready, 1)
                else:
                    act.wait_ge(q_ps, n - NB + 1)
                    nc.scalar.activation(hl[:, n % 2, 0, :], ps[:, (5 + n - NB) % 8, :], ACT.Copy, scale=SCALE).then_inc(hi_ready, 1)
                if n:
                    place_block(n - 1)
            place_block(NB + 2 * CC - 1)
            for kind, *which in steps0:
                m = m0
                if kind == "rows":
                    t, = which
                    rows(m, t, t % 2, 6)
                elif kind == "gate":
                    t, = which
                    act.wait_ge(m.g_ps, t + 1)
                    at_least(act, m.ga_sb, t - 1)
                    nc.scalar.activation(th[:, t % 2, :], ps[:, 4, 0:m.H], ACT.Tanh, scale=0.5).then_inc(m.th_sb, 1)
                elif kind == "turn":
                    t, = which
                    act.wait_ge(m.h_ps, t + 1)
                    at_least(act, m.y_ps, t)
                    nc.scalar.copy(hT[0:m.HP, t % 2], ps[0:m.HP, 7, :].rearrange("p (b n) -> p b n", n=P)).then_inc(m.hT_sb, 1)
                elif kind == "send":
                    g, = which
                    act.wait_ge(nmax_ready, 2 * (g + 1))
                    act.dma_start(nmax_dram[g].rearrange("w i n -> i w n"), nmax[:, :, g, :].bitcast(F32)).then_inc(nmax_out, 16)
                elif kind == "fetch":
                    g, = which
                    b, kv = divmod(g, KV)
                    act.wait_ge(nmax_out, 16 * (g + 1))
                    for s in range(2):
                        row = 64 * s + 3 * HD
                        act.dma_start(qa[row:row + 2, 2 * kv:2 * kv + 2, b * S:(b + 1) * S].bitcast(F32),
                                      nmax_dram[g, :, 8 * s:8 * (s + 1), :].rearrange("w (pair t) n -> w pair (t n)", pair=2)
                                      ).then_inc(nmax_in, 16)
                elif kind == "prob":
                    g, i = which
                    kb, j = divmod(i, GRP)
                    n = g * 16 + i
                    act.wait_ge(st_ps, n + 1)
                    at_least(act, pv_used, g * TPS + kb - 1)
                    nc.scalar.activation(pT[:, kb % 2, j, kb * P:S], ps[:, 1 + n % 2, kb * P:S], ACT.Exp).then_inc(p_sb, 1)
                elif kind == "value" and which[1] == TPS - 1:
                    g = which[0]
                    act.wait_ge(pv_used, TPS * (g + 1))
                    if g >= 2:
                        act.wait_ge(s_ps, unit_of["out", g - 2] + 1)
                    nc.scalar.copy(oT[:, g % 2, :], ps[:, 3, :]).then_inc(o_sb, 1)
            for c in range(2 * CC):
                act.wait_ge(ot_ps, c + 1)
                nc.scalar.copy(xT[:, c // 2, (c % 2) * S:(c % 2 + 1) * S], ps[:, c, :]).then_inc(ot_sb, 1)
            sqrt_var(1)
            evacuate_xT(1)
            route_exp(m1)
            def exp_min(n, src):
                dst = emin[:, n % 2, 0:src.shape[-1]]
                if n >= 2:
                    act.wait_ge(f1, n - 1)
                nc.scalar.activation(dst, src, ACT.Relu, scale=-1.0).then_inc(relu1, 1)
                act.wait_ge(relu1, n + 1)
                nc.scalar.activation(dst, dst, ACT.Exp, scale=-1.0).then_inc(exp1, 1)

            for c in range(2 * CC):
                act.wait_ge(q1_ps, c + 1)
                exp_min(c, ps[:, (5 + c) % 8, :])
            for t in range(NT):
                act.wait_ge(k1_ps, t + 1)
                nc.scalar.copy(vf[:, t, :, 0:P], ps[:, 1 + t % 3, D:2 * D].rearrange("p (c n) -> p c n", n=P)).then_inc(v1_sb, 1)
                exp_min(2 * CC + t, ps[:, 1 + t % 3, 0:D])
            for b in range(NB):
                act.wait_ge(sh_g, b + 1)
                at_least(act, sh_ga_ready, b)
                nc.scalar.activation(sh_th, ps[:, SHARED_BANKS[b][0], :], ACT.Tanh, scale=0.5).then_inc(sh_tanh, 1)
            for i in range(2 * CC):
                b, c = divmod(i, CC)
                if i == CC:
                    rows(m1, 0, 0)
                act.wait_ge(ot1_ps, i + 1)
                nc.scalar.copy(xT[:, c, b * S:(b + 1) * S], ps[:, 5 + i % 3, :]).then_inc(ot1_sb, 1)
            run_tiles(act, m1, tile_parts)

        @block.vector
        def _(dve):
            chain = [0]

            def link(ins):
                chain[0] += 1
                ins.then_inc(dve_c, 1)
                dve.wait_ge(dve_c, chain[0])

            def add_attention(i):
                for t in (2 * i, 2 * i + 1):
                    wait_added(dve, m0, t)
                dve.wait_ge(wo_ps, i + 1)
                nc.vector.tensor_tensor(acc[:, 2 * i:2 * i + 2, :], ps[:, 4 + i, :].rearrange("p (t c) -> p t c", t=2),
                                        acc[:, 2 * i:2 * i + 2, :], ALU.add).then_inc(wo_add, 1)
                dve.wait_ge(wo_add, i + 1)

            def layernorm(n):
                for t in range(NT):
                    if n == 0:
                        if t % TPS == 0:
                            dve.wait_ge(x_in[t // TPS], 16)
                    elif t % 2 == 0:
                        add_attention(t // 2)
                    last = nc.vector.bn_stats(bn[:, t, :], acc[:, t, :])
                link(last)
                for t in range(NT):
                    last = nc.vector.bn_aggr(mv[:, t, :], bn[:, t, :])
                link(last)
                nc.vector.tensor_scalar(rstd[:, 0, :], mv[:, :, 1], EPS_LN, None, ALU.add).then_inc(var_ready, 1)
                dve.wait_ge(std_ready, n + 1)
                link(nc.vector.reciprocal(rstd[:, 2, :], rstd[:, 1, :]))
                link(nc.vector.tensor_tensor(rstd[:, 3, :], rstd[:, 2, :], rstd[:, 2, :], ALU.mult))
                link(nc.vector.tensor_tensor(rstd[:, 3, :], rstd[:, 3, :], rstd[:, 0, :], ALU.mult))
                link(nc.vector.tensor_scalar(rstd[:, 3, :], rstd[:, 3, :], -0.5, 1.5, ALU.mult, ALU.add))
                link(nc.vector.tensor_tensor(rstd[:, 2, :], rstd[:, 2, :], rstd[:, 3, :], ALU.mult))
                if n:
                    dve.wait_ge(ot_ps, CC * 2)
                for t in range(NT):
                    nc.vector.tensor_scalar(xn[:, t, :], acc[:, t, :], mv[:, t, 0:1], rstd[:, 2, t:t + 1],
                                            ALU.subtract, ALU.mult).then_inc(xn_ready, 1)

            def evacuate_xT(n):
                for half in range(2):
                    dve.wait_ge(xT_ps, NT * n + TPS * (half + 1))
                    nc.vector.tensor_copy(xT[:, 1, half * S:(half + 1) * S], ps[:, 2 + half, :]).then_inc(xT_dve, 1)

            def choose(m):
                K, E = m.K, m.E
                dve.wait_ge(m.lg_ps, 1)
                link(nc.vector.tensor_copy(m.logits[:], ps[:, 4, 0:NT * m.E].rearrange("p (t e) -> p t e", t=NT)))
                for t in range(NT):
                    last = nc.vector.max(m.best[:, t, :], m.logits[:, t, :])
                link(last)
                for t in range(NT):
                    last = nc.vector.max_index(m.index[:, t, :], m.best[:, t, :], m.logits[:, t, :])
                link(last)
                nc.vector.tensor_tensor(m.weight[:], m.best[:], m.best[:, :, 0:1].to_broadcast([P, NT, 8]),
                                        ALU.subtract).then_inc(m.ex_in, 1)
                link(nc.vector.tensor_copy(m.choice[:], m.index[:, :, 0:K]))
                for k in range(K):
                    last = nc.vector.tensor_tensor(
                        m.onehot[:, k], m.choice[:, :, k:k + 1].to_broadcast([P, NT, E]),
                        iota_p[:, 0:E].unsqueeze(1).to_broadcast([P, NT, E]), ALU.is_equal)
                link(last)
                link(nc.vector.tensor_tensor(m.member[:], m.onehot[:, 0], m.onehot[:, 1], ALU.add))
                for k in range(2, K):
                    link(nc.vector.tensor_tensor(m.member[:], m.member[:], m.onehot[:, k], ALU.add))
                link(nc.vector.memset(m.earlier[:, 0, :], 0.0))
                for t in range(NT - 1):
                    link(nc.vector.tensor_tensor(m.earlier[:, t + 1, :], m.earlier[:, t, :], m.member[:, t, :], ALU.add))
                nc.vector.tensor_tensor(m.earlier[:, NT, :], m.earlier[:, NT - 1, :], m.member[:, NT - 1, :],
                                        ALU.add).then_inc(m.member_ready, 1)
                dve.wait_ge(m.ex_out, 1)
                n_sum = K if m is m0 else E
                link(nc.vector.tensor_reduce(m.wsum[:, 0, :], m.weight[:, :, 0:n_sum], AX.X, ALU.add))
                link(nc.vector.reciprocal(m.wsum[:, 1, :], m.wsum[:, 0, :]))
                link(nc.vector.tensor_tensor(m.weight[:, :, 0:K], m.weight[:, :, 0:K],
                                             m.wsum[:, 1, :].unsqueeze(2).to_broadcast([P, NT, K]), ALU.mult))

            def slots(m, part):
                (first_slots, pair_slots, tile_experts)[part](m)

            def first_slots(m):
                K, E = m.K, m.E
                dve.wait_ge(m.rank_ps, 1)
                count = ps[:, 4, NT * E:(NT + 1) * E]
                link(nc.vector.tensor_scalar(m.cnti[:, 0, :], count, float(P - 1), None, ALU.add))
                link(nc.vector.tensor_scalar(m.cnti[:, 1, :], m.cnti[:, 0, :], 7, None, ALU.logical_shift_right))
                link(nc.vector.tensor_copy(m.cnt[:, 1, :], m.cnti[:, 1, :]))
                link(nc.vector.memset(m.cnt[:, 0, :], 1.0))
                link(nc.vector.tensor_tensor_scan(m.cnt[:, 2, :], m.cnt[:, 0, :], m.cnt[:, 1, :], 0.0, ALU.mult, ALU.add))
                link(nc.vector.tensor_tensor(m.cnt[:, 3, :], m.cnt[:, 2, :], m.cnt[:, 1, :], ALU.subtract))
                link(nc.vector.tensor_scalar(m.cnt[:, 3, :], m.cnt[:, 3, :], float(P), None, ALU.mult))
                link(nc.vector.tensor_tensor(m.slot[:], ps[:, 4, 0:NT * E].rearrange("p (t e) -> p t e", t=NT),
                                             m.cnt[:, 3:4, :].to_broadcast([P, NT, E]), ALU.add))

            def pair_slots(m):
                for k in range(m.K):
                    last = nc.vector.tensor_tensor(m.onehot[:, k], m.onehot[:, k], m.slot[:], ALU.mult)
                link(last)
                link(nc.vector.tensor_reduce(m.slotk[:], m.onehot[:], AX.X, ALU.add))
                nc.vector.tensor_copy(m.sloti[:], m.slotk[:]).then_inc(m.slots_ready, 1)

            def tile_experts(m):
                E = m.E
                link(nc.vector.tensor_tensor(m.cmp[:], m.cnt[0:1, 2:3, :].to_broadcast([1, m.tiles, E]),
                                             iota_p[0:1, 0:m.tiles].unsqueeze(2).to_broadcast([1, m.tiles, E]), ALU.is_le))
                link(nc.vector.tensor_reduce(m.tile_e[:], m.cmp[:], AX.X, ALU.add))
                link(nc.vector.tensor_scalar(m.tile_e[:], m.tile_e[:], float(E - 1), None, ALU.min))
                link(nc.vector.tensor_copy(m.tab[:, 0, :], m.tile_e[:]))
                link(nc.vector.tensor_scalar(m.tab[:, 1, :], m.tab[:, 0, :], 32.0, 32.0, ALU.mult, ALU.add))
                link(nc.vector.tensor_scalar(m.cum[:], m.cnt[0:1, 2, :], 1.0, None, ALU.add))
                link(nc.vector.tensor_scalar(m.tab[:, 2, :], m.tile_e[:], float(m.reciprocal), None, ALU.mult))
                link(nc.vector.tensor_scalar(m.tab[:, 2, :], m.tab[:, 2, :], m.SHIFT, None, ALU.logical_shift_right))
                link(nc.vector.tensor_scalar(m.cmp[:, :, 0], m.tab[:, 2, :], -float(m.ring), None, ALU.mult))
                nc.vector.tensor_tensor(m.tab[:, 2, :], m.cmp[:, :, 0], m.tile_e[:], ALU.add).then_inc(m.tab_ready, 1)

            def split_slots(m):
                dve.wait_ge(m.slots_ready, 1)
                slots_of = m.sloti[:].rearrange("p k t -> p (k t)").bitcast(I32)
                nc.vector.tensor_scalar(m.split[:, 0, :], slots_of, 7, None, ALU.logical_shift_right)
                link(nc.vector.tensor_scalar(m.split[:, 1, :], slots_of, P - 1, None, ALU.bitwise_and))
                link(nc.vector.tensor_copy(m.splitf[:], m.split[:]))

            def place_ids(m, k):
                T = m.tiles
                w = k % 2
                at_least(dve, m.hot_used, k - 1)
                tile_of = m.splitf[:, 0, k * NT:(k + 1) * NT]
                row_of = m.splitf[:, 1, k * NT:(k + 1) * NT]
                link(nc.vector.tensor_tensor(m.hot_tile, tile_of.unsqueeze(2).to_broadcast([P, NT, T]),
                                             iota_p[:, 0:T].unsqueeze(1).to_broadcast([P, NT, T]), ALU.is_equal))
                nc.vector.tensor_scalar(m.hot_id[:, w, 0], m.hot_tile, tokid[:, 0:1], None, ALU.mult)
                link(nc.vector.tensor_tensor(m.hot_id[:, w, 1], m.hot_tile,
                                             place[:, k, :].unsqueeze(2).to_broadcast([P, NT, T]), ALU.mult))
                nc.vector.tensor_tensor(m.hot_row[:, w], row_of.unsqueeze(2).to_broadcast([P, NT, P]),
                                        iota_p[:].unsqueeze(1).to_broadcast([P, NT, P]), ALU.is_equal).then_inc(m.hot_ready, 1)

            def integer_ids(m):
                dve.wait_ge(m.hot_used, m.K)
                taken = ps[:, 4, 0:m.tiles]
                nc.vector.tensor_copy(m.taken[:], taken)
                link(nc.vector.scalar_tensor_tensor(out=m.spare[:, 1, :], in0=taken, scalar=0.0, in1=m.spare[:, 0, :],
                                                    op0=ALU.is_equal, op1=ALU.mult))
                nc.vector.tensor_scalar(m.ids[:].bitcast(I32), m.taken[:], NTOK - 1, None, ALU.bitwise_and)
                link(nc.vector.scalar_tensor_tensor(out=m.spare[:, 2, :], in0=taken, scalar=-float(NTOK), in1=m.spare[:, 1, :],
                                                    op0=ALU.add, op1=ALU.add))
                nc.vector.tensor_copy(m.dest[:], m.spare[:, 2, :]).then_inc(m.ids_ready, 1)

            def tile_parts(m, t, p):
                half = p["half"]
                if p["ug"]:
                    dve.wait_ge(m.th_sb, t + 1)
                    nc.vector.scalar_tensor_tensor(out=ga[:, half, 0:m.H], in0=th[:, half, 0:m.H], scalar=1.0,
                                                   in1=ps[:, 2 + half, 0:m.H], op0=ALU.add, op1=ALU.mult).then_inc(m.ga_sb, 1)
                    dve.wait_ge(m.ga_sb, t + 1)
                    dve.wait_ge(m.u_ps, t + 1)
                    at_least(dve, m.h_ps, t - 1)
                    nc.vector.scalar_tensor_tensor(out=hh[:, half, 0:m.H], in0=ga[:, half, 0:m.H], scalar=0.5,
                                                   in1=ps[:, half, 0:m.H], op0=ALU.mult, op1=ALU.mult).then_inc(m.h_sb, 1)
                if p["down"]:
                    dve.wait_ge(m.y_ps, t)
                    at_least(dve, m.y_out[p["ybuf"]], p["stored"])
                    nc.vector.tensor_copy(ysb[:, p["ybuf"], :], ps[:, 6, 0:D]).then_inc(m.y_sb, 1)

            def combine(m, t):
                dve.wait_ge(m.back[t], 16)
                for k in range(m.K):
                    n = m.K * t + k
                    at_least(dve, m.added, n)
                    nc.vector.scalar_tensor_tensor(out=acc[:, t, :], in0=m.z[:, t % m.zbuf, k, :], scalar=m.weight[:, t, k:k + 1],
                                                   in1=acc[:, t, :], op0=ALU.mult, op1=ALU.add).then_inc(m.added, 1)

            layernorm(0)
            dve.wait_ge(const, N_CONST)
            nc.vector.memset(vaug[:], 1.0)
            evacuate_xT(0)
            for n in range(16):
                nc.vector.tensor_scalar(sel[:, n, :], code[:, n // 4, :], shift[:, n // 8, n % 4:n % 4 + 1], None, ALU.is_equal)
            link(nc.vector.tensor_scalar(one_at[:, 1, :], one_at[:, 0, :], 0.0, None, ALU.is_equal))
            nc.vector.tensor_reduce(one_at[:, 2, 0:1], one_at[:, 1, :], AX.X, ALU.add).then_inc(sel_ready, 1)

            def low_part(n):
                dve.wait_ge(hi_ready, n + 1)
                if n < NB:
                    nc.vector.tensor_tensor(hl[0:KV * HD, n % 2, 1, :], ps[0:KV * HD, 1 + n, :],
                                            hl[0:KV * HD, n % 2, 0, :].bitcast(F32), ALU.subtract).then_inc(lo_ready, 1)
                else:
                    nc.vector.scalar_tensor_tensor(out=hl[:, n % 2, 1, :], in0=ps[:, (5 + n - NB) % 8, :], scalar=SCALE,
                                                   in1=hl[:, n % 2, 0, :].bitcast(F32),
                                                   op0=ALU.mult, op1=ALU.subtract).then_inc(lo_ready, 1)

            choose(m0)
            for n in range(NB):
                low_part(n)
            for part in range(3):
                slots(m0, part)
            split_slots(m0)
            low_part(2)
            low_part(3)
            for k in range(m0.K):
                place_ids(m0, k)
            integer_ids(m0)
            low_part(4)
            low_part(5)
            dve.wait_ge(v_ps, 1)
            nc.vector.tensor_copy(vaug[:, :, :, 0:HD],
                                  ps[:, 3, :].rearrange("p (t h d) -> p t h d", t=NT, d=HD)).then_inc(v_sb, 1)
            dve.wait_ge(m0.xn_stored, 16)
            for kind, *which in steps0:
                m = m0
                if kind == "hidden":
                    t, = which
                    dve.wait_ge(m.th_sb, t + 1)
                    nc.vector.scalar_tensor_tensor(out=ga[:, t % 2, :], in0=th[:, t % 2, :], scalar=1.0,
                                                   in1=ps[:, 4, 0:m.H], op0=ALU.add, op1=ALU.mult).then_inc(m.ga_sb, 1)
                    dve.wait_ge(m.ga_sb, t + 1)
                    dve.wait_ge(m.u_ps, t + 1)
                    at_least(dve, m.h_ps, t - 1)
                    nc.vector.scalar_tensor_tensor(out=hh[:, t % 2, :], in0=ga[:, t % 2, :], scalar=0.5,
                                                   in1=ps[:, 5, 0:m.H], op0=ALU.mult, op1=ALU.mult).then_inc(m.h_sb, 1)
                elif kind == "down":
                    t, = which
                    dve.wait_ge(m.y_ps, t + 2)
                    at_least(dve, m.y_out[t % YBUF], 16 * (t // YBUF))
                    nc.vector.tensor_copy(ysb[:, t % YBUF, :], ps[:, 6, 0:D]).then_inc(m.y_sb, 1)
                elif kind == "score":
                    g, i = which
                    j, qt = group_order(i)
                    dve.wait_ge(s_ps, unit_of[kind, g, i] + 1)
                    nc.vector.tensor_reduce(rowmax[:, g, i:i + 1], ps[:, 0, 0:(qt + 1) * P], AX.X, ALU.max).then_inc(s_read, 1)
                elif kind == "neg":
                    g, = which
                    dve.wait_ge(s_ps, unit_of[kind, g] + 1)
                    nc.vector.tensor_scalar(nmax[:, 0, g, :], ps[0:16, 0, 0:P], -1.0, None, ALU.mult).then_inc(nmax_ready, 1)
                    dve.wait_ge(nmax_ready, 2 * g + 1)
                    nc.vector.scalar_tensor_tensor(out=nmax[:, 1, g, :], in0=ps[0:16, 0, 0:P], scalar=-1.0,
                                                   in1=nmax[:, 0, g, :].bitcast(F32), op0=ALU.mult,
                                                   op1=ALU.subtract).then_inc(nmax_ready, 1)
                elif kind == "out":
                    g, = which
                    b, kv = divmod(g, KV)
                    dve.wait_ge(s_ps, unit_of[kind, g] + 1)
                    made = ps[:, 0, :].rearrange("p (t j d) -> p t j d", t=TPS, d=2 * HD)
                    link(nc.vector.reciprocal(rsum[:, g % 2], made[:, :, :, HD]))
                    for t in range(TPS):
                        last = nc.vector.tensor_tensor(
                            xn[:, b * TPS + t, kv * 64:(kv + 1) * 64].rearrange("p (j d) -> p j d", d=HD),
                            made[:, t, :, 0:HD], rsum[:, g % 2, t, :].unsqueeze(2).to_broadcast([P, GRP, HD]), ALU.mult)
                    last.then_inc(o_norm, 1)
                elif kind == "add":
                    combine(m, which[0])
            for b in range(YBUF):
                dve.wait_ge(m0.y_out[b], 16 * len(range(b, m0.tiles, YBUF)))
            nc.vector.memset(vf[:, :, :, P:P + 1], 1.0)
            layernorm(1)
            evacuate_xT(1)
            choose(m1)
            for c in range(2 * CC):
                dve.wait_ge(exp1, c + 1)
                nc.vector.scalar_tensor_tensor(out=qf[:, c // 2, (c % 2) * S:(c % 2 + 1) * S], in0=ps[:, (5 + c) % 8, :], scalar=0.0,
                                               in1=emin[:, c % 2, :], op0=ALU.max, op1=ALU.add).then_inc(f1, 1)
            def key_features(t):
                dve.wait_ge(exp1, 2 * CC + t + 1)
                nc.vector.scalar_tensor_tensor(out=kf[:, t, :], in0=ps[:, 1 + t % 3, 0:D], scalar=0.0,
                                               in1=emin[:, t % 2, 0:D], op0=ALU.max, op1=ALU.add).then_inc(f1, 1)

            key_features(0)
            key_features(1)
            slots(m1, 0)
            key_features(2)
            slots(m1, 1)
            key_features(3)
            slots(m1, 2)
            key_features(4)
            split_slots(m1)
            key_features(5)
            place_ids(m1, 0)
            key_features(6)
            key_features(7)
            place_ids(m1, 1)
            integer_ids(m1)
            for b in range(NB):
                dve.wait_ge(sh_tanh, b + 1)
                at_least(dve, sh_sb, b)
                nc.vector.scalar_tensor_tensor(out=sh_ga, in0=sh_th, scalar=1.0, in1=ps[:, SHARED_BANKS[b][0], :],
                                               op0=ALU.add, op1=ALU.mult).then_inc(sh_ga_ready, 1)
                dve.wait_ge(sh_ga_ready, b + 1)
                dve.wait_ge(sh_u, b + 1)
                nc.vector.scalar_tensor_tensor(out=shT[:, b * S:(b + 1) * S], in0=sh_ga, scalar=0.5, in1=ps[:, SHARED_BANKS[b][1], :],
                                               op0=ALU.mult, op1=ALU.mult).then_inc(sh_sb, 1)
                dve.wait_ge(kv_ps, b + 1)
                for c in range(CC):
                    at = 2 * P * c
                    nc.vector.tensor_tensor(kvd[:, b, c, 0:P], ps[:, 5 + b, at:at + P], same_head[:], ALU.mult).then_inc(kv_sb, 1)
                    nc.vector.tensor_scalar(kvd[:, b, c, P:KVW], same_head[:, 0:P:HD], ps[:, 5 + b, at + P:at + P + 1], None,
                                            ALU.mult).then_inc(kv_sb, 1)
            for t in range(NT):
                dve.wait_ge(nd_ps, t + 1)
                made = ps[:, t % 4, 0:CC * KVW].rearrange("p (c n) -> p c n", c=CC)
                link(nc.vector.tensor_scalar(den[:, t, 0], made[:, :, P:KVW], 1e-6, None, ALU.add))
                link(nc.vector.reciprocal(den[:, t, 1], den[:, t, 0]))
                for c in range(CC):
                    ins = nc.vector.tensor_tensor(att[:, t, c * P:(c + 1) * P].rearrange("p (h d) -> p h d", d=HD),
                                                  made[:, c, 0:P].rearrange("p (h d) -> p h d", d=HD),
                                                  den[:, t, 1, c, :].unsqueeze(2).to_broadcast([P, P // HD, HD]), ALU.mult)
                ins.then_inc(nd_read, 1)
            for i in range(NT // 2):
                dve.wait_ge(wo1_ps, i + 1)
                nc.vector.tensor_tensor(acc[:, 2 * i:2 * i + 2, :], ps[:, i, :].rearrange("p (t c) -> p t c", t=2),
                                        acc[:, 2 * i:2 * i + 2, :], ALU.add).then_inc(wo1_add, 1)
            dve.wait_ge(wo1_add, NT // 2)
            run_tiles(dve, m1, tile_parts)
            for t in range(NT):
                combine(m1, t)

        @block.tensor
        def _(pe):
            mm_ = nc.tensor.matmul

            def transpose_x(n):
                if n:
                    pe.wait_ge(wo_add, NT // 2)
                for t in range(NT):
                    pe.wait_ge(xn_ready, NT * n + t + 1)
                    for c in range(CC):
                        last = nc.tensor.transpose(ps[:, 2 * c + t // TPS, (t % TPS) * P:(t % TPS + 1) * P],
                                                   xn[:, t, c * P:(c + 1) * P], ident[:])
                    last.then_inc(xT_ps, 1)

            def logits(m):
                for t in range(NT):
                    for c in range(CC):
                        last = mm_(ps[:, 4, t * m.E:(t + 1) * m.E], xT[:, c, t * P:(t + 1) * P], m.gate[:, c, :],
                                   start=c == 0, stop=c == CC - 1)
                last.then_inc(m.lg_ps, 1)

            def ranks(m):
                pe.wait_ge(m.member_ready, 1)
                n = NT * m.E
                mm_(ps[:, 4, 0:n + m.E], onesb[:], m.earlier[:].rearrange("p t e -> p (t e)"), start=True, stop=False,
                    skip_group_check=True)
                mm_(ps[:, 4, 0:n], before[:], m.member[:].rearrange("p t e -> p (t e)"), start=False, stop=True,
                    skip_group_check=True).then_inc(m.rank_ps, 1)

            def place_ids(m, k):
                if k == 0:
                    pe.wait_ge(m.tab_ready, 1)
                pe.wait_ge(m.hot_ready, k + 1)
                for t in range(NT):
                    for part in range(2):
                        last = mm_(ps[:, 4, 0:m.tiles], m.hot_row[:, k % 2, t, :], m.hot_id[:, k % 2, part, t, :],
                                   start=k == 0 and t == 0 and part == 0, stop=k == m.K - 1 and t == NT - 1 and part == 1)
                last.then_inc(m.hot_used, 1)

            def rows(m, t, arrived):
                xbuf, count = arrived
                if isinstance(t, int) and t < EARLY:
                    pe.wait_ge(m.early_in[t], 16)
                    source = early[:, t]
                else:
                    pe.wait_ge(m.gathered[xbuf], count)
                    source = xg[:, xbuf]
                at_least(pe, m.x_sb, t)
                for c in range(CC):
                    last = nc.tensor.transpose(ps[:, 4, c * P:(c + 1) * P], source[:, c * P:(c + 1) * P], ident[:])
                last.then_inc(m.x_ps, 1)

            slots_read = []

            def tile_parts(m, t, p):
                half = p["half"]
                if p["count"] == 0:
                    slots_read.clear()

                def slot_of(tile):
                    return nc.tensor.value_load(m.tab[0:1, 2, bass.ds(tile, 1)], min_val=0, max_val=m.ring - 1)

                if p["row"]:
                    rows(m, t + 1, (p["xbuf"], p["gathered"]))
                if p["ug"]:
                    if p["count"] == 0:
                        slots_read.append(slot_of(t))
                    slot = slots_read[p["count"]]
                    pe.wait_ge(m.x_sb, t + 1)
                    at_least(pe, m.h_sb, t - 1)
                    for which, bank, ready in ((1, 2 + half, m.g_ps), (0, half, m.u_ps)):
                        for c in range(CC):
                            last = mm_(ps[:, bank, 0:m.H], xgT[:, half, c, :],
                                       m.wug[:, bass.ds(slot, 1), c, which, :].rearrange("p a n -> p (a n)"),
                                       start=c == 0, stop=c == CC - 1)
                        last.then_inc(ready, 1)
                if p["next"]:
                    slots_read.append(slot_of(t + 1))
                if p["down"]:
                    slot = slots_read[p["count"] - 2] if p["count"] >= 2 else slot_of(t - 2)
                if p["hid"]:
                    pe.wait_ge(m.h_sb, t)
                    at_least(pe, m.hT_sb, t - 1)
                    for b in range(m.HB):
                        last = nc.tensor.transpose(ps[0:m.HP, 5, b * P:(b + 1) * P],
                                                   hh[:, 1 - half, b * m.HP:(b + 1) * m.HP], ident[:])
                    last.then_inc(m.h_ps, 1)
                if p["down"]:
                    pe.wait_ge(m.hT_sb, t - 1)
                    at_least(pe, m.y_sb, t - 2)
                    for b in range(m.HB):
                        last = mm_(ps[:, 6, 0:D], hT[0:m.HP, half, b, :],
                                   m.wd[:, bass.ds(slot, 1), b, :].rearrange("p a n -> p (a n)"),
                                   start=b == 0, stop=b == m.HB - 1)
                    last.then_inc(m.y_ps, 1)

            def first_rows(m):
                rows(m, 0, (0, 16))

            pe.sem_inc(m0.y_ps, 1)
            pe.sem_inc(m1.y_ps, 1)
            pe.wait_ge(const, N_CONST)
            transpose_x(0)
            pe.wait_ge(xT_act, 2)
            pe.wait_ge(xT_dve, 2)
            pe.wait_ge(g_in, 32)
            logits(m0)
            pe.wait_ge(w_in0, 64)
            for b in range(NB):
                for c in range(CC):
                    last = mm_(ps[0:KV * HD, 1 + b, :], wk0[:, c, :], xT[:, c, b * S:(b + 1) * S], start=c == 0, stop=c == CC - 1)
                last.then_inc(k_ps, 1)

            def q_block(i):
                mm, b = divmod(i, NB)
                for c in range(CC):
                    last = mm_(ps[:, (5 + i) % 8, :], wq0[:, c, mm * P:(mm + 1) * P], xT[:, c, b * S:(b + 1) * S],
                               start=c == 0, stop=c == CC - 1)
                last.then_inc(q_ps, 1)

            def select(n):
                pe.wait_ge(hi_ready, n + 1)
                pe.wait_ge(lo_ready, n + 1)
                if n == 0:
                    pe.wait_ge(lo_ready, NB)
                first, height = (8, KV * HD) if n < NB else (0, P)
                for j in range(4):
                    u = 4 * n + j
                    at_least(pe, qk_in, u - 1)
                    for w in range(2):
                        last = mm_(ps[:, 1 + u % 2, :], sel[0:height, first + 4 * w + j, :], hl[0:height, n % 2, w, :],
                                   start=w == 0, stop=w == 1)
                    last.then_inc(sel_ps, 1)

            q_block(0)
            q_block(1)
            ranks(m0)
            for n in range(NB):
                select(n)
            q_block(2)
            q_block(3)
            for t in range(NT):
                for c in range(CC):
                    last = mm_(ps[:, 3, t * 64:(t + 1) * 64], xT[:, c, t * P:(t + 1) * P], wv0[:, c, :],
                               start=c == 0, stop=c == CC - 1)
            last.then_inc(v_ps, 1)
            place_ids(m0, 0)
            select(2)
            place_ids(m0, 1)
            select(3)
            place_ids(m0, 2)
            place_ids(m0, 3)
            select(4)
            select(5)
            pe.wait_ge(v_sb, 1)
            pe.wait_ge(m0.ids_ready, 1)
            pe.wait_ge(qk_in, 4 * (NB + 2 * CC))

            def free_unit(n):
                if n:
                    kind, g, *i = units[n - 1]
                    if kind == "score":
                        pe.wait_ge(s_read, 16 * g + i[0] + 1)
                    elif kind == "neg":
                        pe.wait_ge(nmax_ready, 2 * g + 2)
                    else:
                        pe.wait_ge(o_norm, g + 1)

            def slot_of(m, t):
                return nc.tensor.value_load(m.tab[0:1, 2, t:t + 1], min_val=0, max_val=m.ring - 1)

            for kind, *which in steps0:
                m = m0
                if kind == "rows":
                    t, = which
                    pe.wait_ge(m.gathered[t % XBUF], 16 * (t // XBUF + 1))
                    at_least(pe, m.y_sb, t - 2)
                    at_least(pe, m.x_sb, t)
                    for c in range(CC):
                        last = nc.tensor.transpose(ps[:, 6, c * P:(c + 1) * P], xg[:, t % XBUF, c * P:(c + 1) * P], ident[:])
                    last.then_inc(m.x_ps, 1)
                elif kind in ("gate", "up"):
                    t, = which
                    if kind == "gate":
                        slot = slot_of(m, t)
                        loaded = nc.tensor.value_load(m.tab[0:1, 1, t:t + 1], min_val=32, max_val=32 * m.E)
                        pe.wait_ge(m.w_loaded, loaded)
                        pe.wait_ge(m.x_sb, t + 1)
                        at_least(pe, m.ga_sb, t)
                    else:
                        at_least(pe, m.h_sb, t)
                    part, bank, ready = (1, 4, m.g_ps) if kind == "gate" else (0, 5, m.u_ps)
                    for c in range(CC):
                        last = mm_(ps[:, bank, 0:m.H], xgT[:, t % 2, c, :],
                                   m.wug[:, bass.ds(slot, 1), c, part, :].rearrange("p a n -> p (a n)"),
                                   start=c == 0, stop=c == CC - 1)
                    last.then_inc(ready, 1)
                elif kind == "turn":
                    t, = which
                    pe.wait_ge(m.h_sb, t + 1)
                    at_least(pe, m.hT_sb, t)
                    for b in range(m.HB):
                        last = nc.tensor.transpose(ps[0:m.HP, 7, b * P:(b + 1) * P], hh[:, t % 2, b * m.HP:(b + 1) * m.HP], ident[:])
                    last.then_inc(m.h_ps, 1)
                elif kind == "down":
                    t, = which
                    slot_d = slot_of(m, t)
                    pe.wait_ge(m.hT_sb, t + 1)
                    at_least(pe, m.y_sb, t)
                    pe.wait_ge(m.x_sb, min(t + 3, m.tiles))
                    for b in range(m.HB):
                        last = mm_(ps[:, 6, 0:D], hT[0:m.HP, t % 2, b, :],
                                   m.wd[:, bass.ds(slot_d, 1), b, :].rearrange("p a n -> p (a n)"),
                                   start=b == 0, stop=b == m.HB - 1)
                    last.then_inc(m.y_ps, 1)
                elif kind == "score":
                    g, i = which
                    j, qt = group_order(i)
                    b, kv = divmod(g, KV)
                    free_unit(unit_of[kind, g, i])
                    L = (qt + 1) * P
                    r = 64 * (j % 2)
                    h = kv * GRP + j
                    q0 = b * S + qt * P
                    mm_(ps[:, 0, 0:L], qa[r:r + 3 * HD, h // 2, q0:q0 + P], ka[r:r + 3 * HD, kv, b * S:b * S + L],
                        start=True, stop=False, skip_group_check=True)
                    mm_(ps[:, 0, qt * P:L], identb[:], mask_qk[:], start=False, stop=True,
                        skip_group_check=True).then_inc(s_ps, 1)
                elif kind == "neg":
                    g, = which
                    free_unit(unit_of[kind, g])
                    pe.wait_ge(s_read, 16 * (g + 1))
                    nc.tensor.transpose(ps[0:16, 0, 0:P], rowmax[:, g, :], ident[:]).then_inc(s_ps, 1)
                elif kind == "prob":
                    g, i = which
                    kb, j = divmod(i, GRP)
                    b, kv = divmod(g, KV)
                    n = g * 16 + i
                    at_least(pe, p_sb, n - 1)
                    if i == 0:
                        pe.wait_ge(nmax_in, 32 * (g + 1))
                    k0 = b * S + kb * P
                    r = 64 * (j % 2)
                    h = kv * GRP + j
                    mm_(ps[:, 1 + n % 2, kb * P:S], ka[r:r + 3 * HD + 2, kv, k0:k0 + P], qa[r:r + 3 * HD + 2, h // 2, k0:(b + 1) * S],
                        start=True, stop=False, skip_group_check=True)
                    mm_(ps[:, 1 + n % 2, kb * P:(kb + 1) * P], identb[:], mask_kq[:], start=False, stop=True,
                        skip_group_check=True).then_inc(st_ps, 1)
                elif kind == "value":
                    g, kb = which
                    b, kv = divmod(g, KV)
                    pe.wait_ge(p_sb, g * 16 + 4 * (kb + 1))
                    if kb == 0:
                        at_least(pe, o_sb, g)
                    for j in range(GRP):
                        last = mm_(ps[32 * j:32 * j + 32, 3, kb * P:S], vaug[:, b * TPS + kb, kv, :], pT[:, kb % 2, j, kb * P:S],
                                   start=kb == 0, stop=kb == TPS - 1, skip_group_check=True)
                    last.then_inc(pv_used, 1)
                elif kind == "out":
                    g, = which
                    free_unit(unit_of[kind, g])
                    pe.wait_ge(o_sb, g + 1)
                    for t in range(TPS):
                        last = nc.tensor.transpose(ps[:, 0, t * P:(t + 1) * P], oT[:, g % 2, t * P:(t + 1) * P], ident[:])
                    last.then_inc(s_ps, 1)
            pe.wait_ge(o_norm, G)
            pe.wait_ge(p_sb, 16 * G)
            pe.wait_ge(o_sb, G)
            for i in range(2 * CC):
                c, b = i // 2, i % 2
                for t in range(TPS):
                    last = nc.tensor.transpose(ps[:, i, t * P:(t + 1) * P], xn[:, b * TPS + t, c * P:(c + 1) * P], ident[:])
                last.then_inc(ot_ps, 1)
            pe.wait_ge(ot_sb, 2 * CC)
            pe.wait_ge(m0.h_sb, m0.tiles)
            pe.wait_ge(m0.hT_sb, m0.tiles)
            pe.wait_ge(m0.y_sb, m0.tiles)
            for t in range(NT):
                for c in range(CC):
                    last = mm_(ps[:, 4 + t // 2, (t % 2) * D:(t % 2 + 1) * D], xT[:, c, t * P:(t + 1) * P], wo0[:, c, :],
                               start=c == 0, stop=c == CC - 1)
                if t % 2:
                    last.then_inc(wo_ps, 1)

            def shared_expert(b):
                pe.wait_ge(ws_in, 32)
                for part, bank, ready in ((1, SHARED_BANKS[b][0], sh_g), (0, SHARED_BANKS[b][1], sh_u)):
                    for c in range(CC):
                        last = mm_(ps[:, bank, :], ws_ug[:, c, part, :], xT[:, c, b * S:(b + 1) * S], start=c == 0, stop=c == CC - 1)
                    last.then_inc(ready, 1)

            transpose_x(1)
            pe.wait_ge(xT_act, 4)
            pe.wait_ge(xT_dve, 4)
            logits(m1)
            pe.wait_ge(w_in1, 48)
            for i in range(2 * CC):
                mm, b = i // 2, i % 2
                for c in range(CC):
                    last = mm_(ps[:, (5 + i) % 8, :], wq1[:, c, mm * P:(mm + 1) * P], xT[:, c, b * S:(b + 1) * S],
                               start=c == 0, stop=c == CC - 1)
                last.then_inc(q1_ps, 1)
            ranks(m1)
            for t in range(NT):
                if t >= 3:
                    pe.wait_ge(f1, 2 * CC + t - 2)
                for c in range(CC):
                    last = mm_(ps[:, 1 + t % 3, :], xT[:, c, t * P:(t + 1) * P], wkv1[:, c, :], start=c == 0, stop=c == CC - 1)
                last.then_inc(k1_ps, 1)
            pe.wait_ge(f1, 2 * CC)
            shared_expert(0)
            pe.wait_ge(f1, 2 * CC + NT)
            pe.wait_ge(v1_sb, NT)
            for b in range(NB):
                for c in range(CC):
                    for t in range(TPS):
                        tt = b * TPS + t
                        last = mm_(ps[:, 5 + b, 2 * P * c:2 * P * c + P + 1], kf[:, tt, c * P:(c + 1) * P], vf[:, tt, c, :],
                                   start=t == 0, stop=t == TPS - 1)
                last.then_inc(kv_ps, 1)
            place_ids(m1, 0)
            place_ids(m1, 1)
            shared_expert(1)
            pe.wait_ge(sh_sb, NB)
            for t in range(NT):
                b = t // TPS
                pe.wait_ge(kv_sb, 2 * CC * (b + 1))
                at_least(pe, nd_read, t - 3)
                for c in range(CC):
                    last = mm_(ps[:, t % 4, c * KVW:(c + 1) * KVW], qf[:, c, t * P:(t + 1) * P], kvd[:, b, c, 0:KVW],
                               start=True, stop=True)
                last.then_inc(nd_ps, 1)

            def turn_attention(b):
                pe.wait_ge(nd_read, TPS * (b + 1))
                for c in range(CC):
                    i = CC * b + c
                    if i == 3:
                        pe.wait_ge(ot1_sb, 1)
                    for t in range(TPS):
                        last = nc.tensor.transpose(ps[:, 5 + i % 3, t * P:(t + 1) * P], att[:, b * TPS + t, c * P:(c + 1) * P],
                                                   ident[:])
                    last.then_inc(ot1_ps, 1)

            def project_attention(b):
                pe.wait_ge(ot1_sb, CC * (b + 1))
                pe.wait_ge(nd_read, TPS * (b + 1) + 2 * (1 - b))
                for t in range(b * TPS, (b + 1) * TPS):
                    at = ps[:, t // 2, (t % 2) * D:(t % 2 + 1) * D]
                    for c in range(CC):
                        mm_(at, xT[:, c, t * P:(t + 1) * P], wo1[:, c, :], start=c == 0, stop=False)
                    last = mm_(at, shT[:, t * P:(t + 1) * P], ws_d[:], start=False, stop=True)
                    if t % 2:
                        last.then_inc(wo1_ps, 1)

            turn_attention(0)
            pe.wait_ge(m1.ids_ready, 1)
            first_rows(m1)
            project_attention(0)
            turn_attention(1)
            project_attention(1)
            pe.wait_ge(wo1_add, NT // 2)
            pe.wait_ge(m1.w_loaded, 32)
            run_tiles(pe, m1, tile_parts)


_ORDER = ["x", "wq0", "wk0", "wv0", "wo0", "gate0", "wug0", "wd0", "wq1", "wkv1", "wo1", "gate1", "wug1", "wd1", "ws_ug", "ws_d"]


def kernel(**inputs):
    import numpy as np
    import concourse.bacc as bacc
    from concourse.bass_utils import run_bass_kernel_spmd

    g = {k: np.asarray(v) for k, v in inputs.items()}

    def gate_up(up, gate):
        both = np.stack([up, gate], 1).transpose(0, 3, 1, 2)
        e, c, two, h = both.shape
        return both.reshape(e, c // P, P, two, h).transpose(0, 2, 1, 3, 4)

    def down(w, hp):
        e, c, h = w.shape
        return w.transpose(0, 2, 1).reshape(e, h // hp, hp, c).transpose(0, 2, 1, 3)

    x = g["L0_attn_x"]
    arrays = {
        "x": x.reshape(-1, D),
        "wq0": g["L0_attn_Wq"], "wk0": g["L0_attn_Wk"], "wv0": g["L0_attn_Wv"], "wo0": g["L0_attn_Wo"],
        "gate0": g["L0_ffn_gate_inp"].T,
        "wug0": gate_up(g["L0_ffn_W_up"], g["L0_ffn_W_gate"]), "wd0": down(g["L0_ffn_W_down"], 112),
        "wq1": g["L1_attn_Wq"].T,
        "wkv1": np.concatenate([g["L1_attn_Wk"].T, g["L1_attn_Wv"].T], 1),
        "wo1": g["L1_attn_Wo"].T,
        "gate1": g["L1_ffn_gate_w"].T,
        "wug1": gate_up(g["L1_ffn_w3"], g["L1_ffn_w1"]), "wd1": down(g["L1_ffn_w2"], P),
        "ws_ug": gate_up(g["L1_ffn_ws3"][None], g["L1_ffn_ws1"][None])[0], "ws_d": g["L1_ffn_ws2"].T,
    }
    arrays = {k: np.ascontiguousarray(v) for k, v in arrays.items()}
    nc = bacc.Bacc("TRN2", target_bir_lowering=False, num_devices=1)
    args = {k: nc.dram_tensor("in_" + k, arrays[k].shape, F32, kind="ExternalInput").ap() for k in _ORDER}
    out = nc.dram_tensor("out", arrays["x"].shape, F32, kind="ExternalOutput").ap()
    build(nc, args, out)
    r = run_bass_kernel_spmd(nc, [{"in_" + k: arrays[k] for k in _ORDER}], core_ids=[0])
    return r.results[0]["out"].reshape(x.shape)
```
